# Optimizing a Trainium2 kernel written in Bass

```python
import numpy as np
import jax
import jax.numpy as jnp

def _softmax(x, axis=-1):
    return jax.nn.softmax(x, axis=axis)

def _gelu(x):
    return jax.nn.gelu(x, approximate=True)

def _silu(x):
    return jax.nn.silu(x)

def _sigmoid(x):
    return jax.nn.sigmoid(x)

def _layernorm(x, axis=-1, eps=1e-05):
    m = jnp.mean(x, axis=axis, keepdims=True)
    v = jnp.var(x, axis=axis, keepdims=True)
    return (x - m) / jnp.sqrt(v + eps)

def _scatter_add(tgt, idx, src, axis=0):
    return tgt.at[idx].add(src)

def _segment_sum(src, seg, n):
    return jax.ops.segment_sum(src, seg, n)
kernel_name = 'mk_gnn_ffn_d1_gnn_r32_c3d6ba'

def setup_inputs(seed: int=0):
    np.random.seed(seed)
    _w = jnp.asarray

    def _rec_inputs():
        import jax
        import jax.numpy as jnp
        _gk = jax.random.key(seed)
        x = -0.0006008 + 1.001 * jax.random.normal(jax.random.fold_in(_gk, 1), (3125, 256), jnp.float32)
        _s = jax.random.randint(jax.random.fold_in(_gk, 2), (25000,), 0, 3125, jnp.int32)
        _d = jax.random.randint(jax.random.fold_in(_gk, 3), (25000,), 0, 3125, jnp.int32)
        _loop = jnp.arange(3125, dtype=jnp.int32)
        src = jnp.concatenate([_s, _d, _loop])
        dst = jnp.concatenate([_d, _s, _loop])
        _o = jnp.argsort(dst, stable=True)
        src = src[_o]
        dst = dst[_o]
        edge_attr_64 = 5.96457e-05 + 0.999887 * jax.random.normal(jax.random.fold_in(_gk, 12), (53125, 64), jnp.float32)
        node_vec1 = jax.random.uniform(jax.random.fold_in(_gk, 13), (3125, 1), jnp.float32, 0.0, 0.999943)
        return (x, src, dst, edge_attr_64, node_vec1)
    x, src, dst, edge_attr_64, node_vec1 = _rec_inputs()

    def _L0_gnn_setup():
        import jax, jax.numpy as jnp
        import numpy as np
        N_NODES = 10000
        N_EDGES = 5000
        IN_FEATS = 256
        E_DIMS = 64
        NEG_SLOPE = 0.01
        key = jax.random.key(seed)
        ks = jax.random.split(key, 8)
        h = jax.random.normal(ks[0], (N_NODES, IN_FEATS), dtype=jnp.float32)
        w = jax.random.normal(ks[1], (N_EDGES, E_DIMS), dtype=jnp.float32)
        snorm_n = jax.random.uniform(ks[2], (N_NODES, 1), dtype=jnp.float32)
        edge_src = jax.random.randint(ks[3], (N_EDGES,), 0, N_NODES, dtype=jnp.int64)
        edge_dst = jax.random.randint(ks[4], (N_EDGES,), 0, N_NODES, dtype=jnp.int64)
        W_self = jax.random.normal(ks[5], (IN_FEATS, IN_FEATS), dtype=jnp.float32) * np.sqrt(2.0 / IN_FEATS)
        W_func = jax.random.normal(ks[6], (IN_FEATS, IN_FEATS), dtype=jnp.float32) * np.sqrt(2.0 / IN_FEATS)
        W_att = jax.random.normal(ks[7], (1, 2 * IN_FEATS + E_DIMS), dtype=jnp.float32) * np.sqrt(2.0 / (2 * IN_FEATS + E_DIMS))
        return {'h': h, 'w': w, 'snorm_n': snorm_n, 'edge_src': edge_src, 'edge_dst': edge_dst, 'W_self': W_self, 'W_func': W_func, 'W_att': W_att}
    _L0_gnn_all = _L0_gnn_setup()
    _L0_gnn_in = {k: v for k, v in _L0_gnn_all.items() if k in ('W_self', 'W_func', 'W_att')}
    del _L0_gnn_all

    def _L0_ffn_setup():
        import jax, jax.numpy as jnp
        import numpy as np
        N_EXPERTS = 8
        TOP_K = 2
        key = jax.random.key(seed)
        ks = jax.random.split(key, 5)
        B, T, C, E, H = (8, 64, 256, 8, 682)
        scale = 1.0 / np.sqrt(C)
        return {'x': jax.random.normal(ks[0], (B, T, C), dtype=jnp.float32), 'router_w': jax.random.normal(ks[1], (E, C), dtype=jnp.float32) * scale, 'w1': jax.random.normal(ks[2], (E, H, C), dtype=jnp.float32) * scale, 'w2': jax.random.normal(ks[3], (E, C, H), dtype=jnp.float32) * (1.0 / np.sqrt(H)), 'w3': jax.random.normal(ks[4], (E, H, C), dtype=jnp.float32) * scale}
    _L0_ffn_all = _L0_ffn_setup()
    _L0_ffn_in = {k: v for k, v in _L0_ffn_all.items() if k in ('router_w', 'w1', 'w2', 'w3')}
    del _L0_ffn_all
    return {'x': x, 'src': src, 'dst': dst, 'edge_attr_64': edge_attr_64, 'node_vec1': node_vec1, 'L0_gnn_W_self': _L0_gnn_in['W_self'], 'L0_gnn_W_func': _L0_gnn_in['W_func'], 'L0_gnn_W_att': _L0_gnn_in['W_att'], 'L0_ffn_router_w': _L0_ffn_in['router_w'], 'L0_ffn_w1': _L0_ffn_in['w1'], 'L0_ffn_w2': _L0_ffn_in['w2'], 'L0_ffn_w3': _L0_ffn_in['w3']}

def reference(x, src, dst, edge_attr_64, node_vec1, L0_gnn_W_self, L0_gnn_W_func, L0_gnn_W_att, L0_ffn_router_w, L0_ffn_w1, L0_ffn_w2, L0_ffn_w3):
    import jax
    import jax.numpy as jnp

    def _L0_gnn_ref(h, w, snorm_n, edge_src, edge_dst, W_self, W_func, W_att):
        import jax, jax.numpy as jnp
        import numpy as np
        N_NODES = 10000
        N_EDGES = 5000
        IN_FEATS = 256
        E_DIMS = 64
        NEG_SLOPE = 0.01
        N = h.shape[0]
        h_s = h @ W_self.T
        z = h @ W_func.T
        concat_z = jnp.concatenate([z[edge_src], z[edge_dst], w], axis=-1)
        e = jax.nn.leaky_relu(concat_z @ W_att.T, negative_slope=NEG_SLOPE)[:, 0]
        m = jax.ops.segment_max(e, edge_dst, num_segments=N)
        e_exp = jnp.exp(e - m[edge_dst])
        denom = jax.ops.segment_sum(e_exp, edge_dst, num_segments=N)
        alpha = e_exp / denom[edge_dst]
        agg = jax.ops.segment_sum(alpha[:, None] * z[edge_src], edge_dst, num_segments=N)
        h_new = h_s + agg
        deg = jax.ops.segment_sum(jnp.ones_like(e), edge_dst, num_segments=N)
        h_new = jnp.where(deg[:, None] > 0, h_new, h)
        h_new = jax.nn.relu(h_new)
        return h + h_new

    def _L0_ffn_ref(x, router_w, w1, w2, w3):
        import jax, jax.numpy as jnp
        import numpy as np
        N_EXPERTS = 8
        TOP_K = 2
        B, T, C = x.shape
        flat = x.reshape(-1, C)
        logits = flat @ router_w.T
        probs = jax.nn.softmax(logits, axis=-1)
        topk_probs, topk_idx = jax.lax.top_k(probs, TOP_K)
        topk_probs = topk_probs / (jnp.sum(topk_probs, axis=-1, keepdims=True) + 1e-09)
        onehot = jax.nn.one_hot(topk_idx, N_EXPERTS, dtype=flat.dtype)
        gates = jnp.einsum('nk,nke->ne', topk_probs, onehot)
        h1 = jnp.einsum('nc,ehc->neh', flat, w1)
        h3 = jnp.einsum('nc,ehc->neh', flat, w3)
        h = jax.nn.silu(h1) * h3
        y = jnp.einsum('neh,ech->nec', h, w2)
        out = jnp.einsum('ne,nec->nc', gates, y)
        return out.reshape(B, T, C)
    x = x + _L0_gnn_ref(_layernorm(x, axis=-1), edge_attr_64, node_vec1, src, dst, L0_gnn_W_self, L0_gnn_W_func, L0_gnn_W_att)
    x = x + _L0_ffn_ref(_layernorm(x, axis=-1)[None], L0_ffn_router_w, L0_ffn_w1, L0_ffn_w2, L0_ffn_w3)[0]
    return x

_drawn_inputs = setup_inputs


def setup_inputs(seed=0):
    import zlib

    import numpy as np

    out = dict(_drawn_inputs(seed))
    spreads = {}
    factors = {}
    for name, (base, spread) in spreads.items():
        noise = np.random.default_rng([zlib.crc32(name.encode()), seed]).standard_normal(out[name].shape)
        drawn = base * np.exp(spread * noise) if base else spread * noise
        out[name] = jnp.asarray(drawn.astype(out[name].dtype))
    for name, factor in factors.items():
        out[name] = (out[name] * factor).astype(out[name].dtype)
    return out
```

```python
from contextlib import ExitStack

import concourse.bass as bass
from concourse import mybir

P = 128
N, C, EDGES, EF = 3125, 256, 53125, 64
E, H = 8, 682
TILES = -(-N // P)
NP = TILES * P
G = 256
KG = G // P
GROUPS = -(-EDGES // (4 * G)) * 4
RING = 4
PATH = GROUPS + TILES - 1
PAIRS = GROUPS * TILES
PAD_DST = TILES * P
ZR = C + 2
TR = C + E
KC = C // P
HC = [(a, min(P, H - a)) for a in range(0, H, P)]
NH = len(HC)
HA = 3 * P
HB = H - HA
W1_AT, W3_AT, W2_AT = 0, KC * H, 2 * KC * H
WE = W2_AT + NH * C
SLOTS = (2 * N + E * (P - 1)) // P
DUMP = NP
OUT_ROWS = NP + P
NODE_RING = 5
SLOPE = 0.01
QE = GROUPS * G // P
S2 = 2 * TILES
RE = TILES * E
LATE = S2 * SLOTS + 3 * H + NH * P + 2 * C
EPS = 1e-5
MASKED = -1e30
NO_MAX = -1e26
assert PATH % RING == 0 and PAIRS % RING == 0 and TILES % NODE_RING == 0 and SLOTS % RING == 0


def build(nc, x, src, dst, dst_last, wt, w_func, w_func_t, w_self_t, att_nodes, att_edge, router, experts,
          out):
    fp32, i32, bf16 = mybir.dt.float32, mybir.dt.int32, mybir.dt.bfloat16
    ALU, ACT, AX = mybir.AluOpType, mybir.ActivationFunctionType, mybir.AxisListType
    ztab = nc.dram_tensor("ztab", [NP, ZR], fp32, kind="Internal").ap()
    ttab = nc.dram_tensor("ttab", [NP, TR], fp32, kind="Internal").ap()

    with ExitStack() as ctx:
        def sb(name, shape, dt=fp32):
            return ctx.enter_context(nc.sbuf_tensor(name, shape, dt))

        def sem(name):
            return ctx.enter_context(nc.semaphore(name))

        W = sb("W", [P, E, WE])
        acc = sb("acc", [P, TILES * ZR])
        late = sb("late", [P, LATE])
        ident = sb("ident", [P, P])
        iota_row = sb("iota_row", [P, P])
        before = sb("before", [P, P])
        ones = sb("ones", [P, 2 * P])
        zero_rows = sb("zero_rows", [P, C])
        wself_sb = sb("wself_sb", [P, KC, C])
        router_sb = sb("router_sb", [P, KC, E])
        attn_e = sb("attn_e", [EF, P])
        attn_col = sb("attn_col", [EF, 1])
        att_n = sb("att_n", [P, KC, 2])
        node_id = sb("node_id", [P, TILES])
        valid = sb("valid", [P, TILES])
        thr = sb("thr", [P, TILES])
        scal = sb("scal", [P, TILES * 3])
        rstd = sb("rstd", [P, TILES])
        nmr = sb("nmr", [P, TILES])
        eps = sb("eps", [P, 1])
        inv_den = sb("inv_den", [P, TILES])
        has_edge = sb("has_edge", [P, TILES])
        no_edge = sb("no_edge", [P, TILES])
        logits = sb("logits", [P, TILES * E])
        path_i = sb("path_i", [1, PATH], i32)
        path_j = sb("path_j", [1, PATH], i32)
        flag = sb("flag", [1, 1], i32)
        expert_of = sb("expert_of", [1, SLOTS], i32)
        slot_rows = sb("slot_rows", [P, SLOTS * 2], i32)
        row_ix = sb("row_ix", [P, RING, 2], i32)
        xg = sb("xg", [P, RING, TR])
        xT = sb("xT", [P, 2, KC, P])
        tick = sb("tick", [P, 1])

        def carve(region, at, shape, dt=fp32):
            n = 1
            for d in shape:
                n *= d
            words = n if dt != bf16 else n // 2
            v = region[:, at:at + words]
            if dt != fp32:
                v = v.bitcast(dt)
            if len(shape) == 2:
                v = v.rearrange("p (a b) -> p a b", b=shape[1])
            return v, at + words

        z, o = W[:, 3, :], 0
        dst_here, o = carve(z, o, [QE], i32)
        dst_next, o = carve(z, o, [QE], i32)
        falls, o = carve(z, o, [QE])
        last_dst, o = carve(z, o, [2], i32)
        last_f, o = carve(z, o, [2])
        start, o = carve(z, o, [2])
        ge_thr, o = carve(z, o, [TILES])
        step_no, o = carve(z, o, [PATH])
        begun, o = carve(z, o, [2, PATH])
        fell, o = carve(z, o, [1])
        io_i, o = carve(z, o, [P], i32)
        io_s, o = carve(z, o, [PATH], i32)
        io_t, o = carve(z, o, [TILES], i32)
        io_n, o = carve(z, o, [TILES], i32)
        assert o <= WE
        z, o = W[:, 4, :], 0
        wfx, o = carve(z, o, [KC, ZR])
        wf_nat, o = carve(z, o, [KC, C])
        hnT, o = carve(z, o, [NODE_RING, C])
        hn1, o = carve(z, o, [NODE_RING, C])
        st6, o = carve(z, o, [NODE_RING, 6])
        mv2, o = carve(z, o, [NODE_RING, 2])
        norm2, o = carve(z, o, [NODE_RING, 3])
        assert o <= WE
        z, o = W[:, 5, :], 0
        x_in, o = carve(z, o, [NODE_RING, C])
        hn, o = carve(z, o, [NODE_RING, C])
        z_out, _ = carve(z, o, [NODE_RING, ZR])
        x2, _ = carve(z, o, [NODE_RING, C])
        assert o + NODE_RING * ZR <= WE
        z, o = W[:, 6, :], 0
        zg, o = carve(z, o, [RING * KG, ZR])
        wt_in, o = carve(z, o, [RING, G])
        dst_in, o = carve(z, o, [RING, G], i32)
        src_in, o = carve(z, o, [RING, KG], i32)
        assert o <= WE
        o = 0
        x_hn, o = carve(z, o, [NODE_RING, C])
        idle, o = carve(z, o, [NODE_RING, C])
        hn2T, o = carve(z, o, [NODE_RING, C])
        assert o <= WE
        z, o = W[:, 7, :], 0
        score, o = carve(z, o, [2, G])
        e_hi, o = carve(z, o, [2, G])
        e_lo, o = carve(z, o, [2, G])
        prob, o = carve(z, o, [2, G])
        probT, o = carve(z, o, [2, G])
        mask, o = carve(z, o, [G])
        bias, o = carve(z, o, [2, 3])
        corr, o = carve(z, o, [RING])
        small, o = carve(z, o, [4])
        assert o <= WE
        ohr, o = carve(acc, 0, [S2, P], bf16)
        oht, o = carve(acc, o, [S2, SLOTS], bf16)
        iota_b, o = carve(acc, o, [P], bf16)
        slots_f, o = carve(acc, o, [S2])
        slots_i, o = carve(acc, o, [S2], i32)
        st_i, o = carve(acc, o, [S2], i32)
        sr_i, o = carve(acc, o, [S2], i32)
        st_f, o = carve(acc, o, [S2])
        sr_f, o = carve(acc, o, [S2])
        st_b, o = carve(acc, o, [S2], bf16)
        sr_b, o = carve(acc, o, [S2], bf16)
        tile_b, o = carve(acc, o, [S2], bf16)
        io_slot, o = carve(acc, o, [SLOTS], i32)
        slot_no, o = carve(acc, o, [SLOTS])
        slot_b, o = carve(acc, o, [SLOTS], bf16)
        tok, o = carve(acc, o, [SLOTS])
        unused, o = carve(acc, o, [SLOTS])
        row_f, o = carve(acc, o, [SLOTS])
        exp_cmp, o = carve(acc, o, [SLOTS, E - 1])
        exp_f, o = carve(acc, o, [SLOTS])
        p_plus1, o = carve(acc, o, [1])
        dump_p, o = carve(acc, o, [1])
        io_p, o = carve(acc, o, [1], i32)
        exp_neg, o = carve(acc, o, [E])
        io_e, o = carve(acc, o, [E], i32)
        assert o <= TILES * ZR
        moving, behind = carve(late, 0, [S2, 2 * SLOTS], bf16)
        o = behind
        s_act, o = carve(late, o, [H])
        hid, o = carve(late, o, [2, H])
        hidT, o = carve(late, o, [NH * P])
        y_out, o = carve(late, o, [2, C])
        assert o <= LATE
        o = behind
        ex, o = carve(late, o, [TILES, E])
        probs, o = carve(late, o, [TILES, E])
        rest, o = carve(late, o, [TILES, E])
        eq, o = carve(late, o, [TILES, E])
        cand, o = carve(late, o, [TILES, E])
        top0, o = carve(late, o, [TILES, E])
        top1, o = carve(late, o, [TILES, E])
        both, o = carve(late, o, [TILES, E])
        gates, o = carve(late, o, [TILES, E])
        cum, o = carve(late, o, [E, TILES])
        cum_ex, o = carve(late, o, [E, TILES])
        slot, o = carve(late, o, [E, TILES])
        tmp_ej, o = carve(late, o, [E, TILES])
        t25, o = carve(late, o, [6, TILES])
        e8, o = carve(late, o, [6, E])
        assert o <= LATE
        Wf = W[:, :, :].rearrange("p e w -> p (e w)")
        xg_flat = xg[:, :, :].rearrange("p a b -> p (a b)")

        ps = [ctx.enter_context(nc.psum_tensor(f"bank{b}", [P, 512], fp32)) for b in range(8)]

        pool_consts = sem("pool_consts")
        blank = sem("blank")
        late_ramps = sem("late_ramps")
        eps_ready = sem("eps_ready")
        attn_ready = sem("attn_ready")
        weights_in = sem("weights_in")
        x_loaded = [sem(f"x_loaded{k}") for k in range(NODE_RING)]
        z_stored = [sem(f"z_stored{k}") for k in range(NODE_RING)]
        att_psum = sem("att_psum")
        wfx_ready = sem("wfx_ready")
        bn_done = sem("bn_done")
        stats_ready = sem("stats_ready")
        std_ready = sem("std_ready")
        rstd_ready = sem("rstd_ready")
        hn_ready = sem("hn_ready")
        hnT_psum = sem("hnT_psum")
        hnT_ready = sem("hnT_ready")
        z_psum = sem("z_psum")
        z_ready = sem("z_ready")
        chain = sem("chain")
        dst_flat_in = sem("dst_flat_in")
        begun_ready = sem("begun_ready")
        path_psum = sem("path_psum")
        path_ready = sem("path_ready")
        src_loaded = [sem(f"src_loaded{k}") for k in range(RING)]
        edge_loaded = [sem(f"edge_loaded{k}") for k in range(RING)]
        z_gathered = [sem(f"z_gathered{k}") for k in range(RING)]
        scores_psum = sem("scores_psum")
        masked = sem("masked")
        max_done = sem("max_done")
        plus_s2 = sem("plus_s2")
        leaky_done = sem("leaky_done")
        newmax_done = sem("newmax_done")
        bias_ready = sem("bias_ready")
        run_done = sem("run_done")
        exps_done = sem("exps_done")
        prob_ready = sem("prob_ready")
        probT_psum = sem("probT_psum")
        probT_ready = sem("probT_ready")
        sum_psum = sem("sum_psum")
        acc_done = sem("acc_done")
        steps_over = sem("steps_over")
        den_ready = sem("den_ready")
        x_again = [sem(f"x_again{k}") for k in range(NODE_RING)]
        hn1_ready = sem("hn1_ready")
        idle_ready = sem("idle_ready")
        xhn_ready = sem("xhn_ready")
        hn1T_psum = sem("hn1T_psum")
        hn1T_ready = sem("hn1T_ready")
        hs_psum = sem("hs_psum")
        with_hs = sem("with_hs")
        or_idle = sem("or_idle")
        x2_ready = sem("x2_ready")
        bn2_done = sem("bn2_done")
        stats2_ready = sem("stats2_ready")
        std2_ready = sem("std2_ready")
        rstd2_ready = sem("rstd2_ready")
        norm2_ready = sem("norm2_ready")
        hn2_ready = sem("hn2_ready")
        hn2T_psum = sem("hn2T_psum")
        hn2T_ready = sem("hn2T_ready")
        logit_psum = sem("logit_psum")
        logit_ready = sem("logit_ready")
        x2_stored = [sem(f"x2_stored{k}") for k in range(NODE_RING)]
        hn2_stored = [sem(f"hn2_stored{k}") for k in range(NODE_RING)]
        dump_stored = sem("dump_stored")
        shifted = sem("shifted")
        exp_ready = sem("exp_ready")
        gates_ready = sem("gates_ready")
        gates_stored = sem("gates_stored")
        choice_ready = sem("choice_ready")
        rank_psum = sem("rank_psum")
        onehot_ready = sem("onehot_ready")
        token_psum = sem("token_psum")
        slots_ready = sem("slots_ready")
        experts_in = [sem(f"experts_in{e}") for e in range(E)]
        ix_ready = sem("ix_ready")
        row_gathered = [sem(f"row_gathered{k}") for k in range(RING)]
        xT_psum = sem("xT_psum")
        xT_ready = sem("xT_ready")
        up_a_psum = sem("up_a_psum")
        up_b_psum = sem("up_b_psum")
        silu_a = sem("silu_a")
        silu_b = sem("silu_b")
        hid_a_ready = sem("hid_a_ready")
        hid_b_ready = sem("hid_b_ready")
        hidT_psum = sem("hidT_psum")
        hidT_by_act = sem("hidT_by_act")
        hidT_by_dve = sem("hidT_by_dve")
        y_psum = sem("y_psum")
        y_ready = sem("y_ready")
        y_added = sem("y_added")
        passed = {str(eng.engine): sem(f"passed{n}") for n, eng in enumerate((nc.vector, nc.gpsimd))}
        block = ctx.enter_context(nc.Block())

        def run(eng, total, ring, peel, stages):
            def turn(r, k):
                for lag, stage in stages:
                    q, kk = divmod(k - lag, ring)
                    t = r * ring + (k - lag)
                    if isinstance(t, int) and not 0 <= t < total:
                        continue
                    stage(t, kk, r + q)
            for r in range(peel):
                for k in range(ring):
                    turn(r, k)
            with eng.Fori(peel, total // ring) as r:
                for k in range(ring):
                    turn(r, k)
            for k in range(max(lag for lag, _ in stages)):
                turn(total // ring, k)

        def at_least(t, n):
            return not isinstance(t, int) or t >= n

        def bank_back(k):
            return 1 if k == 0 else 2

        def held(eng):
            eng.sem_inc(passed[str(eng.engine)], 1)

        def cols(t, n, width=None):
            return bass.ds(t * n, n if width is None else width)

        class Sorted:
            total = PATH

            def group(self, eng, s):
                return eng.value_load(path_i[0:1, bass.ds(s, 1)], min_val=0, max_val=GROUPS - 1)

            def tile(self, eng, s):
                return eng.value_load(path_j[0:1, bass.ds(s, 1)], min_val=0, max_val=TILES - 1)

        class Unsorted:
            total = PAIRS

            def group(self, eng, s):
                return s % GROUPS

            def tile(self, eng, s):
                return s // GROUPS

        def branch(eng, steps):
            eng.wait_ge(path_ready, 1)
            falls_at = eng.value_load(flag[0:1, 0:1], min_val=0, max_val=1)
            with eng.If(falls_at == 0):
                steps(Sorted())
            with eng.Else():
                steps(Unsorted())
            eng.sem_inc(steps_over, 1)
            eng.wait_ge(steps_over, 5)

        @block.sync
        def _(sp):
            sp.dma_start(wf_nat, w_func.rearrange("(k p) c -> p k c", p=P)).then_inc(weights_in, 16)
            sp.dma_start(wfx[:, :, 0:C], w_func_t.rearrange("(k p) c -> p k c", p=P))\
                .then_inc(weights_in, 16)
            sp.dma_start(att_n[:, :, :], att_nodes.rearrange("(k p) c -> p k c", p=P))\
                .then_inc(weights_in, 16)
            for k in range(NODE_RING):
                sp.dma_start(x_in[:, k, :], x[cols(k, P), :]).then_inc(x_loaded[k], 16)
            sp.dma_start(wself_sb[:, :, :], w_self_t.rearrange("(k p) c -> p k c", p=P))\
                .then_inc(weights_in, 16)
            sp.dma_start(router_sb[:, :, :], router.rearrange("(k p) c -> p k c", p=P))\
                .then_inc(weights_in, 16)
            sp.dma_start(attn_col[:, :], att_edge).then_inc(weights_in, 16)
            flat = dst.rearrange("g e -> (g e)")
            sp.dma_start(dst_here, flat[0:P * QE].rearrange("(p q) -> p q", q=QE)).then_inc(dst_flat_in, 16)
            sp.dma_start(dst_next, flat[1:P * QE + 1].rearrange("(p q) -> p q", q=QE)).then_inc(dst_flat_in, 16)
            sp.dma_start(last_dst, dst_last).then_inc(dst_flat_in, 16)

            def x_load(t, k, r):
                if at_least(t, NODE_RING):
                    sp.wait_ge(hn_ready, t - NODE_RING + 1)
                    sp.dma_start(x_in[:, k, :], x[cols(t, P), :]).then_inc(x_loaded[k], 16)

            def z_store(t, k, r):
                sp.wait_ge(z_ready, t + 1)
                sp.dma_start(ztab[cols(t, P), :], z_out[:, k, :]).then_inc(z_stored[k], 16)

            run(sp, TILES, NODE_RING, 2, [(0, x_load), (3, z_store)])
            for e in range(3):
                sp.dma_start(W[:, e, :], experts[e, :, :]).then_inc(experts_in[e], 16)
            sp.wait_ge(path_ready, 1)
            sp.dma_start(W[:, 3, :], experts[3, :, :]).then_inc(experts_in[3], 16)
            sp.wait_ge(pool_consts, 8)
            sp.dma_start(out[DUMP:OUT_ROWS, :], zero_rows[:, :]).then_inc(dump_stored, 16)

            def steps(way):
                def load(s, k, r):
                    g = way.group(sp, s)
                    if at_least(s, RING):
                        sp.wait_ge(z_gathered[k], 16 * KG * r)
                    sp.dma_start(src_in[:, k, :], src[bass.ds(g, 1), :, :].rearrange("g p k -> p (g k)"))\
                        .then_inc(src_loaded[k], 16)
                    if at_least(s, RING):
                        sp.wait_ge(scores_psum, s - RING + 1)
                        sp.wait_ge(masked, s - RING + 1)
                    sp.dma_start(wt_in[0:EF, k, :], wt[bass.ds(g, 1), :, :].rearrange("g p k -> p (g k)"))\
                        .then_inc(edge_loaded[k], 16)
                    sp.dma_start(dst_in[:, k, :], dst[bass.ds(g, 1), :].to_broadcast([P, G]))\
                        .then_inc(edge_loaded[k], 16)
                run(sp, way.total, RING, 1, [(0, load)])
            branch(sp, steps)

            def x_load_again(t, k, r):
                if at_least(t, NODE_RING):
                    sp.wait_ge(xhn_ready, t - NODE_RING + 1)
                    sp.wait_ge(hn1_ready, t - NODE_RING + 1)
                sp.dma_start(x_in[:, k, :], x[cols(t, P), :]).then_inc(x_again[k], 16)

            def x2_store(t, k, r):
                sp.wait_ge(x2_ready, t + 1)
                sp.dma_start(out[cols(t, P), :], x2[:, k, :]).then_inc(x2_stored[k], 16)

            def hn2_store(t, k, r):
                sp.wait_ge(hn2_ready, t + 1)
                sp.dma_start(ttab[cols(t, P), 0:C], hn[:, k, :]).then_inc(hn2_stored[k], 16)

            run(sp, TILES, NODE_RING, 2, [(0, x_load_again), (3, x2_store), (4, hn2_store)])
            sp.wait_ge(logit_ready, TILES)
            for k in range(NODE_RING):
                sp.wait_ge(x2_stored[k], 16 * (TILES // NODE_RING))
                sp.wait_ge(hn2_stored[k], 16 * (TILES // NODE_RING))
            for e in range(4, E):
                sp.dma_start(W[:, e, :], experts[e, :, :]).then_inc(experts_in[e], 16)
            sp.wait_ge(gates_ready, 1)
            sp.dma_start(ttab[:, C:TR].rearrange("(t p) e -> p t e", p=P), gates).then_inc(gates_stored, 16)
            sp.wait_ge(gates_stored, 16)
            sp.wait_ge(dump_stored, 16)
            sp.wait_ge(y_added, 16 * SLOTS)

        @block.gpsimd
        def _(pool):
            nc.gpsimd.memset(ident[:, :], 0.0).then_inc(blank, 1)
            nc.gpsimd.memset(before[:, :], 1.0).then_inc(blank, 1)
            nc.gpsimd.memset(ones[:, :], 1.0).then_inc(pool_consts, 1)
            pool.wait_ge(blank, 2)
            nc.gpsimd.affine_select(out=ident[:, :], in_=ident[:, :], compare_op=ALU.not_equal, fill=1.0,
                                    base=0, pattern=[[-1, P]], channel_multiplier=1).then_inc(pool_consts, 1)
            nc.gpsimd.affine_select(out=before[:, :], in_=before[:, :], compare_op=ALU.is_gt, fill=0.0,
                                    base=0, pattern=[[1, P]], channel_multiplier=-1).then_inc(pool_consts, 1)
            nc.gpsimd.iota(io_i, pattern=[[1, P]], base=0, channel_multiplier=0).then_inc(pool_consts, 1)
            nc.gpsimd.iota(io_n, pattern=[[P, TILES]], base=0, channel_multiplier=1).then_inc(pool_consts, 1)
            nc.gpsimd.iota(io_t, pattern=[[P, TILES]], base=P, channel_multiplier=0).then_inc(pool_consts, 1)
            nc.gpsimd.iota(io_s, pattern=[[1, PATH]], base=0, channel_multiplier=0).then_inc(pool_consts, 1)
            nc.gpsimd.memset(zero_rows[:, :], 0.0).then_inc(pool_consts, 1)
            for k in range(NODE_RING):
                pool.wait_ge(z_stored[k], 16 * (TILES // NODE_RING))

            def steps(way):
                def gather(s, k, r):
                    pool.wait_ge(src_loaded[k], 16 * (r + 1))
                    if at_least(s, RING):
                        pool.wait_ge(sum_psum, s - RING + 1)
                    held(pool)
                    for c in range(KG):
                        nc.gpsimd.indirect_dma_start(
                            out=zg[:, k * KG + c, :], out_offset=None, in_=ztab,
                            in_offset=bass.IndirectOffsetOnAxis(ap=src_in[:, k, c:c + 1], axis=0))\
                            .then_inc(z_gathered[k], 16)
                run(pool, way.total, RING, 1, [(0, gather)])
            branch(pool, steps)

            def x_plus_hn(t, k, r):
                pool.wait_ge(hn1_ready, t + 1)
                if at_least(t, NODE_RING):
                    pool.wait_ge(x2_ready, t - NODE_RING + 1)
                nc.gpsimd.tensor_tensor(x_hn[:, k, :], x_in[:, k, :], hn1[:, k, :], ALU.add)\
                    .then_inc(xhn_ready, 1)

            run(pool, TILES, NODE_RING, 1, [(0, x_plus_hn)])
            pool.wait_ge(x2_ready, TILES)
            nc.gpsimd.iota(io_slot, pattern=[[1, SLOTS]], base=0, channel_multiplier=0).then_inc(late_ramps, 1)
            nc.gpsimd.iota(io_p, pattern=[[0, 1]], base=1, channel_multiplier=1).then_inc(late_ramps, 1)
            nc.gpsimd.iota(io_e, pattern=[[1, E]], base=-E, channel_multiplier=0).then_inc(late_ramps, 1)

            pool.wait_ge(gates_stored, 16)
            pool.wait_ge(dump_stored, 16)
            for k in range(NODE_RING):
                pool.wait_ge(x2_stored[k], 16 * (TILES // NODE_RING))
                pool.wait_ge(hn2_stored[k], 16 * (TILES // NODE_RING))
            pool.wait_ge(slots_ready, 1)

            def add(t, k, r):
                pool.wait_ge(y_ready, t + 1)
                held(pool)
                nc.gpsimd.indirect_dma_start(
                    out=out, out_offset=bass.IndirectOffsetOnAxis(ap=row_ix[:, k, 1:2], axis=0),
                    in_=y_out[:, k % 2, :], in_offset=None, compute_op=ALU.add).then_inc(y_added, 16)
                pool.wait_ge(y_added, 16 * (t + 1))

            def gather_rows(t, k, r):
                nc.gpsimd.tensor_copy(row_ix[:, k, :], slot_rows[:, cols(t, 2)]).then_inc(ix_ready, 1)
                pool.wait_ge(ix_ready, t + 1)
                held(pool)
                nc.gpsimd.indirect_dma_start(
                    out=xg[:, k, :], out_offset=None, in_=ttab,
                    in_offset=bass.IndirectOffsetOnAxis(ap=row_ix[:, k, 0:1], axis=0))\
                    .then_inc(row_gathered[k], 16)

            run(pool, SLOTS, RING, 1, [(3, add), (0, gather_rows)])

        @block.scalar
        def _(act):
            act.wait_ge(eps_ready, 1)

            def std(t, k, r):
                act.wait_ge(stats_ready, t + 1)
                nc.scalar.activation(norm2[:, k, 0:1], mv2[:, k, 1:2], ACT.Sqrt, bias=eps[:, 0:1])\
                    .then_inc(std_ready, 1)

            def hnT_copy(t, k, r):
                act.wait_ge(hnT_psum, t + 1)
                if at_least(t, NODE_RING):
                    act.wait_ge(z_psum, t - NODE_RING + 1)
                nc.scalar.activation(hnT[:, k, :], ps[k % 2][:, 0:C], ACT.Copy).then_inc(hnT_ready, 1)

            run(act, TILES, NODE_RING, 2, [(0, std), (1, hnT_copy)])

            def steps(way):
                def exps(s, k, r):
                    b = k % 2
                    act.wait_ge(bias_ready, s + 1)
                    if at_least(s, 2):
                        act.wait_ge(prob_ready, s - 1)
                    nc.scalar.activation(e_hi[:, b, :], score[:, b, :], ACT.Exp, bias=bias[:, b, 0:1],
                                         scale=1.0).then_inc(exps_done, 1)
                    nc.scalar.activation(e_lo[:, b, :], score[:, b, :], ACT.Exp, bias=bias[:, b, 1:2],
                                         scale=SLOPE).then_inc(exps_done, 1)
                    if at_least(s, RING):
                        act.wait_ge(acc_done, s - RING + 1)
                    nc.scalar.activation(corr[:, k:k + 1], bias[:, b, 2:3], ACT.Exp).then_inc(exps_done, 1)

                def probT_copy(s, k, r):
                    act.wait_ge(probT_psum, s + 1)
                    if at_least(s, 2):
                        act.wait_ge(sum_psum, s - 1)
                    nc.scalar.activation(probT[:, k % 2, :], ps[2 + k % 2][:, 0:G], ACT.Copy)\
                        .then_inc(probT_ready, 1)
                run(act, way.total, RING, 1, [(0, exps), (1, probT_copy)])
            branch(act, steps)

            act.wait_ge(den_ready, 1)

            def hn_again(t, k, r):
                act.wait_ge(x_again[k], 16 * (r + 1))
                if at_least(t, NODE_RING):
                    act.wait_ge(xhn_ready, t - NODE_RING + 1)
                    act.wait_ge(hn1T_psum, t - NODE_RING + 1)
                nc.scalar.activation(hn1[:, k, :], x_in[:, k, :], ACT.Identity, bias=nmr[:, bass.ds(t, 1)],
                                     scale=rstd[:, bass.ds(t, 1)]).then_inc(hn1_ready, 1)
                act.wait_ge(hn1_ready, t + 1)
                if at_least(t, NODE_RING):
                    act.wait_ge(or_idle, t - NODE_RING + 1)
                nc.scalar.activation(idle[:, k, :], hn1[:, k, :], ACT.Copy,
                                     scale=no_edge[:, bass.ds(t, 1)]).then_inc(idle_ready, 1)

            def hn1T_copy(t, k, r):
                act.wait_ge(hn1T_psum, t + 1)
                if at_least(t, NODE_RING):
                    act.wait_ge(hs_psum, t - NODE_RING + 1)
                nc.scalar.activation(hnT[:, k, :], ps[k % 2][:, 0:C], ACT.Copy).then_inc(hn1T_ready, 1)

            def std2(t, k, r):
                act.wait_ge(stats2_ready, t + 1)
                nc.scalar.activation(norm2[:, k, 0:1], mv2[:, k, 1:2], ACT.Sqrt, bias=eps[:, 0:1])\
                    .then_inc(std2_ready, 1)

            def hn_second(t, k, r):
                act.wait_ge(norm2_ready, t + 1)
                if at_least(t, NODE_RING):
                    act.wait_ge(hn2_stored[k], 16 * r)
                    act.wait_ge(hn2T_psum, t - NODE_RING + 1)
                nc.scalar.activation(hn[:, k, :], x2[:, k, :], ACT.Identity, bias=norm2[:, k, 2:3],
                                     scale=norm2[:, k, 1:2]).then_inc(hn2_ready, 1)

            def hn2T_copy(t, k, r):
                act.wait_ge(hn2T_psum, t + 1)
                if at_least(t, NODE_RING):
                    act.wait_ge(logit_psum, t - NODE_RING + 1)
                nc.scalar.activation(hn2T[:, k, :], ps[4 + k % 2][:, 0:C], ACT.Copy).then_inc(hn2T_ready, 1)

            run(act, TILES, NODE_RING, 2, [(0, hn_again), (1, hn1T_copy), (2, std2), (3, hn_second),
                                           (4, hn2T_copy)])

            act.wait_ge(shifted, 1)
            nc.scalar.activation(ex, probs, ACT.Exp).then_inc(exp_ready, 1)

            act.wait_ge(slots_ready, 1)

            def xT_copy(t, k, r):
                act.wait_ge(xT_psum, t + 1)
                if at_least(t, 2):
                    act.wait_ge(up_b_psum, t - 1)
                nc.scalar.activation(xT[:, k % 2, :, :].rearrange("p k c -> p (k c)"), ps[4][:, 0:C], ACT.Copy)\
                    .then_inc(xT_ready, 1)

            def silu_first(t, k, r):
                if at_least(t, 1):
                    act.wait_ge(hid_a_ready, t)
                act.wait_ge(up_a_psum, t + 1)
                nc.scalar.activation(s_act[:, 0:HA], ps[0][:, 0:HA], ACT.Silu).then_inc(silu_a, 1)

            def hidT_copy(t, k, r):
                act.wait_ge(hidT_psum, t + 1)
                if at_least(t, 1):
                    act.wait_ge(y_psum, t)
                nc.scalar.activation(hidT[:, 0:4 * P], ps[6][:, 0:4 * P], ACT.Copy).then_inc(hidT_by_act, 1)

            def silu_second(t, k, r):
                if at_least(t, 1):
                    act.wait_ge(hid_b_ready, t)
                act.wait_ge(up_b_psum, t + 1)
                nc.scalar.activation(s_act[:, HA:H], ps[2][:, 0:HB], ACT.Silu).then_inc(silu_b, 1)

            run(act, SLOTS, RING, 1, [(1, silu_first), (2, hidT_copy), (1, silu_second), (0, xT_copy)])

        @block.tensor
        def _(pe):
            mm, tr = nc.tensor.matmul, nc.tensor.transpose
            pe.wait_ge(pool_consts, 2)
            pe.wait_ge(weights_in, 96)
            for m in range(KC):
                for k in range(KC):
                    last = mm(ps[7][:, 2 * m:2 * m + 2], wf_nat[:, k, m * P:(m + 1) * P], att_n[:, k, :],
                              start=(k == 0), stop=(k == KC - 1))
            last.then_inc(att_psum, 1)
            pe.wait_ge(wfx_ready, 1)

            def transposed(bank, rows_ap):
                for c in range(KC):
                    last = tr(bank[:, c * P:(c + 1) * P], rows_ap[:, c * P:(c + 1) * P], ident[:, :])
                return last

            def hn_T(t, k, r):
                pe.wait_ge(hn_ready, t + 1)
                if at_least(t, 1):
                    pe.wait_ge(hnT_ready, t + 1 - bank_back(k) if at_least(t, 2) else t)
                transposed(ps[k % 2], hn[:, k, :]).then_inc(hnT_psum, 1)

            def z_of(t, k, r):
                pe.wait_ge(hnT_ready, t + 1)
                if at_least(t, 2):
                    pe.wait_ge(z_ready, t + 1 - bank_back(k))
                for c in range(KC):
                    last = mm(ps[2 + k % 2][:, 0:ZR], hnT[:, k, c * P:(c + 1) * P], wfx[:, c, :],
                              start=(c == 0), stop=(c == KC - 1))
                last.then_inc(z_psum, 1)

            run(pe, TILES, NODE_RING, 2, [(0, hn_T), (1, z_of)])

            pe.wait_ge(begun_ready, 1)
            mm(ps[5][0:1, 0:PATH], ones[:, 0:1], begun[:, 0, :], start=True, stop=False)
            mm(ps[5][0:1, 0:PATH], ones[0:GROUPS - 1 - P, 0:1], begun[0:GROUPS - 1 - P, 1, :],
               start=False, stop=True)
            mm(ps[6][0:1, 0:1], fell, ones[:, 0:1], start=True, stop=True).then_inc(path_psum, 1)

            def steps(way):
                def scores(s, k, r):
                    b = k % 2
                    pe.wait_ge(edge_loaded[k], 32 * (r + 1))
                    if at_least(s, 2):
                        pe.wait_ge(max_done, s - 1)
                    mm(ps[b][:, 0:G], attn_e[:, :], wt_in[0:EF, k, :], start=True, stop=False)
                    pe.wait_ge(z_gathered[k], 16 * KG * (r + 1))
                    for c in range(KG):
                        s1 = zg[:, k * KG + c, C:C + 1].to_broadcast([P, P])
                        last = mm(ps[b][:, c * P:(c + 1) * P], s1, ident[:, :], start=False, stop=(c == KG - 1))
                    last.then_inc(scores_psum, 1)

                def prob_T(s, k, r):
                    b = k % 2
                    pe.wait_ge(prob_ready, s + 1)
                    if at_least(s, 2):
                        pe.wait_ge(probT_ready, s - 1)
                    transposed(ps[2 + b], prob[:, b, :]).then_inc(probT_psum, 1)

                def weighted(s, k, r):
                    b = k % 2
                    pe.wait_ge(probT_ready, s + 1)
                    if at_least(s, 2):
                        pe.wait_ge(acc_done, s - 1)
                    for c in range(KG):
                        last = mm(ps[4 + b][:, 0:ZR], probT[:, b, c * P:(c + 1) * P], zg[:, k * KG + c, :],
                                  start=(c == 0), stop=(c == KG - 1))
                    last.then_inc(sum_psum, 1)
                run(pe, way.total, RING, 1, [(0, scores), (1, prob_T), (2, weighted)])
            pe.wait_ge(attn_ready, 1)
            branch(pe, steps)

            def hn1_T(t, k, r):
                pe.wait_ge(hn1_ready, t + 1)
                if at_least(t, 1):
                    pe.wait_ge(hn1T_ready, t + 1 - bank_back(k) if at_least(t, 2) else t)
                transposed(ps[k % 2], hn1[:, k, :]).then_inc(hn1T_psum, 1)

            def self_part(t, k, r):
                pe.wait_ge(hn1T_ready, t + 1)
                if at_least(t, 2):
                    pe.wait_ge(with_hs, t + 1 - bank_back(k))
                for c in range(KC):
                    last = mm(ps[2 + k % 2][:, 0:C], hnT[:, k, c * P:(c + 1) * P], wself_sb[:, c, :],
                              start=(c == 0), stop=(c == KC - 1))
                last.then_inc(hs_psum, 1)

            def hn2_T(t, k, r):
                pe.wait_ge(hn2_ready, t + 1)
                if at_least(t, 1):
                    pe.wait_ge(hn2T_ready, t + 1 - bank_back(k) if at_least(t, 2) else t)
                transposed(ps[4 + k % 2], hn[:, k, :]).then_inc(hn2T_psum, 1)

            def logits_of(t, k, r):
                pe.wait_ge(hn2T_ready, t + 1)
                if at_least(t, 2):
                    pe.wait_ge(logit_ready, t + 1 - bank_back(k))
                for c in range(KC):
                    last = mm(ps[6 + k % 2][:, 0:E], hn2T[:, k, c * P:(c + 1) * P], router_sb[:, c, :],
                              start=(c == 0), stop=(c == KC - 1))
                last.then_inc(logit_psum, 1)

            run(pe, TILES, NODE_RING, 2, [(0, hn1_T), (1, self_part), (3, hn2_T), (4, logits_of)])

            pe.wait_ge(choice_ready, 1)
            pe.wait_ge(pool_consts, 3)
            chosen = both.rearrange("p t e -> p e t")
            mm(ps[0][:, 0:RE], before[:, :], chosen, start=True, stop=True)
            mm(ps[1][:, 0:RE], ones[:, 0:P], chosen, start=True, stop=True).then_inc(rank_psum, 1)
            pe.wait_ge(onehot_ready, 1)
            for q in range(S2):
                last = mm(ps[2][:, 0:2 * SLOTS], ohr[:, q, :], moving[:, q, :], start=(q == 0),
                          stop=(q == S2 - 1))
            last.then_inc(token_psum, 1)

            pe.wait_ge(slots_ready, 1)
            for e in range(E):
                pe.wait_ge(experts_in[e], 16)

            def expert(t):
                return pe.value_load(expert_of[0:1, bass.ds(t, 1)], min_val=0, max_val=E - 1)

            def tokens_T(t, k, r):
                pe.wait_ge(row_gathered[k], 16 * (r + 1))
                if at_least(t, 1):
                    pe.wait_ge(xT_ready, t)
                transposed(ps[4], xg[:, k, 0:C]).then_inc(xT_psum, 1)

            def up(e, k, lo, n, banks):
                for bank, at in zip(banks, (W1_AT, W3_AT)):
                    for c in range(KC):
                        last = mm(bank[:, 0:n], xT[:, k % 2, c, :], Wf[:, bass.ds(e * WE + (at + c * H + lo), n)],
                                  start=(c == 0), stop=(c == KC - 1))
                return last

            def up_first(t, k, r):
                e = expert(t)
                pe.wait_ge(xT_ready, t + 1)
                if at_least(t, 1):
                    pe.wait_ge(hid_a_ready, t)
                up(e, k, 0, HA, (ps[0], ps[1])).then_inc(up_a_psum, 1)

            def up_second(t, k, r):
                e = expert(t)
                if at_least(t, 1):
                    pe.wait_ge(hid_b_ready, t)
                up(e, k, HA, HB, (ps[2], ps[3])).then_inc(up_b_psum, 1)

            def hidden_T(t, k, r):
                pe.wait_ge(hid_a_ready, t + 1)
                pe.wait_ge(hid_b_ready, t + 1)
                if at_least(t, 1):
                    pe.wait_ge(hidT_by_act, t)
                    pe.wait_ge(hidT_by_dve, t)
                for i, (a, n) in enumerate(HC):
                    last = tr(ps[6 + i // 4][0:n, (i % 4) * P:(i % 4 + 1) * P], hid[:, k % 2, a:a + n],
                              ident[:, :])
                last.then_inc(hidT_psum, 1)

            def down(t, k, r):
                e = expert(t)
                pe.wait_ge(hidT_by_act, t + 1)
                pe.wait_ge(hidT_by_dve, t + 1)
                if at_least(t, 1):
                    pe.wait_ge(y_ready, t)
                for i, (a, n) in enumerate(HC):
                    last = mm(ps[5][:, 0:C], hidT[0:n, i * P:(i + 1) * P],
                              Wf[0:n, bass.ds(e * WE + (W2_AT + i * C), C)], start=(i == 0), stop=(i == NH - 1))
                last.then_inc(y_psum, 1)

            run(pe, SLOTS, RING, 1, [(1, up_first), (2, hidden_T), (1, up_second), (2, down), (0, tokens_T)])

        @block.vector
        def _(dve):
            v = nc.vector
            count = [0]

            def link(ins):
                count[0] += 1
                ins.then_inc(chain, 1)
                dve.wait_ge(chain, count[0])

            v.memset(eps[:, :], EPS).then_inc(eps_ready, 1)
            link(v.memset(acc[:, :], 0.0))
            link(v.memset(z_out[:, :, C + 1:ZR], 1.0))
            dve.wait_ge(pool_consts, 7)
            v.tensor_copy(iota_row[:, :], io_i)
            v.tensor_copy(thr[:, :], io_t)
            v.tensor_copy(step_no, io_s)
            link(v.tensor_copy(node_id[:, :], io_n))
            link(v.tensor_scalar(valid[:, :], node_id[:, :], float(N), None, ALU.is_lt))
            dve.wait_ge(weights_in, 96)
            v.tensor_copy(attn_e[:, :], attn_col[:, :].to_broadcast([EF, P])).then_inc(attn_ready, 1)
            dve.wait_ge(att_psum, 1)
            for m in range(KC):
                last = v.tensor_copy(wfx[:, m, C:ZR], ps[7][:, 2 * m:2 * m + 2])
            last.then_inc(wfx_ready, 1)

            def norm(t, k, r):
                dve.wait_ge(x_loaded[k], 16 * (r + 1))
                v.bn_stats(st6[:, k, :], x_in[:, k, :]).then_inc(bn_done, 1)
                dve.wait_ge(bn_done, t + 1)
                held(dve)
                v.bn_aggr(mv2[:, k, :], st6[:, k, :]).then_inc(stats_ready, 1)

            def normed(t, k, r):
                dve.wait_ge(std_ready, t + 1)
                v.reciprocal(norm2[:, k, 1:2], norm2[:, k, 0:1]).then_inc(rstd_ready, 1)
                dve.wait_ge(rstd_ready, t + 1)
                held(dve)
                v.tensor_copy(rstd[:, bass.ds(t, 1)], norm2[:, k, 1:2])
                v.scalar_tensor_tensor(nmr[:, bass.ds(t, 1)], mv2[:, k, 0:1], -1.0, norm2[:, k, 1:2], ALU.mult,
                                       ALU.mult)
                if at_least(t, NODE_RING):
                    dve.wait_ge(hnT_psum, t - NODE_RING + 1)
                v.tensor_scalar(hn[:, k, :], x_in[:, k, :], mv2[:, k, 0:1], norm2[:, k, 1:2],
                                ALU.subtract, ALU.mult).then_inc(hn_ready, 1)

            def z_copy(t, k, r):
                bank = ps[2 + k % 2]
                dve.wait_ge(z_psum, t + 1)
                if at_least(t, NODE_RING):
                    dve.wait_ge(z_stored[k], 16 * r)
                v.tensor_copy(z_out[:, k, 0:C + 1], bank[:, 0:C + 1])
                v.tensor_copy(scal[:, cols(t, 3, 1)], bank[:, C + 1:ZR])
                v.tensor_scalar(scal[:, bass.ds(t * 3 + 1, 1)], bank[:, C + 1:ZR], SLOPE, None, ALU.mult)\
                    .then_inc(z_ready, 1)

            run(dve, TILES, NODE_RING, 2, [(0, norm), (1, normed), (3, z_copy)])
            link(v.memset(scal[:, :].rearrange("p (t c) -> p t c", c=3)[:, :, 2], NO_MAX))
            dve.wait_ge(dst_flat_in, 48)
            link(v.tensor_tensor(falls, dst_here, dst_next, ALU.is_gt))
            link(v.tensor_reduce(fell, falls, AX.X, ALU.max))
            for c, n in enumerate((P, GROUPS - P)):
                link(v.tensor_copy(last_f[0:n, c:c + 1], last_dst[0:n, c:c + 1]))
                link(v.tensor_scalar(ge_thr[0:n, 0:TILES - 1], thr[0:n, 0:TILES - 1], last_f[0:n, c:c + 1], None,
                                     ALU.is_le))
                link(v.tensor_reduce(start[0:n, c:c + 1], ge_thr[0:n, 0:TILES - 1], AX.X, ALU.add))
                link(v.tensor_scalar(start[0:n, c:c + 1], start[0:n, c:c + 1], node_id[0:n, c:c + 1], 1.0,
                                     ALU.add, ALU.add))
                link(v.tensor_scalar(begun[0:n, c, :], step_no[0:n, :], start[0:n, c:c + 1], None, ALU.is_ge))
            v.memset(tick[:, :], 0.0).then_inc(begun_ready, 1)
            dve.wait_ge(path_psum, 1)
            v.tensor_scalar(flag[0:1, :], ps[6][0:1, 0:1], 0.0, None, ALU.is_gt)
            v.tensor_copy(path_i[0:1, :], ps[5][0:1, 0:PATH])
            link(v.tensor_tensor(path_j[0:1, :], step_no[0:1, :], ps[5][0:1, 0:PATH], ALU.subtract))
            v.memset(tick[:, :], 0.0).then_inc(path_ready, 1)

            def steps(way):
                def scale_of(s, k, r):
                    b = k % 2
                    j = way.tile(dve, s)
                    dve.wait_ge(edge_loaded[k], 32 * (r + 1))
                    v.tensor_scalar(mask, dst_in[:, k, :], node_id[:, bass.ds(j, 1)], MASKED,
                                    ALU.not_equal, ALU.mult).then_inc(masked, 1)
                    dve.wait_ge(masked, s + 1)
                    dve.wait_ge(scores_psum, s + 1)
                    if at_least(s, 2):
                        dve.wait_ge(exps_done, 3 * (s - 1))
                    held(dve)
                    v.tensor_tensor_reduce(out=score[:, b, :], in0=ps[b][:, 0:G], in1=mask, scale=1.0,
                                           scalar=2 * MASKED, op0=ALU.add, op1=ALU.max,
                                           accum_out=small[:, 0:1]).then_inc(max_done, 1)
                    dve.wait_ge(max_done, s + 1)
                    v.tensor_scalar(small[:, 1:2], small[:, 0:1], scal[:, bass.ds(j * 3, 1)], None, ALU.add)\
                        .then_inc(plus_s2, 1)
                    dve.wait_ge(plus_s2, s + 1)
                    v.scalar_tensor_tensor(small[:, 2:3], small[:, 1:2], SLOPE, small[:, 1:2], ALU.mult, ALU.max)\
                        .then_inc(leaky_done, 1)
                    dve.wait_ge(leaky_done, s + 1)
                    if at_least(s, 1):
                        dve.wait_ge(run_done, s)
                    v.tensor_tensor(small[:, 3:4], small[:, 2:3], scal[:, bass.ds(j * 3 + 2, 1)], ALU.max)\
                        .then_inc(newmax_done, 1)
                    dve.wait_ge(newmax_done, s + 1)
                    v.tensor_scalar(bias[:, b, :], scal[:, bass.ds(j * 3, 3)], small[:, 3:4], None,
                                    ALU.subtract).then_inc(bias_ready, 1)
                    dve.wait_ge(bias_ready, s + 1)
                    held(dve)
                    v.tensor_copy(scal[:, bass.ds(j * 3 + 2, 1)], small[:, 3:4]).then_inc(run_done, 1)

                def probs_of(s, k, r):
                    b = k % 2
                    dve.wait_ge(exps_done, 3 * (s + 1))
                    if at_least(s, 2):
                        dve.wait_ge(probT_psum, s - 1)
                    v.tensor_tensor(prob[:, b, :], e_hi[:, b, :], e_lo[:, b, :], ALU.max)\
                        .then_inc(prob_ready, 1)

                def add_sum(s, k, r):
                    j = way.tile(dve, s)
                    dve.wait_ge(sum_psum, s + 1)
                    if at_least(s, 1):
                        dve.wait_ge(acc_done, s)
                    at = acc[:, cols(j, ZR)]
                    v.scalar_tensor_tensor(at, at, corr[:, k:k + 1], ps[4 + k % 2][:, 0:ZR], ALU.mult, ALU.add)\
                        .then_inc(acc_done, 1)
                run(dve, way.total, RING, 1, [(0, scale_of), (1, probs_of), (2, add_sum)])
                dve.wait_ge(acc_done, way.total)
            branch(dve, steps)

            den = acc[:, :].rearrange("p (t c) -> p t c", c=ZR)[:, :, C + 1]
            v.tensor_scalar(has_edge[:, :], den, 0.0, None, ALU.is_gt)
            v.tensor_scalar(no_edge[:, :], den, 0.0, None, ALU.is_le)
            link(v.tensor_scalar(inv_den[:, :], den, 1e-30, None, ALU.max))
            link(v.reciprocal(inv_den[:, :], inv_den[:, :]))
            v.memset(tick[:, :], 0.0).then_inc(den_ready, 1)

            def new_x(t, k, r):
                a = acc[:, cols(t, ZR, C)]
                dve.wait_ge(hs_psum, t + 1)
                v.scalar_tensor_tensor(a, a, inv_den[:, bass.ds(t, 1)], ps[2 + k % 2][:, 0:C], ALU.mult, ALU.add)\
                    .then_inc(with_hs, 1)
                dve.wait_ge(with_hs, t + 1)
                dve.wait_ge(idle_ready, t + 1)
                v.scalar_tensor_tensor(a, a, has_edge[:, bass.ds(t, 1)], idle[:, k, :], ALU.mult, ALU.add)\
                    .then_inc(or_idle, 1)
                dve.wait_ge(or_idle, t + 1)
                dve.wait_ge(xhn_ready, t + 1)
                if at_least(t, NODE_RING):
                    dve.wait_ge(x2_stored[k], 16 * r)
                    dve.wait_ge(hn2_ready, t - NODE_RING + 1)
                v.scalar_tensor_tensor(x2[:, k, :], a, 0.0, x_hn[:, k, :], ALU.max, ALU.add).then_inc(x2_ready, 1)
                dve.wait_ge(x2_ready, t + 1)
                v.bn_stats(st6[:, k, :], x2[:, k, :]).then_inc(bn2_done, 1)
                dve.wait_ge(bn2_done, t + 1)
                held(dve)
                v.bn_aggr(mv2[:, k, :], st6[:, k, :]).then_inc(stats2_ready, 1)

            def scale2(t, k, r):
                dve.wait_ge(std2_ready, t + 1)
                v.reciprocal(norm2[:, k, 1:2], norm2[:, k, 0:1]).then_inc(rstd2_ready, 1)
                dve.wait_ge(rstd2_ready, t + 1)
                v.scalar_tensor_tensor(norm2[:, k, 2:3], mv2[:, k, 0:1], -1.0, norm2[:, k, 1:2], ALU.mult,
                                       ALU.mult).then_inc(norm2_ready, 1)

            def logit_copy(t, k, r):
                dve.wait_ge(logit_psum, t + 1)
                v.tensor_copy(logits[:, cols(t, E)], ps[6 + k % 2][:, 0:E]).then_inc(logit_ready, 1)

            run(dve, TILES, NODE_RING, 2, [(1, new_x), (2, scale2), (4, logit_copy)])
            dve.wait_ge(logit_ready, TILES)

            lg = logits[:, :].rearrange("p (t e) -> p t e", e=E)

            def over_e(a):
                return a.unsqueeze(2).to_broadcast([P, TILES, E])

            def flat(a):
                return a.rearrange("p a b -> p (a b)")

            dve.wait_ge(late_ramps, 3)
            link(v.tensor_copy(exp_neg, io_e))
            link(v.tensor_reduce(t25[:, 0, :], lg, AX.X, ALU.max))
            link(v.tensor_tensor(probs, lg, over_e(t25[:, 0, :]), ALU.subtract))
            v.memset(tick[:, :], 0.0).then_inc(shifted, 1)
            dve.wait_ge(exp_ready, 1)
            link(v.tensor_reduce(t25[:, 1, :], ex, AX.X, ALU.add))
            link(v.reciprocal(t25[:, 1, :], t25[:, 1, :]))
            link(v.tensor_tensor(probs, ex, over_e(t25[:, 1, :]), ALU.mult))
            en = exp_neg.unsqueeze(1).to_broadcast([P, TILES, E])
            for c, (of, top) in enumerate(((probs, top0), (rest, top1))):
                best = t25[:, 2 + c, :]
                link(v.tensor_reduce(best, of, AX.X, ALU.max))
                link(v.tensor_tensor(eq, of, over_e(best), ALU.is_ge))
                link(v.tensor_tensor(cand, eq, en, ALU.mult))
                link(v.tensor_reduce(t25[:, 4, :], cand, AX.X, ALU.min))
                link(v.tensor_tensor(top, en, over_e(t25[:, 4, :]), ALU.is_equal))
                if c == 0:
                    link(v.scalar_tensor_tensor(flat(rest), flat(top0), -2.0, flat(probs), ALU.mult, ALU.add))
            link(v.tensor_tensor(t25[:, 5, :], t25[:, 2, :], t25[:, 3, :], ALU.add))
            link(v.tensor_scalar(t25[:, 5, :], t25[:, 5, :], 1e-9, None, ALU.add))
            link(v.reciprocal(t25[:, 5, :], t25[:, 5, :]))
            link(v.tensor_tensor(both, top0, top1, ALU.add))
            link(v.tensor_tensor(gates, probs, both, ALU.mult))
            link(v.tensor_tensor(gates, gates, over_e(t25[:, 5, :]), ALU.mult))
            v.memset(tick[:, :], 0.0).then_inc(gates_ready, 1)
            for top in (top0, top1):
                link(v.tensor_tensor(top, top, over_e(valid[:, :]), ALU.mult))
            link(v.tensor_tensor(both, both, over_e(valid[:, :]), ALU.mult))
            v.memset(tick[:, :], 0.0).then_inc(choice_ready, 1)
            dve.wait_ge(rank_psum, 1)
            link(v.tensor_tensor_scan(flat(cum), ones[:, 0:RE], ps[1][:, 0:RE], 0.0, ALU.mult, ALU.add))
            link(v.tensor_tensor(flat(cum_ex), flat(cum), ps[1][:, 0:RE], ALU.subtract))
            link(v.tensor_tensor(e8[:, 0, :], cum[:, :, TILES - 1], cum_ex[:, :, 0], ALU.subtract))
            link(v.tensor_scalar(t25[:, 0, :], thr[:, :], -float(P), None, ALU.add))
            link(v.tensor_tensor(tmp_ej, e8[:, 0, :].unsqueeze(2).to_broadcast([P, E, TILES]),
                                 t25[:, 0, :].unsqueeze(1).to_broadcast([P, E, TILES]), ALU.is_gt))
            link(v.tensor_reduce(e8[:, 1, :], tmp_ej, AX.X, ALU.add))
            link(v.tensor_tensor_scan(e8[:, 2, :], ones[:, 0:E], e8[:, 1, :], 0.0, ALU.mult, ALU.add))
            link(v.tensor_tensor(e8[:, 3, :], e8[:, 2, :], e8[:, 1, :], ALU.subtract))
            link(v.scalar_tensor_tensor(e8[:, 4, :], e8[:, 3, :], float(P), cum_ex[:, :, 0], ALU.mult,
                                        ALU.subtract))
            link(v.tensor_tensor(flat(slot), flat(cum_ex), ps[0][:, 0:RE], ALU.add))
            link(v.tensor_tensor(slot, slot, e8[:, 4, :].unsqueeze(2).to_broadcast([P, E, TILES]), ALU.add))
            for c, top in enumerate((top0, top1)):
                link(v.tensor_tensor(cand, top, slot.rearrange("p e t -> p t e"), ALU.mult))
                link(v.tensor_reduce(slots_f[:, c * TILES:(c + 1) * TILES], cand, AX.X, ALU.add))
            link(v.tensor_copy(slots_i, slots_f))
            v.tensor_scalar(st_i, slots_i, 7, None, ALU.logical_shift_right)
            link(v.tensor_scalar(sr_i, slots_i, P - 1, None, ALU.bitwise_and))
            v.tensor_copy(st_f, st_i)
            link(v.tensor_copy(sr_f, sr_i))
            link(v.tensor_scalar(sr_f, sr_f, 1.0, None, ALU.add))
            for c in range(2):
                a = sr_f[:, c * TILES:(c + 1) * TILES]
                link(v.tensor_tensor(a, a, valid[:, :], ALU.mult))
                v.tensor_copy(tile_b[:, c * TILES:(c + 1) * TILES], iota_row[:, 0:TILES])
            link(v.tensor_scalar(sr_f, sr_f, -1.0, None, ALU.add))
            v.tensor_copy(sr_b, sr_f)
            v.tensor_copy(st_b, st_f)
            v.tensor_copy(iota_b, iota_row[:, :])
            link(v.tensor_copy(slot_no, io_slot))
            v.tensor_copy(slot_b, slot_no)
            link(v.tensor_copy(p_plus1, io_p))
            link(v.tensor_scalar(dump_p, p_plus1, float(DUMP), None, ALU.add))
            v.tensor_tensor(ohr, iota_b.unsqueeze(1).to_broadcast([P, S2, P]),
                            sr_b.unsqueeze(2).to_broadcast([P, S2, P]), ALU.is_equal)
            link(v.tensor_tensor(oht, slot_b.unsqueeze(1).to_broadcast([P, S2, SLOTS]),
                                 st_b.unsqueeze(2).to_broadcast([P, S2, SLOTS]), ALU.is_equal))
            v.tensor_tensor(moving[:, :, 0:SLOTS], oht, tile_b.unsqueeze(2).to_broadcast([P, S2, SLOTS]),
                            ALU.mult)
            link(v.tensor_scalar(moving[:, :, SLOTS:2 * SLOTS], oht, p_plus1, None, ALU.mult))
            v.memset(tick[:, :], 0.0).then_inc(onehot_ready, 1)
            link(v.tensor_tensor(exp_cmp, e8[:, 3, 1:E].unsqueeze(1).to_broadcast([P, SLOTS, E - 1]),
                                 slot_no.unsqueeze(2).to_broadcast([P, SLOTS, E - 1]), ALU.is_le))
            link(v.tensor_reduce(exp_f, exp_cmp, AX.X, ALU.add))
            link(v.tensor_copy(expert_of[0:1, :], exp_f[0:1, :]))
            dve.wait_ge(token_psum, 1)
            link(v.tensor_copy(tok, ps[2][:, SLOTS:2 * SLOTS]))
            link(v.scalar_tensor_tensor(tok, ps[2][:, 0:SLOTS], float(P), tok, ALU.mult, ALU.add))
            link(v.tensor_scalar(tok, tok, -1.0, None, ALU.add))
            link(v.tensor_scalar(unused, tok, 0.0, None, ALU.is_lt))
            link(v.scalar_tensor_tensor(row_f, unused, dump_p, tok, ALU.mult, ALU.add))
            link(v.tensor_scalar(tok, tok, 0.0, None, ALU.max))
            pair = slot_rows[:, :].rearrange("p (t c) -> p t c", c=2)
            v.tensor_copy(pair[:, :, 0], tok)
            link(v.tensor_copy(pair[:, :, 1], row_f))
            dve.wait_ge(gates_stored, 16)
            v.memset(tick[:, :], 0.0).then_inc(slots_ready, 1)

            def hid_first(t, k, r):
                dve.wait_ge(silu_a, t + 1)
                v.tensor_tensor(hid[:, k % 2, 0:HA], s_act[:, 0:HA], ps[1][:, 0:HA], ALU.mult)\
                    .then_inc(hid_a_ready, 1)

            def hid_second(t, k, r):
                dve.wait_ge(silu_b, t + 1)
                v.tensor_tensor(hid[:, k % 2, HA:H], s_act[:, HA:H], ps[3][:, 0:HB], ALU.mult)\
                    .then_inc(hid_b_ready, 1)

            def hidT_rest(t, k, r):
                dve.wait_ge(hidT_psum, t + 1)
                if at_least(t, 1):
                    dve.wait_ge(y_psum, t)
                n = HC[-1][1]
                v.tensor_copy(hidT[:, 4 * P:5 * P], ps[7][:, 0:P])
                v.tensor_copy(hidT[0:n, 5 * P:6 * P], ps[7][0:n, P:2 * P]).then_inc(hidT_by_dve, 1)

            def gated(t, k, r):
                e = dve.value_load(expert_of[0:1, bass.ds(t, 1)], min_val=0, max_val=E - 1)
                dve.wait_ge(y_psum, t + 1)
                if at_least(t, 2):
                    dve.wait_ge(y_added, 16 * (t - 1))
                v.tensor_scalar(y_out[:, k % 2, :], ps[5][:, 0:C], xg_flat[:, bass.ds(e + (k * TR + C), 1)],
                                None, ALU.mult).then_inc(y_ready, 1)

            run(dve, SLOTS, RING, 1, [(1, hid_first), (2, hidT_rest), (1, hid_second), (2, gated)])


def kernel(x, src, dst, edge_attr_64, node_vec1, L0_gnn_W_self, L0_gnn_W_func, L0_gnn_W_att,
           L0_ffn_router_w, L0_ffn_w1, L0_ffn_w2, L0_ffn_w3):
    import numpy as np
    import concourse.bacc as bacc
    from concourse.bass_utils import run_bass_kernel_spmd

    pad = lambda a, n, value=0: np.concatenate([a, np.full((n - a.shape[0],) + a.shape[1:], value, a.dtype)])
    f = lambda a: np.ascontiguousarray(a)
    x, src, dst = np.asarray(x), np.asarray(src), np.asarray(dst)
    ea, att = np.asarray(edge_attr_64), np.asarray(L0_gnn_W_att)
    wfunc, wself = np.asarray(L0_gnn_W_func), np.asarray(L0_gnn_W_self)
    w1, w2, w3 = np.asarray(L0_ffn_w1), np.asarray(L0_ffn_w2), np.asarray(L0_ffn_w3)
    n = GROUPS * G
    up = [w.transpose(0, 2, 1).reshape(E, KC, P, H).transpose(0, 2, 1, 3).reshape(E, P, KC * H) for w in (w1, w3)]
    w2p = np.concatenate([w2.transpose(0, 2, 1), np.zeros((E, NH * P - H, C), w2.dtype)], axis=1)
    down = w2p.reshape(E, NH, P, C).transpose(0, 2, 1, 3).reshape(E, P, NH * C)
    dst_rows = pad(dst, n + G, PAD_DST).reshape(GROUPS + 1, G)
    arrays = {
        "in_x": f(pad(x, NP)),
        "in_src": f(pad(src, n).reshape(GROUPS, KG, P).transpose(0, 2, 1)),
        "in_dst": f(dst_rows),
        "in_last": f(pad(dst_rows[0:GROUPS, G - 1], 2 * P, PAD_DST).reshape(2, P).T),
        "in_wt": f(pad(ea, n).reshape(GROUPS, G, EF).transpose(0, 2, 1)),
        "in_wfunc": f(wfunc),
        "in_wfunct": f(wfunc.T),
        "in_wselft": f(wself.T),
        "in_attn": f(att[0, 0:2 * C].reshape(2, C).T),
        "in_atte": f(att[0, 2 * C:].reshape(EF, 1)),
        "in_router": f(np.asarray(L0_ffn_router_w).T),
        "in_experts": f(np.concatenate([up[0], up[1], down], axis=2)),
    }
    nc = bacc.Bacc("TRN2", target_bir_lowering=False, num_devices=1)
    args = [nc.dram_tensor(k, a.shape, mybir.dt.from_np(a.dtype), kind="ExternalInput").ap()
            for k, a in arrays.items()]
    out = nc.dram_tensor("out_rows", (OUT_ROWS, C), mybir.dt.float32, kind="ExternalOutput").ap()
    build(nc, *args, out)
    r = run_bass_kernel_spmd(nc, [arrays], core_ids=[0])
    return r.results[0]["out_rows"][0:N]
```

```python
from contextlib import ExitStack

import concourse.bass as bass
from concourse import mybir

P = 128
N, C, EDGES, EF = 3125, 256, 53125, 64
E, H = 8, 682
TILES = -(-N // P)
NP = TILES * P
G = 512
KG = G // P
LOADS = 8
GROUPS = -(-EDGES // (LOADS * G)) * LOADS
RING = 4
PATH = GROUPS + TILES - 1
PAIRS = GROUPS * TILES
PAD_DST = TILES * P
ZR = C + 2
TR = C + E
KC = C // P
HC = [(a, min(P, H - a)) for a in range(0, H, P)]
NH = len(HC)
HA = 3 * P
HB = H - HA
W1_AT, W3_AT, W2_AT = 0, KC * H, 2 * KC * H
WE = W2_AT + NH * C
SLOTS = (2 * N + E * (P - 1)) // P
DUMP = NP
OUT_ROWS = NP + P
NODE_RING = 5
SLOPE = 0.01
QE = GROUPS * G // P
PAIRS_OF_GROUPS = GROUPS // 2
AT_ONCE = 2
EDGE_LOADS = PAIRS_OF_GROUPS // AT_ONCE
S2 = 2 * TILES
RE = TILES * E
LATE = max(S2 * SLOTS + 3 * H + NH * P + 2 * C, 12 * G)
EPS = 1e-5
MASKED = -1e30
NO_MAX = -1e26
assert GROUPS <= P and PATH % RING == 0 and PAIRS % LOADS == 0 and EDGE_LOADS == TILES + 1
assert TILES % NODE_RING == 0 and SLOTS % RING == 0


def build(nc, x, src, dst, dst_last, wt, w_func, w_func_t, w_self_t, att_nodes, att_edge, router, experts,
          out):
    fp32, i32, bf16 = mybir.dt.float32, mybir.dt.int32, mybir.dt.bfloat16
    ALU, ACT, AX = mybir.AluOpType, mybir.ActivationFunctionType, mybir.AxisListType
    ztab = nc.dram_tensor("ztab", [NP, ZR], fp32, kind="Internal").ap()
    ttab = nc.dram_tensor("ttab", [NP, TR], fp32, kind="Internal").ap()

    with ExitStack() as ctx:
        def sb(name, shape, dt=fp32):
            return ctx.enter_context(nc.sbuf_tensor(name, shape, dt))

        def sem(name):
            return ctx.enter_context(nc.semaphore(name))

        W = sb("W", [P, E, WE])
        acc = sb("acc", [P, TILES * ZR])
        late = sb("late", [P, LATE])
        ident = sb("ident", [P, P])
        iota_row = sb("iota_row", [P, P])
        before = sb("before", [P, P])
        ones = sb("ones", [P, 2 * P])
        zero_rows = sb("zero_rows", [P, C])
        wself_sb = sb("wself_sb", [P, KC, C])
        router_sb = sb("router_sb", [P, KC, E])
        att_e = sb("att_e", [P, 2])
        att_n = sb("att_n", [P, KC, 2])
        node_id = sb("node_id", [P, TILES])
        valid = sb("valid", [P, TILES])
        thr = sb("thr", [P, TILES])
        scal = sb("scal", [P, TILES * 3])
        rstd = sb("rstd", [P, TILES])
        nmr = sb("nmr", [P, TILES])
        eps = sb("eps", [P, 1])
        inv_den = sb("inv_den", [P, TILES])
        has_edge = sb("has_edge", [P, TILES])
        no_edge = sb("no_edge", [P, TILES])
        logits = sb("logits", [P, TILES * E])
        path_i = sb("path_i", [1, PATH], i32)
        path_j = sb("path_j", [1, PATH], i32)
        path_next = sb("path_next", [1, P], i32)
        flag = sb("flag", [1, 1], i32)
        expert_of = sb("expert_of", [1, SLOTS], i32)
        slot_rows = sb("slot_rows", [P, SLOTS * 2], i32)
        row_ix = sb("row_ix", [P, RING, 2], i32)
        xg = sb("xg", [P, RING, TR])
        xT = sb("xT", [P, 2, KC, P])
        tick = sb("tick", [P, 1])

        def carve(region, at, shape, dt=fp32):
            n = 1
            for d in shape:
                n *= d
            words = n if dt != bf16 else n // 2
            v = region[:, at:at + words]
            if dt != fp32:
                v = v.bitcast(dt)
            if len(shape) == 2:
                v = v.rearrange("p (a b) -> p a b", b=shape[1])
            return v, at + words

        z, o = W[:, 3, :], 0
        dst_here, o = carve(z, o, [QE], i32)
        dst_next, o = carve(z, o, [QE], i32)
        falls, o = carve(z, o, [QE])
        last_dst, o = carve(z, o, [1], i32)
        last_f, o = carve(z, o, [1])
        start, o = carve(z, o, [1])
        ge_thr, o = carve(z, o, [TILES])
        step_no, o = carve(z, o, [PATH])
        begun, o = carve(z, o, [PATH])
        fell, o = carve(z, o, [1])
        io_i, o = carve(z, o, [P], i32)
        io_s, o = carve(z, o, [PATH], i32)
        io_t, o = carve(z, o, [TILES], i32)
        io_n, o = carve(z, o, [TILES], i32)
        assert o <= WE
        edge_score, o = carve(z, o, [GROUPS * KG])
        q, o = carve(z, o, [LOADS * KG])
        q_step, o = carve(z, o, [RING, KG])
        bias, o = carve(z, o, [2, 3])
        corr, o = carve(z, o, [RING])
        small, o = carve(z, o, [RING, 4])
        src_in, o = carve(z, o, [LOADS, KG], i32)
        assert o <= WE
        z, o = W[:, 4, :], 0
        wfx, o = carve(z, o, [KC, ZR])
        wf_nat, o = carve(z, o, [KC, C])
        hnT, o = carve(z, o, [NODE_RING, C])
        hn1, o = carve(z, o, [NODE_RING, C])
        st6, o = carve(z, o, [NODE_RING, 6])
        mv2, o = carve(z, o, [NODE_RING, 2])
        norm2, o = carve(z, o, [NODE_RING, 3])
        assert o <= WE
        z, o = W[:, 5, :], 0
        x_in, o = carve(z, o, [NODE_RING, C])
        hn, o = carve(z, o, [NODE_RING, C])
        z_out, _ = carve(z, o, [NODE_RING, ZR])
        x2, _ = carve(z, o, [NODE_RING, C])
        assert o + NODE_RING * ZR <= WE
        z = W[:, 5:7, :].rearrange("p e w -> p (e w)")
        zg, o = carve(z, 0, [LOADS * KG, ZR])
        assert o <= 2 * WE
        zg_flat = z
        z = W[:, 6, :]
        o = 0
        x_hn, o = carve(z, o, [NODE_RING, C])
        idle, o = carve(z, o, [NODE_RING, C])
        hn2T, o = carve(z, o, [NODE_RING, C])
        assert o <= WE
        dst_in, o = carve(W[:, 7, :], 0, [LOADS * G], i32)
        assert o <= WE
        vec_in, o = carve(late, 0, [NODE_RING, AT_ONCE * G])
        assert o <= LATE
        mask, o = carve(late, 0, [2, G])
        score, o = carve(late, o, [2, G])
        e_hi, o = carve(late, o, [2, G])
        e_lo, o = carve(late, o, [2, G])
        prob, o = carve(late, o, [2, G])
        probT, o = carve(late, o, [2, G])
        assert o <= LATE
        ohr, o = carve(acc, 0, [S2, P], bf16)
        oht, o = carve(acc, o, [S2, SLOTS], bf16)
        iota_b, o = carve(acc, o, [P], bf16)
        slots_f, o = carve(acc, o, [S2])
        slots_i, o = carve(acc, o, [S2], i32)
        st_i, o = carve(acc, o, [S2], i32)
        sr_i, o = carve(acc, o, [S2], i32)
        st_f, o = carve(acc, o, [S2])
        sr_f, o = carve(acc, o, [S2])
        st_b, o = carve(acc, o, [S2], bf16)
        sr_b, o = carve(acc, o, [S2], bf16)
        tile_b, o = carve(acc, o, [S2], bf16)
        io_slot, o = carve(acc, o, [SLOTS], i32)
        slot_no, o = carve(acc, o, [SLOTS])
        slot_b, o = carve(acc, o, [SLOTS], bf16)
        tok, o = carve(acc, o, [SLOTS])
        unused, o = carve(acc, o, [SLOTS])
        row_f, o = carve(acc, o, [SLOTS])
        exp_cmp, o = carve(acc, o, [SLOTS, E - 1])
        exp_f, o = carve(acc, o, [SLOTS])
        p_plus1, o = carve(acc, o, [1])
        dump_p, o = carve(acc, o, [1])
        io_p, o = carve(acc, o, [1], i32)
        exp_neg, o = carve(acc, o, [E])
        io_e, o = carve(acc, o, [E], i32)
        assert o <= TILES * ZR
        moving, behind = carve(late, 0, [S2, 2 * SLOTS], bf16)
        o = behind
        s_act, o = carve(late, o, [H])
        hid, o = carve(late, o, [2, H])
        hidT, o = carve(late, o, [NH * P])
        y_out, o = carve(late, o, [2, C])
        assert o <= LATE
        o = behind
        ex, o = carve(late, o, [TILES, E])
        probs, o = carve(late, o, [TILES, E])
        rest, o = carve(late, o, [TILES, E])
        eq, o = carve(late, o, [TILES, E])
        cand, o = carve(late, o, [TILES, E])
        top0, o = carve(late, o, [TILES, E])
        top1, o = carve(late, o, [TILES, E])
        both, o = carve(late, o, [TILES, E])
        gates, o = carve(late, o, [TILES, E])
        cum, o = carve(late, o, [E, TILES])
        cum_ex, o = carve(late, o, [E, TILES])
        slot, o = carve(late, o, [E, TILES])
        tmp_ej, o = carve(late, o, [E, TILES])
        t25, o = carve(late, o, [6, TILES])
        e8, o = carve(late, o, [6, E])
        assert o <= LATE
        Wf = W[:, :, :].rearrange("p e w -> p (e w)")
        xg_flat = xg[:, :, :].rearrange("p a b -> p (a b)")

        ps = [ctx.enter_context(nc.psum_tensor(f"bank{b}", [P, 512], fp32)) for b in range(8)]

        pool_consts = sem("pool_consts")
        blank = sem("blank")
        late_ramps = sem("late_ramps")
        eps_ready = sem("eps_ready")
        att_blank = sem("att_blank")
        vec_loaded = [sem(f"vec_loaded{k}") for k in range(NODE_RING)]
        vec_used = sem("vec_used")
        edge_score_ready = sem("edge_score_ready")
        weights_in = sem("weights_in")
        x_loaded = [sem(f"x_loaded{k}") for k in range(NODE_RING)]
        z_stored = [sem(f"z_stored{k}") for k in range(NODE_RING)]
        att_psum = sem("att_psum")
        wfx_ready = sem("wfx_ready")
        bn_done = sem("bn_done")
        stats_ready = sem("stats_ready")
        std_ready = sem("std_ready")
        rstd_ready = sem("rstd_ready")
        nmr_ready = sem("nmr_ready")
        hn_ready = sem("hn_ready")
        hnT_psum = sem("hnT_psum")
        hnT_ready = sem("hnT_ready")
        z_psum = sem("z_psum")
        z_ready = sem("z_ready")
        chain = sem("chain")
        dst_flat_in = sem("dst_flat_in")
        begun_ready = sem("begun_ready")
        path_psum = sem("path_psum")
        path_ready = sem("path_ready")
        src_loaded = [sem(f"src_loaded{k}") for k in range(LOADS)]
        dst_loaded = [sem(f"dst_loaded{k}") for k in range(LOADS)]
        z_gathered = [sem(f"z_gathered{k}") for k in range(LOADS)]
        dst_here_now = sem("dst_here_now")
        q_of_load = sem("q_of_load")
        q_ready = sem("q_ready")
        scores_psum = sem("scores_psum")
        masked = sem("masked")
        max_done = sem("max_done")
        plus_s2 = sem("plus_s2")
        leaky_done = sem("leaky_done")
        newmax_done = sem("newmax_done")
        bias_ready = sem("bias_ready")
        run_done = sem("run_done")
        exps_done = sem("exps_done")
        prob_ready = sem("prob_ready")
        probT_psum = sem("probT_psum")
        probT_ready = sem("probT_ready")
        sum_psum = sem("sum_psum")
        acc_done = sem("acc_done")
        steps_over = sem("steps_over")
        den_ready = sem("den_ready")
        x_again = [sem(f"x_again{k}") for k in range(NODE_RING)]
        hn1_ready = sem("hn1_ready")
        idle_ready = sem("idle_ready")
        xhn_ready = sem("xhn_ready")
        hn1T_psum = sem("hn1T_psum")
        hn1T_ready = sem("hn1T_ready")
        hs_psum = sem("hs_psum")
        with_hs = sem("with_hs")
        or_idle = sem("or_idle")
        x2_ready = sem("x2_ready")
        bn2_done = sem("bn2_done")
        stats2_ready = sem("stats2_ready")
        std2_ready = sem("std2_ready")
        rstd2_ready = sem("rstd2_ready")
        norm2_ready = sem("norm2_ready")
        hn2_ready = sem("hn2_ready")
        hn2T_psum = sem("hn2T_psum")
        hn2T_ready = sem("hn2T_ready")
        logit_psum = sem("logit_psum")
        logit_ready = sem("logit_ready")
        x2_stored = [sem(f"x2_stored{k}") for k in range(NODE_RING)]
        hn2_stored = [sem(f"hn2_stored{k}") for k in range(NODE_RING)]
        dump_stored = sem("dump_stored")
        shifted = sem("shifted")
        exp_ready = sem("exp_ready")
        gates_ready = sem("gates_ready")
        gates_stored = sem("gates_stored")
        choice_ready = sem("choice_ready")
        rank_psum = sem("rank_psum")
        onehot_ready = sem("onehot_ready")
        token_psum = sem("token_psum")
        slots_ready = sem("slots_ready")
        experts_in = [sem(f"experts_in{e}") for e in range(E)]
        ix_ready = sem("ix_ready")
        row_gathered = [sem(f"row_gathered{k}") for k in range(RING)]
        xT_psum = sem("xT_psum")
        xT_ready = sem("xT_ready")
        up_a_psum = sem("up_a_psum")
        up_b_psum = sem("up_b_psum")
        silu_a = sem("silu_a")
        silu_b = sem("silu_b")
        hid_a_ready = sem("hid_a_ready")
        hid_b_ready = sem("hid_b_ready")
        hidT_psum = sem("hidT_psum")
        hidT_by_act = sem("hidT_by_act")
        hidT_by_dve = sem("hidT_by_dve")
        y_psum = sem("y_psum")
        y_ready = sem("y_ready")
        y_added = sem("y_added")
        passed = {str(eng.engine): sem(f"passed{n}") for n, eng in enumerate((nc.vector, nc.gpsimd))}
        block = ctx.enter_context(nc.Block())

        def run(eng, total, ring, peel, stages):
            def turn(r, k):
                for lag, stage in stages:
                    q, kk = divmod(k - lag, ring)
                    t = r * ring + (k - lag)
                    if isinstance(t, int) and not 0 <= t < total:
                        continue
                    stage(t, kk, r + q)
            for r in range(peel):
                for k in range(ring):
                    turn(r, k)
            with eng.Fori(peel, total // ring) as r:
                for k in range(ring):
                    turn(r, k)
            for k in range(max(lag for lag, _ in stages)):
                turn(total // ring, k)

        def at_least(t, n):
            return not isinstance(t, int) or t >= n

        def bank_back(k):
            return 1 if k == 0 else 2

        def held(eng):
            eng.sem_inc(passed[str(eng.engine)], 1)

        def cols(t, n, width=None):
            return bass.ds(t * n, n if width is None else width)

        class Sorted:
            total = PATH
            loads = GROUPS

            def load_of(self, eng, s):
                return eng.value_load(path_i[0:1, bass.ds(s, 1)], min_val=0, max_val=GROUPS - 1)

            def group(self, n):
                return n

            def tile(self, eng, s):
                return eng.value_load(path_j[0:1, bass.ds(s, 1)], min_val=0, max_val=TILES - 1)

            def steps_until(self, eng, n):
                return eng.value_load(path_next[0:1, bass.ds(n, 1)], min_val=1, max_val=PATH)

        class Unsorted:
            total = PAIRS
            loads = PAIRS

            def load_of(self, eng, s):
                return s

            def group(self, n):
                return n % GROUPS

            def tile(self, eng, s):
                return s // GROUPS

            def steps_until(self, eng, n):
                return n + 1

        def once(eng, value):
            return value if isinstance(value, int) else eng.snap(value)

        def branch(eng, steps):
            eng.wait_ge(path_ready, 1)
            falls_at = eng.value_load(flag[0:1, 0:1], min_val=0, max_val=1)
            with eng.If(falls_at == 0):
                steps(Sorted())
            with eng.Else():
                steps(Unsorted())
            eng.sem_inc(steps_over, 1)
            eng.wait_ge(steps_over, 5)

        @block.sync
        def _(sp):
            flat = dst.rearrange("g e -> (g e)")
            sp.dma_start(dst_here, flat[0:P * QE].rearrange("(p q) -> p q", q=QE)).then_inc(dst_flat_in, 16)
            sp.dma_start(dst_next, flat[1:P * QE + 1].rearrange("(p q) -> p q", q=QE)).then_inc(dst_flat_in, 16)
            sp.dma_start(last_dst, dst_last).then_inc(dst_flat_in, 16)
            sp.dma_start(wf_nat, w_func.rearrange("(k p) c -> p k c", p=P)).then_inc(weights_in, 16)
            sp.dma_start(wfx[:, :, 0:C], w_func_t.rearrange("(k p) c -> p k c", p=P))\
                .then_inc(weights_in, 16)
            sp.dma_start(att_n[:, :, :], att_nodes.rearrange("(k p) c -> p k c", p=P))\
                .then_inc(weights_in, 16)
            for k in range(NODE_RING):
                sp.dma_start(x_in[:, k, :], x[cols(k, P), :]).then_inc(x_loaded[k], 16)
            sp.dma_start(wself_sb[:, :, :], w_self_t.rearrange("(k p) c -> p k c", p=P))\
                .then_inc(weights_in, 16)
            sp.dma_start(router_sb[:, :, :], router.rearrange("(k p) c -> p k c", p=P))\
                .then_inc(weights_in, 16)
            sp.wait_ge(att_blank, 1)
            for c in range(2):
                sp.dma_start(att_e[c * EF:(c + 1) * EF, c:c + 1], att_edge).then_inc(weights_in, 16)

            def vectors_load(t, k, r):
                if at_least(t, NODE_RING):
                    sp.wait_ge(vec_used, t - NODE_RING + 1)
                sp.dma_start(vec_in[:, k, :].rearrange("p (b e) -> p b e", e=G),
                             wt[bass.ds(t * AT_ONCE, AT_ONCE), :, :].rearrange("b p e -> p b e"))\
                    .then_inc(vec_loaded[k], 16)

            def x_load(t, k, r):
                if at_least(t, NODE_RING):
                    sp.wait_ge(hn_ready, t - NODE_RING + 1)
                    sp.dma_start(x_in[:, k, :], x[cols(t, P), :]).then_inc(x_loaded[k], 16)

            def z_store(t, k, r):
                sp.wait_ge(z_ready, t + 1)
                sp.dma_start(ztab[cols(t, P), :], z_out[:, k, :]).then_inc(z_stored[k], 16)

            run(sp, TILES, NODE_RING, 2, [(0, x_load), (0, vectors_load), (4, z_store)])
            vectors_load(TILES, 0, TILES // NODE_RING)
            for e in range(3):
                sp.dma_start(W[:, e, :], experts[e, :, :]).then_inc(experts_in[e], 16)
            sp.wait_ge(pool_consts, 8)
            sp.dma_start(out[DUMP:OUT_ROWS, :], zero_rows[:, :]).then_inc(dump_stored, 16)

            sp.wait_ge(edge_score_ready, 1)

            def steps(way):
                def load(n, k, r):
                    g = way.group(n)
                    if at_least(n, LOADS):
                        sp.wait_ge(z_gathered[k], 16 * KG * r)
                    sp.dma_start(src_in[:, k, :], src[bass.ds(g, 1), :, :].rearrange("g p k -> p (g k)"))\
                        .then_inc(src_loaded[k], 16)
                    if at_least(n, LOADS):
                        until = way.steps_until(sp, n - LOADS)
                        sp.wait_ge(masked, until)
                    sp.dma_start(dst_in[:, k * G:(k + 1) * G], dst[bass.ds(g, 1), :].to_broadcast([P, G]))\
                        .then_inc(dst_loaded[k], 16)

                def loaded(n, k, r):
                    sp.wait_ge(dst_loaded[k], 16 * (r + 1))
                    sp.sem_inc(dst_here_now, 1)
                run(sp, way.loads, LOADS, 2, [(0, load), (2, loaded)])
            branch(sp, steps)

            def x_load_again(t, k, r):
                if at_least(t, NODE_RING):
                    sp.wait_ge(xhn_ready, t - NODE_RING + 1)
                    sp.wait_ge(hn1_ready, t - NODE_RING + 1)
                sp.dma_start(x_in[:, k, :], x[cols(t, P), :]).then_inc(x_again[k], 16)

            def x2_store(t, k, r):
                sp.wait_ge(x2_ready, t + 1)
                sp.dma_start(out[cols(t, P), :], x2[:, k, :]).then_inc(x2_stored[k], 16)

            def hn2_store(t, k, r):
                sp.wait_ge(hn2_ready, t + 1)
                sp.dma_start(ttab[cols(t, P), 0:C], hn[:, k, :]).then_inc(hn2_stored[k], 16)

            run(sp, TILES, NODE_RING, 2, [(0, x_load_again), (3, x2_store), (4, hn2_store)])
            sp.wait_ge(logit_ready, TILES)
            for k in range(NODE_RING):
                sp.wait_ge(x2_stored[k], 16 * (TILES // NODE_RING))
                sp.wait_ge(hn2_stored[k], 16 * (TILES // NODE_RING))
            for e in range(3, E):
                sp.dma_start(W[:, e, :], experts[e, :, :]).then_inc(experts_in[e], 16)
            sp.wait_ge(gates_ready, 1)
            sp.dma_start(ttab[:, C:TR].rearrange("(t p) e -> p t e", p=P), gates).then_inc(gates_stored, 16)
            sp.wait_ge(gates_stored, 16)
            sp.wait_ge(dump_stored, 16)
            sp.wait_ge(y_added, 16 * SLOTS)

        @block.gpsimd
        def _(pool):
            nc.gpsimd.memset(att_e[:, :], 0.0).then_inc(att_blank, 1)
            nc.gpsimd.memset(ident[:, :], 0.0).then_inc(blank, 1)
            nc.gpsimd.memset(before[:, :], 1.0).then_inc(blank, 1)
            nc.gpsimd.memset(ones[:, :], 1.0).then_inc(pool_consts, 1)
            pool.wait_ge(blank, 2)
            nc.gpsimd.affine_select(out=ident[:, :], in_=ident[:, :], compare_op=ALU.not_equal, fill=1.0,
                                    base=0, pattern=[[-1, P]], channel_multiplier=1).then_inc(pool_consts, 1)
            nc.gpsimd.affine_select(out=before[:, :], in_=before[:, :], compare_op=ALU.is_gt, fill=0.0,
                                    base=0, pattern=[[1, P]], channel_multiplier=-1).then_inc(pool_consts, 1)
            nc.gpsimd.iota(io_i, pattern=[[1, P]], base=0, channel_multiplier=0).then_inc(pool_consts, 1)
            nc.gpsimd.iota(io_n, pattern=[[P, TILES]], base=0, channel_multiplier=1).then_inc(pool_consts, 1)
            nc.gpsimd.iota(io_t, pattern=[[P, TILES]], base=P, channel_multiplier=0).then_inc(pool_consts, 1)
            nc.gpsimd.iota(io_s, pattern=[[1, PATH]], base=0, channel_multiplier=0).then_inc(pool_consts, 1)
            nc.gpsimd.memset(zero_rows[:, :], 0.0).then_inc(pool_consts, 1)
            pool.wait_ge(edge_score_ready, 1)
            for k in range(NODE_RING):
                pool.wait_ge(z_stored[k], 16 * (TILES // NODE_RING))

            def steps(way):
                def gather(n, k, r):
                    if at_least(n, LOADS):
                        until = way.steps_until(pool, n - LOADS)
                        pool.wait_ge(sum_psum, until)
                    pool.wait_ge(src_loaded[k], 16 * (r + 1))
                    held(pool)
                    for c in range(KG):
                        nc.gpsimd.indirect_dma_start(
                            out=zg[:, k * KG + c, :], out_offset=None, in_=ztab,
                            in_offset=bass.IndirectOffsetOnAxis(ap=src_in[:, k, c:c + 1], axis=0))\
                            .then_inc(z_gathered[k], 16)

                def add_s1(n, k, r):
                    pool.wait_ge(z_gathered[k], 16 * KG * (r + 1))
                    nc.gpsimd.tensor_tensor(q[:, k * KG:(k + 1) * KG], edge_score[:, cols(way.group(n), KG)],
                                            zg[:, k * KG:(k + 1) * KG, C], ALU.add).then_inc(q_of_load, 1)
                run(pool, way.loads, LOADS, 2, [(0, gather), (2, add_s1)])
            branch(pool, steps)

            def x_plus_hn(t, k, r):
                pool.wait_ge(hn1_ready, t + 1)
                if at_least(t, NODE_RING):
                    pool.wait_ge(x2_ready, t - NODE_RING + 1)
                nc.gpsimd.tensor_tensor(x_hn[:, k, :], x_in[:, k, :], hn1[:, k, :], ALU.add)\
                    .then_inc(xhn_ready, 1)

            run(pool, TILES, NODE_RING, 1, [(0, x_plus_hn)])
            pool.wait_ge(x2_ready, TILES)
            nc.gpsimd.iota(io_slot, pattern=[[1, SLOTS]], base=0, channel_multiplier=0).then_inc(late_ramps, 1)
            nc.gpsimd.iota(io_p, pattern=[[0, 1]], base=1, channel_multiplier=1).then_inc(late_ramps, 1)
            nc.gpsimd.iota(io_e, pattern=[[1, E]], base=-E, channel_multiplier=0).then_inc(late_ramps, 1)

            pool.wait_ge(gates_stored, 16)
            pool.wait_ge(dump_stored, 16)
            for k in range(NODE_RING):
                pool.wait_ge(x2_stored[k], 16 * (TILES // NODE_RING))
                pool.wait_ge(hn2_stored[k], 16 * (TILES // NODE_RING))
            pool.wait_ge(slots_ready, 1)

            def add(t, k, r):
                pool.wait_ge(y_ready, t + 1)
                held(pool)
                nc.gpsimd.indirect_dma_start(
                    out=out, out_offset=bass.IndirectOffsetOnAxis(ap=row_ix[:, k, 1:2], axis=0),
                    in_=y_out[:, k % 2, :], in_offset=None, compute_op=ALU.add).then_inc(y_added, 16)
                pool.wait_ge(y_added, 16 * (t + 1))

            def gather_rows(t, k, r):
                nc.gpsimd.tensor_copy(row_ix[:, k, :], slot_rows[:, cols(t, 2)]).then_inc(ix_ready, 1)
                pool.wait_ge(ix_ready, t + 1)
                held(pool)
                nc.gpsimd.indirect_dma_start(
                    out=xg[:, k, :], out_offset=None, in_=ttab,
                    in_offset=bass.IndirectOffsetOnAxis(ap=row_ix[:, k, 0:1], axis=0))\
                    .then_inc(row_gathered[k], 16)

            run(pool, SLOTS, RING, 1, [(3, add), (0, gather_rows)])

        @block.scalar
        def _(act):
            act.wait_ge(eps_ready, 1)

            def std(t, k, r):
                act.wait_ge(stats_ready, t + 1)
                nc.scalar.activation(norm2[:, k, 0:1], mv2[:, k, 1:2], ACT.Sqrt, bias=eps[:, 0:1])\
                    .then_inc(std_ready, 1)

            def hn_first(t, k, r):
                act.wait_ge(nmr_ready, t + 1)
                if at_least(t, NODE_RING):
                    act.wait_ge(hnT_psum, t - NODE_RING + 1)
                nc.scalar.activation(hn[:, k, :], x_in[:, k, :], ACT.Identity, bias=nmr[:, bass.ds(t, 1)],
                                     scale=rstd[:, bass.ds(t, 1)]).then_inc(hn_ready, 1)

            def hnT_copy(t, k, r):
                act.wait_ge(hnT_psum, t + 1)
                if at_least(t, NODE_RING):
                    act.wait_ge(z_psum, t - NODE_RING + 1)
                nc.scalar.activation(hnT[:, k, :], ps[k % 2][:, 0:C], ACT.Copy).then_inc(hnT_ready, 1)

            run(act, TILES, NODE_RING, 2, [(0, std), (1, hn_first), (2, hnT_copy)])

            def steps(way):
                def q_copy(s, k, r):
                    n = once(act, way.load_of(act, s))
                    if at_least(s, RING):
                        act.wait_ge(scores_psum, s - RING + 1)
                    act.wait_ge(q_of_load, n + 1)
                    nc.scalar.activation(q_step[:, k, :], q[:, cols(n % LOADS, KG)], ACT.Copy).then_inc(q_ready, 1)

                def exps(s, k, r):
                    b = k % 2
                    act.wait_ge(bias_ready, s + 1)
                    if at_least(s, 2):
                        act.wait_ge(prob_ready, s - 1)
                    nc.scalar.activation(e_hi[:, b, :], score[:, b, :], ACT.Exp, bias=bias[:, b, 0:1],
                                         scale=1.0).then_inc(exps_done, 1)
                    nc.scalar.activation(e_lo[:, b, :], score[:, b, :], ACT.Exp, bias=bias[:, b, 1:2],
                                         scale=SLOPE).then_inc(exps_done, 1)
                    if at_least(s, RING):
                        act.wait_ge(acc_done, s - RING + 1)
                    nc.scalar.activation(corr[:, k:k + 1], bias[:, b, 2:3], ACT.Exp).then_inc(exps_done, 1)

                def probT_copy(s, k, r):
                    act.wait_ge(probT_psum, s + 1)
                    if at_least(s, 2):
                        act.wait_ge(sum_psum, s - 1)
                    nc.scalar.activation(probT[:, k % 2, :], ps[2 + k % 2][:, 0:G], ACT.Copy)\
                        .then_inc(probT_ready, 1)
                run(act, way.total, RING, 2, [(0, q_copy), (2, exps), (3, probT_copy)])
            branch(act, steps)

            act.wait_ge(den_ready, 1)

            def hn_again(t, k, r):
                act.wait_ge(x_again[k], 16 * (r + 1))
                if at_least(t, NODE_RING):
                    act.wait_ge(xhn_ready, t - NODE_RING + 1)
                    act.wait_ge(hn1T_psum, t - NODE_RING + 1)
                nc.scalar.activation(hn1[:, k, :], x_in[:, k, :], ACT.Identity, bias=nmr[:, bass.ds(t, 1)],
                                     scale=rstd[:, bass.ds(t, 1)]).then_inc(hn1_ready, 1)
                act.wait_ge(hn1_ready, t + 1)
                if at_least(t, NODE_RING):
                    act.wait_ge(or_idle, t - NODE_RING + 1)
                nc.scalar.activation(idle[:, k, :], hn1[:, k, :], ACT.Copy,
                                     scale=no_edge[:, bass.ds(t, 1)]).then_inc(idle_ready, 1)

            def hn1T_copy(t, k, r):
                act.wait_ge(hn1T_psum, t + 1)
                if at_least(t, NODE_RING):
                    act.wait_ge(hs_psum, t - NODE_RING + 1)
                nc.scalar.activation(hnT[:, k, :], ps[k % 2][:, 0:C], ACT.Copy).then_inc(hn1T_ready, 1)

            def std2(t, k, r):
                act.wait_ge(stats2_ready, t + 1)
                nc.scalar.activation(norm2[:, k, 0:1], mv2[:, k, 1:2], ACT.Sqrt, bias=eps[:, 0:1])\
                    .then_inc(std2_ready, 1)

            def hn_second(t, k, r):
                act.wait_ge(norm2_ready, t + 1)
                if at_least(t, NODE_RING):
                    act.wait_ge(hn2_stored[k], 16 * r)
                    act.wait_ge(hn2T_psum, t - NODE_RING + 1)
                nc.scalar.activation(hn[:, k, :], x2[:, k, :], ACT.Identity, bias=norm2[:, k, 2:3],
                                     scale=norm2[:, k, 1:2]).then_inc(hn2_ready, 1)

            def hn2T_copy(t, k, r):
                act.wait_ge(hn2T_psum, t + 1)
                if at_least(t, NODE_RING):
                    act.wait_ge(logit_psum, t - NODE_RING + 1)
                nc.scalar.activation(hn2T[:, k, :], ps[4 + k % 2][:, 0:C], ACT.Copy).then_inc(hn2T_ready, 1)

            run(act, TILES, NODE_RING, 2, [(0, hn_again), (1, hn1T_copy), (2, std2), (3, hn_second),
                                           (4, hn2T_copy)])

            act.wait_ge(shifted, 1)
            nc.scalar.activation(ex, probs, ACT.Exp).then_inc(exp_ready, 1)

            act.wait_ge(slots_ready, 1)

            def xT_copy(t, k, r):
                act.wait_ge(xT_psum, t + 1)
                if at_least(t, 2):
                    act.wait_ge(up_b_psum, t - 1)
                nc.scalar.activation(xT[:, k % 2, :, :].rearrange("p k c -> p (k c)"), ps[4][:, 0:C], ACT.Copy)\
                    .then_inc(xT_ready, 1)

            def silu_first(t, k, r):
                if at_least(t, 1):
                    act.wait_ge(hid_a_ready, t)
                act.wait_ge(up_a_psum, t + 1)
                nc.scalar.activation(s_act[:, 0:HA], ps[0][:, 0:HA], ACT.Silu).then_inc(silu_a, 1)

            def hidT_copy(t, k, r):
                act.wait_ge(hidT_psum, t + 1)
                if at_least(t, 1):
                    act.wait_ge(y_psum, t)
                nc.scalar.activation(hidT[:, 0:4 * P], ps[6][:, 0:4 * P], ACT.Copy).then_inc(hidT_by_act, 1)

            def silu_second(t, k, r):
                if at_least(t, 1):
                    act.wait_ge(hid_b_ready, t)
                act.wait_ge(up_b_psum, t + 1)
                nc.scalar.activation(s_act[:, HA:H], ps[2][:, 0:HB], ACT.Silu).then_inc(silu_b, 1)

            run(act, SLOTS, RING, 1, [(1, silu_first), (2, hidT_copy), (1, silu_second), (0, xT_copy)])

        @block.tensor
        def _(pe):
            mm, tr = nc.tensor.matmul, nc.tensor.transpose
            pe.wait_ge(pool_consts, 2)
            pe.wait_ge(begun_ready, 1)
            mm(ps[5][0:1, 0:PATH], ones[0:GROUPS - 1, 0:1], begun[0:GROUPS - 1, :], start=True, stop=True)
            mm(ps[5][0:1, PATH:PATH + P], start, ident[:, :], start=True, stop=True)
            mm(ps[6][0:1, 0:1], fell, ones[:, 0:1], start=True, stop=True).then_inc(path_psum, 1)
            pe.wait_ge(weights_in, 16 * 7)
            for m in range(KC):
                for k in range(KC):
                    last = mm(ps[7][:, 2 * m:2 * m + 2], wf_nat[:, k, m * P:(m + 1) * P], att_n[:, k, :],
                              start=(k == 0), stop=(k == KC - 1))
            last.then_inc(att_psum, 1)
            pe.wait_ge(wfx_ready, 1)

            def transposed(bank, rows_ap, chunks=KC):
                for c in range(chunks):
                    last = tr(bank[:, c * P:(c + 1) * P], rows_ap[:, c * P:(c + 1) * P], ident[:, :])
                return last

            def hn_T(t, k, r):
                pe.wait_ge(hn_ready, t + 1)
                if at_least(t, 1):
                    pe.wait_ge(hnT_ready, t + 1 - bank_back(k) if at_least(t, 2) else t)
                transposed(ps[k % 2], hn[:, k, :]).then_inc(hnT_psum, 1)

            def z_of(t, k, r):
                pe.wait_ge(hnT_ready, t + 1)
                if at_least(t, 2):
                    pe.wait_ge(z_ready, t + 1 - bank_back(k))
                for c in range(KC):
                    last = mm(ps[2 + k % 2][:, 0:ZR], hnT[:, k, c * P:(c + 1) * P], wfx[:, c, :],
                              start=(c == 0), stop=(c == KC - 1))
                last.then_inc(z_psum, 1)

            def edge_scores(t, k, r):
                pe.wait_ge(vec_loaded[k], 16 * (r + 1))
                for b in range(AT_ONCE):
                    at = ps[4][:, bass.ds(t * (2 * AT_ONCE * KG) + 2 * KG * b, 2 * KG)]\
                        .rearrange("p (g c) -> p c g", c=KG)
                    for c in range(KG):
                        last = mm(at[:, c, :], vec_in[:, k, b * G + c * P:b * G + (c + 1) * P], att_e[:, :],
                                  start=True, stop=True)
                last.then_inc(vec_used, 1)

            run(pe, TILES, NODE_RING, 2, [(0, hn_T), (0, edge_scores), (1, z_of)])
            edge_scores(TILES, 0, TILES // NODE_RING)

            def steps(way):
                def scores(s, k, r):
                    pe.wait_ge(q_ready, s + 1)
                    if at_least(s, 2):
                        pe.wait_ge(max_done, s - 1)
                    for c in range(KG):
                        last = mm(ps[k % 2][:, c * P:(c + 1) * P], q_step[:, k, c:c + 1].to_broadcast([P, P]),
                                  ident[:, :], start=True, stop=True)
                    last.then_inc(scores_psum, 1)

                def prob_T(s, k, r):
                    b = k % 2
                    pe.wait_ge(prob_ready, s + 1)
                    if at_least(s, 2):
                        pe.wait_ge(probT_ready, s - 1)
                    transposed(ps[2 + b], prob[:, b, :], KG).then_inc(probT_psum, 1)

                def weighted(s, k, r):
                    b = k % 2
                    at = once(pe, (way.load_of(pe, s) % LOADS) * (KG * ZR))
                    pe.wait_ge(probT_ready, s + 1)
                    if at_least(s, 2):
                        pe.wait_ge(acc_done, s - 1)
                    for c in range(KG):
                        last = mm(ps[4 + b][:, 0:ZR], probT[:, b, c * P:(c + 1) * P], zg_flat[:, bass.ds(at + c * ZR, ZR)],
                                  start=(c == 0), stop=(c == KG - 1))
                    last.then_inc(sum_psum, 1)
                run(pe, way.total, RING, 2, [(0, scores), (3, weighted), (2, prob_T)])
            branch(pe, steps)

            def hn1_T(t, k, r):
                pe.wait_ge(hn1_ready, t + 1)
                if at_least(t, 1):
                    pe.wait_ge(hn1T_ready, t + 1 - bank_back(k) if at_least(t, 2) else t)
                transposed(ps[k % 2], hn1[:, k, :]).then_inc(hn1T_psum, 1)

            def self_part(t, k, r):
                pe.wait_ge(hn1T_ready, t + 1)
                if at_least(t, 2):
                    pe.wait_ge(with_hs, t + 1 - bank_back(k))
                for c in range(KC):
                    last = mm(ps[2 + k % 2][:, 0:C], hnT[:, k, c * P:(c + 1) * P], wself_sb[:, c, :],
                              start=(c == 0), stop=(c == KC - 1))
                last.then_inc(hs_psum, 1)

            def hn2_T(t, k, r):
                pe.wait_ge(hn2_ready, t + 1)
                if at_least(t, 1):
                    pe.wait_ge(hn2T_ready, t + 1 - bank_back(k) if at_least(t, 2) else t)
                transposed(ps[4 + k % 2], hn[:, k, :]).then_inc(hn2T_psum, 1)

            def logits_of(t, k, r):
                pe.wait_ge(hn2T_ready, t + 1)
                if at_least(t, 2):
                    pe.wait_ge(logit_ready, t + 1 - bank_back(k))
                for c in range(KC):
                    last = mm(ps[6 + k % 2][:, 0:E], hn2T[:, k, c * P:(c + 1) * P], router_sb[:, c, :],
                              start=(c == 0), stop=(c == KC - 1))
                last.then_inc(logit_psum, 1)

            run(pe, TILES, NODE_RING, 2, [(0, hn1_T), (1, self_part), (3, hn2_T), (4, logits_of)])

            pe.wait_ge(choice_ready, 1)
            pe.wait_ge(pool_consts, 3)
            chosen = both.rearrange("p t e -> p e t")
            mm(ps[0][:, 0:RE], before[:, :], chosen, start=True, stop=True)
            mm(ps[1][:, 0:RE], ones[:, 0:P], chosen, start=True, stop=True).then_inc(rank_psum, 1)
            pe.wait_ge(onehot_ready, 1)
            for q in range(S2):
                last = mm(ps[2][:, 0:2 * SLOTS], ohr[:, q, :], moving[:, q, :], start=(q == 0),
                          stop=(q == S2 - 1))
            last.then_inc(token_psum, 1)

            pe.wait_ge(slots_ready, 1)
            for e in range(E):
                pe.wait_ge(experts_in[e], 16)

            def expert(t):
                return pe.value_load(expert_of[0:1, bass.ds(t, 1)], min_val=0, max_val=E - 1)

            def tokens_T(t, k, r):
                pe.wait_ge(row_gathered[k], 16 * (r + 1))
                if at_least(t, 1):
                    pe.wait_ge(xT_ready, t)
                transposed(ps[4], xg[:, k, 0:C]).then_inc(xT_psum, 1)

            def up(e, k, lo, n, banks):
                for bank, at in zip(banks, (W1_AT, W3_AT)):
                    for c in range(KC):
                        last = mm(bank[:, 0:n], xT[:, k % 2, c, :], Wf[:, bass.ds(e * WE + (at + c * H + lo), n)],
                                  start=(c == 0), stop=(c == KC - 1))
                return last

            def up_first(t, k, r):
                e = expert(t)
                pe.wait_ge(xT_ready, t + 1)
                if at_least(t, 1):
                    pe.wait_ge(hid_a_ready, t)
                up(e, k, 0, HA, (ps[0], ps[1])).then_inc(up_a_psum, 1)

            def up_second(t, k, r):
                e = expert(t)
                if at_least(t, 1):
                    pe.wait_ge(hid_b_ready, t)
                up(e, k, HA, HB, (ps[2], ps[3])).then_inc(up_b_psum, 1)

            def hidden_T(t, k, r):
                pe.wait_ge(hid_a_ready, t + 1)
                pe.wait_ge(hid_b_ready, t + 1)
                if at_least(t, 1):
                    pe.wait_ge(hidT_by_act, t)
                    pe.wait_ge(hidT_by_dve, t)
                for i, (a, n) in enumerate(HC):
                    last = tr(ps[6 + i // 4][0:n, (i % 4) * P:(i % 4 + 1) * P], hid[:, k % 2, a:a + n],
                              ident[:, :])
                last.then_inc(hidT_psum, 1)

            def down(t, k, r):
                e = expert(t)
                pe.wait_ge(hidT_by_act, t + 1)
                pe.wait_ge(hidT_by_dve, t + 1)
                if at_least(t, 1):
                    pe.wait_ge(y_ready, t)
                for i, (a, n) in enumerate(HC):
                    last = mm(ps[5][:, 0:C], hidT[0:n, i * P:(i + 1) * P],
                              Wf[0:n, bass.ds(e * WE + (W2_AT + i * C), C)], start=(i == 0), stop=(i == NH - 1))
                last.then_inc(y_psum, 1)

            run(pe, SLOTS, RING, 1, [(1, up_first), (2, hidden_T), (1, up_second), (2, down), (0, tokens_T)])

        @block.vector
        def _(dve):
            v = nc.vector
            count = [0]

            def link(ins):
                count[0] += 1
                ins.then_inc(chain, 1)
                dve.wait_ge(chain, count[0])

            v.memset(eps[:, :], EPS).then_inc(eps_ready, 1)
            link(v.memset(acc[:, :], 0.0))
            link(v.memset(z_out[:, :, C + 1:ZR], 1.0))
            dve.wait_ge(pool_consts, 7)
            v.tensor_copy(iota_row[:, :], io_i)
            v.tensor_copy(thr[:, :], io_t)
            v.tensor_copy(step_no, io_s)
            link(v.tensor_copy(node_id[:, :], io_n))
            link(v.tensor_scalar(valid[:, :], node_id[:, :], float(N), None, ALU.is_lt))
            dve.wait_ge(dst_flat_in, 48)
            v.tensor_tensor(falls, dst_here, dst_next, ALU.is_gt)
            link(v.tensor_copy(last_f, last_dst))
            v.tensor_reduce(fell, falls, AX.X, ALU.max)
            link(v.tensor_scalar(ge_thr[:, 0:TILES - 1], thr[:, 0:TILES - 1], last_f, None, ALU.is_le))
            link(v.tensor_reduce(start, ge_thr[:, 0:TILES - 1], AX.X, ALU.add))
            link(v.tensor_scalar(start, start, node_id[:, 0:1], 1.0, ALU.add, ALU.add))
            link(v.tensor_scalar(begun, step_no, start, None, ALU.is_ge))
            v.memset(tick[:, :], 0.0).then_inc(begun_ready, 1)
            dve.wait_ge(path_psum, 1)
            v.tensor_scalar(flag[0:1, :], ps[6][0:1, 0:1], 0.0, None, ALU.is_gt)
            v.tensor_copy(path_i[0:1, :], ps[5][0:1, 0:PATH])
            v.tensor_copy(path_next[0:1, :], ps[5][0:1, PATH:PATH + P])
            link(v.tensor_tensor(path_j[0:1, :], step_no[0:1, :], ps[5][0:1, 0:PATH], ALU.subtract))
            v.memset(tick[:, :], 0.0).then_inc(path_ready, 1)
            dve.wait_ge(weights_in, 16 * 7)
            dve.wait_ge(att_psum, 1)
            for m in range(KC):
                last = v.tensor_copy(wfx[:, m, C:ZR], ps[7][:, 2 * m:2 * m + 2])
            last.then_inc(wfx_ready, 1)

            def norm(t, k, r):
                dve.wait_ge(x_loaded[k], 16 * (r + 1))
                v.bn_stats(st6[:, k, :], x_in[:, k, :]).then_inc(bn_done, 1)
                dve.wait_ge(bn_done, t + 1)
                held(dve)
                v.bn_aggr(mv2[:, k, :], st6[:, k, :]).then_inc(stats_ready, 1)

            def normed(t, k, r):
                dve.wait_ge(std_ready, t + 1)
                v.reciprocal(rstd[:, bass.ds(t, 1)], norm2[:, k, 0:1]).then_inc(rstd_ready, 1)
                dve.wait_ge(rstd_ready, t + 1)
                v.scalar_tensor_tensor(nmr[:, bass.ds(t, 1)], mv2[:, k, 0:1], -1.0, rstd[:, bass.ds(t, 1)], ALU.mult,
                                       ALU.mult).then_inc(nmr_ready, 1)

            def z_copy(t, k, r):
                bank = ps[2 + k % 2]
                dve.wait_ge(z_psum, t + 1)
                if at_least(t, NODE_RING):
                    dve.wait_ge(z_stored[k], 16 * r)
                v.tensor_copy(z_out[:, k, 0:C + 1], bank[:, 0:C + 1])
                v.tensor_copy(scal[:, cols(t, 3, 1)], bank[:, C + 1:ZR])
                v.tensor_scalar(scal[:, bass.ds(t * 3 + 1, 1)], bank[:, C + 1:ZR], SLOPE, None, ALU.mult)\
                    .then_inc(z_ready, 1)

            run(dve, TILES, NODE_RING, 2, [(0, norm), (1, normed), (4, z_copy)])
            link(v.memset(scal[:, :].rearrange("p (t c) -> p t c", c=3)[:, :, 2], NO_MAX))
            dve.wait_ge(vec_used, EDGE_LOADS)
            link(v.tensor_copy(edge_score, ps[4][:, 0:GROUPS * KG]))
            v.memset(tick[:, :], 0.0).then_inc(edge_score_ready, 1)

            def steps(way):
                def mask_of(s, k, r):
                    n = once(dve, way.load_of(dve, s))
                    j = way.tile(dve, s)
                    dve.wait_ge(dst_here_now, n + 1)
                    if at_least(s, 2):
                        dve.wait_ge(max_done, s - 1)
                    v.tensor_scalar(mask[:, k % 2, :], dst_in[:, cols(n % LOADS, G)], node_id[:, bass.ds(j, 1)],
                                    MASKED, ALU.not_equal, ALU.mult).then_inc(masked, 1)

                def largest(s, k, r):
                    b = k % 2
                    dve.wait_ge(masked, s + 1)
                    dve.wait_ge(scores_psum, s + 1)
                    if at_least(s, 2):
                        dve.wait_ge(exps_done, 3 * (s - 1))
                    held(dve)
                    v.tensor_tensor_reduce(out=score[:, b, :], in0=ps[b][:, 0:G], in1=mask[:, b, :], scale=1.0,
                                           scalar=2 * MASKED, op0=ALU.add, op1=ALU.max,
                                           accum_out=small[:, k, 0:1]).then_inc(max_done, 1)

                def with_s2(s, k, r):
                    j = way.tile(dve, s)
                    dve.wait_ge(max_done, s + 1)
                    v.tensor_scalar(small[:, k, 1:2], small[:, k, 0:1], scal[:, bass.ds(j * 3, 1)], None, ALU.add)\
                        .then_inc(plus_s2, 1)

                def leaky(s, k, r):
                    dve.wait_ge(plus_s2, s + 1)
                    v.scalar_tensor_tensor(small[:, k, 2:3], small[:, k, 1:2], SLOPE, small[:, k, 1:2], ALU.mult,
                                           ALU.max).then_inc(leaky_done, 1)

                def new_max(s, k, r):
                    j = once(dve, way.tile(dve, s) * 3)
                    dve.wait_ge(leaky_done, s + 1)
                    if at_least(s, 1):
                        dve.wait_ge(run_done, s)
                    v.tensor_tensor(small[:, k, 3:4], small[:, k, 2:3], scal[:, bass.ds(j + 2, 1)], ALU.max)\
                        .then_inc(newmax_done, 1)
                    dve.wait_ge(newmax_done, s + 1)
                    v.tensor_scalar(bias[:, k % 2, :], scal[:, bass.ds(j, 3)], small[:, k, 3:4], None,
                                    ALU.subtract).then_inc(bias_ready, 1)

                def keep_max(s, k, r):
                    j = way.tile(dve, s)
                    dve.wait_ge(bias_ready, s + 1)
                    held(dve)
                    v.tensor_copy(scal[:, bass.ds(j * 3 + 2, 1)], small[:, k, 3:4]).then_inc(run_done, 1)

                def probs_of(s, k, r):
                    b = k % 2
                    dve.wait_ge(exps_done, 3 * (s + 1))
                    if at_least(s, 2):
                        dve.wait_ge(probT_psum, s - 1)
                    v.tensor_tensor(prob[:, b, :], e_hi[:, b, :], e_lo[:, b, :], ALU.max)\
                        .then_inc(prob_ready, 1)

                def add_sum(s, k, r):
                    j = way.tile(dve, s)
                    dve.wait_ge(sum_psum, s + 1)
                    if at_least(s, 1):
                        dve.wait_ge(acc_done, s)
                    at = acc[:, cols(j, ZR)]
                    v.scalar_tensor_tensor(at, at, corr[:, k:k + 1], ps[4 + k % 2][:, 0:ZR], ALU.mult, ALU.add)\
                        .then_inc(acc_done, 1)
                run(dve, way.total, RING, 2, [(1, largest), (2, keep_max), (0, mask_of), (1, with_s2),
                                              (2, probs_of), (1, leaky), (4, add_sum), (1, new_max)])
                dve.wait_ge(acc_done, way.total)
            branch(dve, steps)

            den = acc[:, :].rearrange("p (t c) -> p t c", c=ZR)[:, :, C + 1]
            v.tensor_scalar(has_edge[:, :], den, 0.0, None, ALU.is_gt)
            v.tensor_scalar(no_edge[:, :], den, 0.0, None, ALU.is_le)
            link(v.tensor_scalar(inv_den[:, :], den, 1e-30, None, ALU.max))
            link(v.reciprocal(inv_den[:, :], inv_den[:, :]))
            v.memset(tick[:, :], 0.0).then_inc(den_ready, 1)

            def new_x(t, k, r):
                a = acc[:, cols(t, ZR, C)]
                dve.wait_ge(hs_psum, t + 1)
                v.scalar_tensor_tensor(a, a, inv_den[:, bass.ds(t, 1)], ps[2 + k % 2][:, 0:C], ALU.mult, ALU.add)\
                    .then_inc(with_hs, 1)
                dve.wait_ge(with_hs, t + 1)
                dve.wait_ge(idle_ready, t + 1)
                v.scalar_tensor_tensor(a, a, has_edge[:, bass.ds(t, 1)], idle[:, k, :], ALU.mult, ALU.add)\
                    .then_inc(or_idle, 1)
                dve.wait_ge(or_idle, t + 1)
                dve.wait_ge(xhn_ready, t + 1)
                if at_least(t, NODE_RING):
                    dve.wait_ge(x2_stored[k], 16 * r)
                    dve.wait_ge(hn2_ready, t - NODE_RING + 1)
                v.scalar_tensor_tensor(x2[:, k, :], a, 0.0, x_hn[:, k, :], ALU.max, ALU.add).then_inc(x2_ready, 1)
                dve.wait_ge(x2_ready, t + 1)
                v.bn_stats(st6[:, k, :], x2[:, k, :]).then_inc(bn2_done, 1)
                dve.wait_ge(bn2_done, t + 1)
                held(dve)
                v.bn_aggr(mv2[:, k, :], st6[:, k, :]).then_inc(stats2_ready, 1)

            def scale2(t, k, r):
                dve.wait_ge(std2_ready, t + 1)
                v.reciprocal(norm2[:, k, 1:2], norm2[:, k, 0:1]).then_inc(rstd2_ready, 1)
                dve.wait_ge(rstd2_ready, t + 1)
                v.scalar_tensor_tensor(norm2[:, k, 2:3], mv2[:, k, 0:1], -1.0, norm2[:, k, 1:2], ALU.mult,
                                       ALU.mult).then_inc(norm2_ready, 1)

            def logit_copy(t, k, r):
                dve.wait_ge(logit_psum, t + 1)
                v.tensor_copy(logits[:, cols(t, E)], ps[6 + k % 2][:, 0:E]).then_inc(logit_ready, 1)

            run(dve, TILES, NODE_RING, 2, [(1, new_x), (2, scale2), (4, logit_copy)])
            dve.wait_ge(logit_ready, TILES)

            lg = logits[:, :].rearrange("p (t e) -> p t e", e=E)

            def over_e(a):
                return a.unsqueeze(2).to_broadcast([P, TILES, E])

            def flat(a):
                return a.rearrange("p a b -> p (a b)")

            dve.wait_ge(late_ramps, 3)
            link(v.tensor_copy(exp_neg, io_e))
            link(v.tensor_reduce(t25[:, 0, :], lg, AX.X, ALU.max))
            link(v.tensor_tensor(probs, lg, over_e(t25[:, 0, :]), ALU.subtract))
            v.memset(tick[:, :], 0.0).then_inc(shifted, 1)
            dve.wait_ge(exp_ready, 1)
            link(v.tensor_reduce(t25[:, 1, :], ex, AX.X, ALU.add))
            link(v.reciprocal(t25[:, 1, :], t25[:, 1, :]))
            link(v.tensor_tensor(probs, ex, over_e(t25[:, 1, :]), ALU.mult))
            en = exp_neg.unsqueeze(1).to_broadcast([P, TILES, E])
            for c, (of, top) in enumerate(((probs, top0), (rest, top1))):
                best = t25[:, 2 + c, :]
                link(v.tensor_reduce(best, of, AX.X, ALU.max))
                link(v.tensor_tensor(eq, of, over_e(best), ALU.is_ge))
                link(v.tensor_tensor(cand, eq, en, ALU.mult))
                link(v.tensor_reduce(t25[:, 4, :], cand, AX.X, ALU.min))
                link(v.tensor_tensor(top, en, over_e(t25[:, 4, :]), ALU.is_equal))
                if c == 0:
                    link(v.scalar_tensor_tensor(flat(rest), flat(top0), -2.0, flat(probs), ALU.mult, ALU.add))
            link(v.tensor_tensor(t25[:, 5, :], t25[:, 2, :], t25[:, 3, :], ALU.add))
            link(v.tensor_scalar(t25[:, 5, :], t25[:, 5, :], 1e-9, None, ALU.add))
            link(v.reciprocal(t25[:, 5, :], t25[:, 5, :]))
            link(v.tensor_tensor(both, top0, top1, ALU.add))
            link(v.tensor_tensor(gates, probs, both, ALU.mult))
            link(v.tensor_tensor(gates, gates, over_e(t25[:, 5, :]), ALU.mult))
            v.memset(tick[:, :], 0.0).then_inc(gates_ready, 1)
            for top in (top0, top1):
                link(v.tensor_tensor(top, top, over_e(valid[:, :]), ALU.mult))
            link(v.tensor_tensor(both, both, over_e(valid[:, :]), ALU.mult))
            v.memset(tick[:, :], 0.0).then_inc(choice_ready, 1)
            dve.wait_ge(rank_psum, 1)
            link(v.tensor_tensor_scan(flat(cum), ones[:, 0:RE], ps[1][:, 0:RE], 0.0, ALU.mult, ALU.add))
            link(v.tensor_tensor(flat(cum_ex), flat(cum), ps[1][:, 0:RE], ALU.subtract))
            link(v.tensor_tensor(e8[:, 0, :], cum[:, :, TILES - 1], cum_ex[:, :, 0], ALU.subtract))
            link(v.tensor_scalar(t25[:, 0, :], thr[:, :], -float(P), None, ALU.add))
            link(v.tensor_tensor(tmp_ej, e8[:, 0, :].unsqueeze(2).to_broadcast([P, E, TILES]),
                                 t25[:, 0, :].unsqueeze(1).to_broadcast([P, E, TILES]), ALU.is_gt))
            link(v.tensor_reduce(e8[:, 1, :], tmp_ej, AX.X, ALU.add))
            link(v.tensor_tensor_scan(e8[:, 2, :], ones[:, 0:E], e8[:, 1, :], 0.0, ALU.mult, ALU.add))
            link(v.tensor_tensor(e8[:, 3, :], e8[:, 2, :], e8[:, 1, :], ALU.subtract))
            link(v.scalar_tensor_tensor(e8[:, 4, :], e8[:, 3, :], float(P), cum_ex[:, :, 0], ALU.mult,
                                        ALU.subtract))
            link(v.tensor_tensor(flat(slot), flat(cum_ex), ps[0][:, 0:RE], ALU.add))
            link(v.tensor_tensor(slot, slot, e8[:, 4, :].unsqueeze(2).to_broadcast([P, E, TILES]), ALU.add))
            for c, top in enumerate((top0, top1)):
                link(v.tensor_tensor(cand, top, slot.rearrange("p e t -> p t e"), ALU.mult))
                link(v.tensor_reduce(slots_f[:, c * TILES:(c + 1) * TILES], cand, AX.X, ALU.add))
            link(v.tensor_copy(slots_i, slots_f))
            v.tensor_scalar(st_i, slots_i, 7, None, ALU.logical_shift_right)
            link(v.tensor_scalar(sr_i, slots_i, P - 1, None, ALU.bitwise_and))
            v.tensor_copy(st_f, st_i)
            link(v.tensor_copy(sr_f, sr_i))
            link(v.tensor_scalar(sr_f, sr_f, 1.0, None, ALU.add))
            for c in range(2):
                a = sr_f[:, c * TILES:(c + 1) * TILES]
                link(v.tensor_tensor(a, a, valid[:, :], ALU.mult))
                v.tensor_copy(tile_b[:, c * TILES:(c + 1) * TILES], iota_row[:, 0:TILES])
            link(v.tensor_scalar(sr_f, sr_f, -1.0, None, ALU.add))
            v.tensor_copy(sr_b, sr_f)
            v.tensor_copy(st_b, st_f)
            v.tensor_copy(iota_b, iota_row[:, :])
            link(v.tensor_copy(slot_no, io_slot))
            v.tensor_copy(slot_b, slot_no)
            link(v.tensor_copy(p_plus1, io_p))
            link(v.tensor_scalar(dump_p, p_plus1, float(DUMP), None, ALU.add))
            v.tensor_tensor(ohr, iota_b.unsqueeze(1).to_broadcast([P, S2, P]),
                            sr_b.unsqueeze(2).to_broadcast([P, S2, P]), ALU.is_equal)
            link(v.tensor_tensor(oht, slot_b.unsqueeze(1).to_broadcast([P, S2, SLOTS]),
                                 st_b.unsqueeze(2).to_broadcast([P, S2, SLOTS]), ALU.is_equal))
            v.tensor_tensor(moving[:, :, 0:SLOTS], oht, tile_b.unsqueeze(2).to_broadcast([P, S2, SLOTS]),
                            ALU.mult)
            link(v.tensor_scalar(moving[:, :, SLOTS:2 * SLOTS], oht, p_plus1, None, ALU.mult))
            v.memset(tick[:, :], 0.0).then_inc(onehot_ready, 1)
            link(v.tensor_tensor(exp_cmp, e8[:, 3, 1:E].unsqueeze(1).to_broadcast([P, SLOTS, E - 1]),
                                 slot_no.unsqueeze(2).to_broadcast([P, SLOTS, E - 1]), ALU.is_le))
            link(v.tensor_reduce(exp_f, exp_cmp, AX.X, ALU.add))
            link(v.tensor_copy(expert_of[0:1, :], exp_f[0:1, :]))
            dve.wait_ge(token_psum, 1)
            link(v.tensor_copy(tok, ps[2][:, SLOTS:2 * SLOTS]))
            link(v.scalar_tensor_tensor(tok, ps[2][:, 0:SLOTS], float(P), tok, ALU.mult, ALU.add))
            link(v.tensor_scalar(tok, tok, -1.0, None, ALU.add))
            link(v.tensor_scalar(unused, tok, 0.0, None, ALU.is_lt))
            link(v.scalar_tensor_tensor(row_f, unused, dump_p, tok, ALU.mult, ALU.add))
            link(v.tensor_scalar(tok, tok, 0.0, None, ALU.max))
            pair = slot_rows[:, :].rearrange("p (t c) -> p t c", c=2)
            v.tensor_copy(pair[:, :, 0], tok)
            link(v.tensor_copy(pair[:, :, 1], row_f))
            dve.wait_ge(gates_stored, 16)
            v.memset(tick[:, :], 0.0).then_inc(slots_ready, 1)

            def hid_first(t, k, r):
                dve.wait_ge(silu_a, t + 1)
                v.tensor_tensor(hid[:, k % 2, 0:HA], s_act[:, 0:HA], ps[1][:, 0:HA], ALU.mult)\
                    .then_inc(hid_a_ready, 1)

            def hid_second(t, k, r):
                dve.wait_ge(silu_b, t + 1)
                v.tensor_tensor(hid[:, k % 2, HA:H], s_act[:, HA:H], ps[3][:, 0:HB], ALU.mult)\
                    .then_inc(hid_b_ready, 1)

            def hidT_rest(t, k, r):
                dve.wait_ge(hidT_psum, t + 1)
                if at_least(t, 1):
                    dve.wait_ge(y_psum, t)
                n = HC[-1][1]
                v.tensor_copy(hidT[:, 4 * P:5 * P], ps[7][:, 0:P])
                v.tensor_copy(hidT[0:n, 5 * P:6 * P], ps[7][0:n, P:2 * P]).then_inc(hidT_by_dve, 1)

            def gated(t, k, r):
                e = dve.value_load(expert_of[0:1, bass.ds(t, 1)], min_val=0, max_val=E - 1)
                dve.wait_ge(y_psum, t + 1)
                if at_least(t, 2):
                    dve.wait_ge(y_added, 16 * (t - 1))
                v.tensor_scalar(y_out[:, k % 2, :], ps[5][:, 0:C], xg_flat[:, bass.ds(e + (k * TR + C), 1)],
                                None, ALU.mult).then_inc(y_ready, 1)

            run(dve, SLOTS, RING, 1, [(1, hid_first), (2, hidT_rest), (1, hid_second), (2, gated)])


def kernel(x, src, dst, edge_attr_64, node_vec1, L0_gnn_W_self, L0_gnn_W_func, L0_gnn_W_att,
           L0_ffn_router_w, L0_ffn_w1, L0_ffn_w2, L0_ffn_w3):
    import numpy as np
    import concourse.bacc as bacc
    from concourse.bass_utils import run_bass_kernel_spmd

    pad = lambda a, n, value=0: np.concatenate([a, np.full((n - a.shape[0],) + a.shape[1:], value, a.dtype)])
    f = lambda a: np.ascontiguousarray(a)
    x, src, dst = np.asarray(x), np.asarray(src), np.asarray(dst)
    ea, att = np.asarray(edge_attr_64), np.asarray(L0_gnn_W_att)
    wfunc, wself = np.asarray(L0_gnn_W_func), np.asarray(L0_gnn_W_self)
    w1, w2, w3 = np.asarray(L0_ffn_w1), np.asarray(L0_ffn_w2), np.asarray(L0_ffn_w3)
    n = GROUPS * G
    up = [w.transpose(0, 2, 1).reshape(E, KC, P, H).transpose(0, 2, 1, 3).reshape(E, P, KC * H) for w in (w1, w3)]
    w2p = np.concatenate([w2.transpose(0, 2, 1), np.zeros((E, NH * P - H, C), w2.dtype)], axis=1)
    down = w2p.reshape(E, NH, P, C).transpose(0, 2, 1, 3).reshape(E, P, NH * C)
    dst_rows = pad(dst, n + G, PAD_DST).reshape(GROUPS + 1, G)
    arrays = {
        "in_x": f(pad(x, NP)),
        "in_src": f(pad(src, n).reshape(GROUPS, KG, P).transpose(0, 2, 1)),
        "in_dst": f(dst_rows),
        "in_last": f(pad(dst_rows[0:GROUPS, G - 1], P, PAD_DST).reshape(P, 1)),
        "in_wt": f(pad(ea, n).reshape(GROUPS, G, EF).transpose(0, 2, 1).reshape(GROUPS // 2, P, G)),
        "in_wfunc": f(wfunc),
        "in_wfunct": f(wfunc.T),
        "in_wselft": f(wself.T),
        "in_attn": f(att[0, 0:2 * C].reshape(2, C).T),
        "in_atte": f(att[0, 2 * C:].reshape(EF, 1)),
        "in_router": f(np.asarray(L0_ffn_router_w).T),
        "in_experts": f(np.concatenate([up[0], up[1], down], axis=2)),
    }
    nc = bacc.Bacc("TRN2", target_bir_lowering=False, num_devices=1)
    args = [nc.dram_tensor(k, a.shape, mybir.dt.from_np(a.dtype), kind="ExternalInput").ap()
            for k, a in arrays.items()]
    out = nc.dram_tensor("out_rows", (OUT_ROWS, C), mybir.dt.float32, kind="ExternalOutput").ap()
    build(nc, *args, out)
    r = run_bass_kernel_spmd(nc, [arrays], core_ids=[0])
    return r.results[0]["out_rows"][0:N]
```

```python
from contextlib import ExitStack

import concourse.bass as bass
from concourse import mybir

P = 128
N, C, EDGES, EF = 3125, 256, 53125, 64
E, H = 8, 682
TILES = -(-N // P)
NP = TILES * P
G = 512
KG = G // P
LOADS = 8
GROUPS = -(-EDGES // (LOADS * G)) * LOADS
RING = 4
PATH = GROUPS + TILES - 1
PAIRS = GROUPS * TILES
PAD_DST = TILES * P
ZR = C + 2
TR = C + E
KC = C // P
HC = [(a, min(P, H - a)) for a in range(0, H, P)]
NH = len(HC)
HA = 3 * P
HB = H - HA
W1_AT, W3_AT, W2_AT = 0, KC * H, 2 * KC * H
WE = W2_AT + NH * C
RAW = 3
PIECES = ((0, 2 * WE // 3), (2 * WE // 3, WE))
SLOTS = (2 * N + E * (P - 1)) // P
DUMP = NP
OUT_ROWS = NP + P
NODE_RING = 5
SUM_LAG = 4
SLOPE = 0.01
QE = GROUPS * G // P
EXPERTS_AFTER = (LOADS, LOADS + 3, LOADS + 6)
AT_ONCE = 4 * KG
EDGE_LOADS = GROUPS * KG // AT_ONCE
S2 = 2 * TILES
RE = TILES * E
LATE = max(S2 * SLOTS + 3 * H + NH * P + 2 * C, 12 * G)
EPS = 1e-5
MASKED = -1e30
NO_MAX = -1e26
assert GROUPS <= P and PATH % RING == 0 and PAIRS % LOADS == 0 and EDGE_LOADS == TILES + 1
assert TILES % NODE_RING == 0 and SLOTS % RING == 0


def build(nc, x, src, dst, dst_last, wt, w_func, w_func_t, w_self_t, att_nodes, att_edge, router, experts,
          out):
    fp32, i32, bf16, fp32r = mybir.dt.float32, mybir.dt.int32, mybir.dt.bfloat16, mybir.dt.float32r
    ALU, ACT, AX = mybir.AluOpType, mybir.ActivationFunctionType, mybir.AxisListType
    ztab = nc.dram_tensor("ztab", [NP, ZR], fp32, kind="Internal").ap()
    ttab = nc.dram_tensor("ttab", [NP, TR], fp32, kind="Internal").ap()

    with ExitStack() as ctx:
        def sb(name, shape, dt=fp32):
            return ctx.enter_context(nc.sbuf_tensor(name, shape, dt))

        def sem(name):
            return ctx.enter_context(nc.semaphore(name))

        with nc.sbuf_tensor("early", [P, 5, WE], fp32) as early:
            pass
        split_w = sb("split_w", [P, 4 * WE], fp32r)
        operands = sb("operands", [P, WE], fp32r)
        W = sb("W", [P, RAW, WE])
        acc = sb("acc", [P, TILES * ZR])
        late = sb("late", [P, LATE])
        ident = sb("ident", [P, P])
        iota_row = sb("iota_row", [P, P])
        before = sb("before", [P, P])
        ones = sb("ones", [P, 2 * P])
        zero_rows = sb("zero_rows", [P, C])
        wself_sb = sb("wself_sb", [P, KC, C])
        router_sb = sb("router_sb", [P, KC, E])
        att_e = sb("att_e", [P, EF])
        att_n = sb("att_n", [P, KC, 2])
        node_id = sb("node_id", [P, TILES])
        valid = sb("valid", [P, TILES])
        thr = sb("thr", [P, TILES])
        scal = sb("scal", [P, TILES * 3])
        rstd = sb("rstd", [P, TILES])
        nmr = sb("nmr", [P, TILES])
        eps = sb("eps", [P, 1])
        inv_den = sb("inv_den", [P, TILES])
        has_edge = sb("has_edge", [P, TILES])
        no_edge = sb("no_edge", [P, TILES])
        logits = sb("logits", [P, TILES * E])
        path_i = sb("path_i", [1, PATH], i32)
        path_j = sb("path_j", [1, PATH], i32)
        turn_word = sb("turn_word", [1, PATH], i32)
        path_next = sb("path_next", [1, P], i32)
        flag = sb("flag", [1, 1], i32)
        split_next = sb("split_next", [1, SLOTS], i32)
        expert_of = sb("expert_of", [1, SLOTS], i32)
        slot_rows = sb("slot_rows", [P, SLOTS * 2], i32)
        row_ix = sb("row_ix", [P, RING, 2], i32)
        xg = sb("xg", [P, RING, TR])
        tick = sb("tick", [P, 1])

        def carve(region, at, shape, dt=fp32):
            n = 1
            for d in shape:
                n *= d
            words = n if dt != bf16 else n // 2
            v = region[:, at:at + words]
            if dt != fp32:
                v = v.bitcast(dt)
            if len(shape) == 2:
                v = v.rearrange("p (a b) -> p a b", b=shape[1])
            return v, at + words

        z, o = early[:, 0, :], 0
        dst_here, o = carve(z, o, [QE], i32)
        dst_next, o = carve(z, o, [QE], i32)
        falls, o = carve(z, o, [QE])
        last_dst, o = carve(z, o, [1], i32)
        last_f, o = carve(z, o, [1])
        start, o = carve(z, o, [1])
        ge_thr, o = carve(z, o, [TILES])
        step_no, o = carve(z, o, [PATH])
        begun, o = carve(z, o, [PATH])
        fell, o = carve(z, o, [1])
        io_i, o = carve(z, o, [P], i32)
        io_s, o = carve(z, o, [PATH], i32)
        io_t, o = carve(z, o, [TILES], i32)
        io_n, o = carve(z, o, [TILES], i32)
        assert o <= WE
        edge_score, o = carve(z, o, [GROUPS * KG])
        q, o = carve(z, o, [LOADS * KG])
        q_step, o = carve(z, o, [RING, KG])
        bias, o = carve(z, o, [2, 3])
        corr, o = carve(z, o, [RING])
        small, o = carve(z, o, [RING, 4])
        src_in, o = carve(z, o, [LOADS, KG], i32)
        step_tile, o = carve(z, o, [PATH])
        word_f, o = carve(z, o, [PATH])
        step_node, o = carve(z, o, [PATH])
        step_terms, o = carve(z, o, [PATH + 1, 3])
        tile_hot, o = carve(z, o, [PATH])
        s2T, o = carve(z, o, [P])
        assert o <= WE
        z, o = early[:, 1, :], 0
        wfx, o = carve(z, o, [KC, ZR])
        wf_nat, o = carve(z, o, [KC, C])
        hnT, o = carve(z, o, [NODE_RING, C])
        hn1, o = carve(z, o, [NODE_RING, C])
        st6, o = carve(z, o, [NODE_RING, 6])
        mv2, o = carve(z, o, [NODE_RING, 2])
        norm2, o = carve(z, o, [NODE_RING, 3])
        assert o <= WE
        z, o = early[:, 2, :], 0
        x_in, o = carve(z, o, [NODE_RING, C])
        hn, o = carve(z, o, [NODE_RING, C])
        z_out, _ = carve(z, o, [NODE_RING, ZR])
        x2, _ = carve(z, o, [NODE_RING, C])
        assert o + NODE_RING * ZR <= WE
        z = early[:, 2:4, :].rearrange("p e w -> p (e w)")
        zg, o = carve(z, 0, [LOADS * KG, ZR])
        assert o <= 2 * WE
        zg_flat = z
        step_terms_flat = step_terms.rearrange("p s c -> p (s c)")
        z = early[:, 3, :]
        o = 0
        x_hn, o = carve(z, o, [NODE_RING, C])
        idle, o = carve(z, o, [NODE_RING, C])
        hn2T, o = carve(z, o, [NODE_RING, C])
        assert o <= WE
        dst_in, o = carve(early[:, 4, :], 0, [LOADS * G], i32)
        assert o <= WE
        vec_prod, o = carve(early[:, 4, :], 0, [2 * AT_ONCE, EF])
        assert o <= WE
        vec_prod_flat = vec_prod.rearrange("p a b -> p (a b)")
        vec_in, o = carve(late, 0, [NODE_RING, AT_ONCE * EF])
        assert o <= LATE
        mask, o = carve(late, 0, [2, G])
        score, o = carve(late, o, [2, G])
        e_hi, o = carve(late, o, [2, G])
        e_lo, o = carve(late, o, [2, G])
        prob, o = carve(late, o, [2, G])
        probT, o = carve(late, o, [2, G])
        assert o <= LATE
        ohr, o = carve(acc, 0, [S2, P], bf16)
        oht, o = carve(acc, o, [S2, SLOTS], bf16)
        iota_b, o = carve(acc, o, [P], bf16)
        slots_f, o = carve(acc, o, [S2])
        slots_i, o = carve(acc, o, [S2], i32)
        st_i, o = carve(acc, o, [S2], i32)
        sr_i, o = carve(acc, o, [S2], i32)
        st_f, o = carve(acc, o, [S2])
        sr_f, o = carve(acc, o, [S2])
        st_b, o = carve(acc, o, [S2], bf16)
        sr_b, o = carve(acc, o, [S2], bf16)
        tile_b, o = carve(acc, o, [S2], bf16)
        io_slot, o = carve(acc, o, [SLOTS], i32)
        slot_no, o = carve(acc, o, [SLOTS])
        slot_b, o = carve(acc, o, [SLOTS], bf16)
        tok, o = carve(acc, o, [SLOTS])
        unused, o = carve(acc, o, [SLOTS])
        row_f, o = carve(acc, o, [SLOTS])
        exp_cmp, o = carve(acc, o, [SLOTS, E - 1])
        exp_f, o = carve(acc, o, [SLOTS])
        split_f, o = carve(acc, o, [SLOTS])
        behind_f, o = carve(acc, o, [SLOTS])
        p_plus1, o = carve(acc, o, [1])
        dump_p, o = carve(acc, o, [1])
        io_p, o = carve(acc, o, [1], i32)
        exp_neg, o = carve(acc, o, [E])
        io_e, o = carve(acc, o, [E], i32)
        assert o <= TILES * ZR
        moving, behind = carve(late, 0, [S2, 2 * SLOTS], bf16)
        o = behind
        s_act, o = carve(late, o, [H])
        hid, o = carve(late, o, [2, H])
        y_out, o = carve(late, o, [2, C])
        assert o <= LATE
        o = behind
        ex, o = carve(late, o, [TILES, E])
        probs, o = carve(late, o, [TILES, E])
        rest, o = carve(late, o, [TILES, E])
        eq, o = carve(late, o, [TILES, E])
        cand, o = carve(late, o, [TILES, E])
        top0, o = carve(late, o, [TILES, E])
        top1, o = carve(late, o, [TILES, E])
        both, o = carve(late, o, [TILES, E])
        gates, o = carve(late, o, [TILES, E])
        cum, o = carve(late, o, [E, TILES])
        cum_ex, o = carve(late, o, [E, TILES])
        slot, o = carve(late, o, [E, TILES])
        tmp_ej, o = carve(late, o, [E, TILES])
        t25, o = carve(late, o, [6, TILES])
        e8, o = carve(late, o, [6, E])
        assert o <= LATE
        xT_hi = operands[:, 0:2 * C]
        xT_lo = operands[:, 2 * C:4 * C]
        hidT_hi = operands[:, 4 * C:4 * C + NH * P]
        hidT_lo = operands[:, 4 * C + NH * P:4 * C + 2 * NH * P]
        Wf = W[:, :, :].rearrange("p e w -> p (e w)")
        scal_by_tile = scal[:, :].rearrange("p (t c) -> p t c", c=3)
        xg_flat = xg[:, :, :].rearrange("p a b -> p (a b)")

        ps = [ctx.enter_context(nc.psum_tensor(f"bank{b}", [P, 512], fp32)) for b in range(8)]

        pool_consts = sem("pool_consts")
        blank = sem("blank")
        late_ramps = sem("late_ramps")
        eps_ready = sem("eps_ready")
        vec_multiplied = sem("vec_multiplied")
        vec_loaded = [sem(f"vec_loaded{k}") for k in range(NODE_RING)]
        vec_used = sem("vec_used")
        edge_score_ready = sem("edge_score_ready")
        weights_in = sem("weights_in")
        x_loaded = [sem(f"x_loaded{k}") for k in range(NODE_RING)]
        z_stored = [sem(f"z_stored{k}") for k in range(NODE_RING)]
        att_psum = sem("att_psum")
        wfx_ready = sem("wfx_ready")
        bn_done = sem("bn_done")
        stats_ready = sem("stats_ready")
        std_ready = sem("std_ready")
        rstd_ready = sem("rstd_ready")
        nmr_ready = sem("nmr_ready")
        hn_ready = sem("hn_ready")
        hnT_psum = sem("hnT_psum")
        hnT_ready = sem("hnT_ready")
        z_psum = sem("z_psum")
        z_ready = sem("z_ready")
        chain = sem("chain")
        dst_flat_in = sem("dst_flat_in")
        begun_ready = sem("begun_ready")
        path_psum = sem("path_psum")
        s2_kept = sem("s2_kept")
        s2T_psum = sem("s2T_psum")
        s2T_ready = sem("s2T_ready")
        s2_spread = sem("s2_spread")
        path_ready = sem("path_ready")
        src_loaded = [sem(f"src_loaded{k}") for k in range(LOADS)]
        dst_loaded = [sem(f"dst_loaded{k}") for k in range(LOADS)]
        z_gathered = [sem(f"z_gathered{k}") for k in range(LOADS)]
        dst_here_now = sem("dst_here_now")
        q_of_load = sem("q_of_load")
        q_ready = sem("q_ready")
        scores_psum = sem("scores_psum")
        masked = sem("masked")
        max_done = sem("max_done")
        plus_s2 = sem("plus_s2")
        leaky_done = sem("leaky_done")
        newmax_done = sem("newmax_done")
        bias_ready = sem("bias_ready")
        run_done = sem("run_done")
        exps_done = sem("exps_done")
        prob_ready = sem("prob_ready")
        probT_psum = sem("probT_psum")
        probT_ready = sem("probT_ready")
        sum_psum = sem("sum_psum")
        acc_done = sem("acc_done")
        steps_over = sem("steps_over")
        den_ready = sem("den_ready")
        hn1_ready = sem("hn1_ready")
        idle_ready = sem("idle_ready")
        xhn_ready = sem("xhn_ready")
        hn1T_psum = sem("hn1T_psum")
        hn1T_ready = sem("hn1T_ready")
        hs_psum = sem("hs_psum")
        with_hs = sem("with_hs")
        or_idle = sem("or_idle")
        x2_ready = sem("x2_ready")
        bn2_done = sem("bn2_done")
        stats2_ready = sem("stats2_ready")
        std2_ready = sem("std2_ready")
        rstd2_ready = sem("rstd2_ready")
        norm2_ready = sem("norm2_ready")
        hn2_ready = sem("hn2_ready")
        hn2T_psum = sem("hn2T_psum")
        hn2T_ready = sem("hn2T_ready")
        logit_psum = sem("logit_psum")
        logit_ready = sem("logit_ready")
        x2_stored = [sem(f"x2_stored{k}") for k in range(NODE_RING)]
        hn2_stored = [sem(f"hn2_stored{k}") for k in range(NODE_RING)]
        dump_stored = sem("dump_stored")
        shifted = sem("shifted")
        exp_ready = sem("exp_ready")
        gates_ready = sem("gates_ready")
        gates_stored = sem("gates_stored")
        choice_ready = sem("choice_ready")
        rank_psum = sem("rank_psum")
        onehot_ready = sem("onehot_ready")
        token_psum = sem("token_psum")
        slots_ready = sem("slots_ready")
        experts_in = [sem(f"experts_in{k}") for k in range(RAW)]
        raw_in = sem("raw_in")
        hi_split = sem("hi_split")
        lo_split = [sem(f"lo_split{p}") for p in range(2)]
        finish_over = sem("finish_over")
        ix_ready = sem("ix_ready")
        row_gathered = [sem(f"row_gathered{k}") for k in range(RING)]
        xT_psum = sem("xT_psum")
        xT_ready = sem("xT_ready")
        xT_lo_ready = sem("xT_lo_ready")
        up_a_psum = sem("up_a_psum")
        up_b_psum = sem("up_b_psum")
        silu_a = sem("silu_a")
        silu_b = sem("silu_b")
        hid_a_ready = sem("hid_a_ready")
        hid_b_ready = sem("hid_b_ready")
        hidT_psum = sem("hidT_psum")
        hidT_hi_ready = sem("hidT_hi_ready")
        hidT_lo_ready = sem("hidT_lo_ready")
        y_psum = sem("y_psum")
        y_ready = sem("y_ready")
        y_added = sem("y_added")
        passed = {str(eng.engine): sem(f"passed{n}") for n, eng in enumerate((nc.vector, nc.gpsimd))}
        block = ctx.enter_context(nc.Block())

        def run(eng, total, ring, peel, stages):
            def turn(r, k):
                for lag, stage in stages:
                    q, kk = divmod(k - lag, ring)
                    t = r * ring + (k - lag)
                    if isinstance(t, int) and not 0 <= t < total:
                        continue
                    stage(t, kk, r + q)
            for r in range(peel):
                for k in range(ring):
                    turn(r, k)
            with eng.Fori(peel, total // ring) as r:
                for k in range(ring):
                    turn(r, k)
            for k in range(max(lag for lag, _ in stages)):
                turn(total // ring, k)

        def at_least(t, n):
            return not isinstance(t, int) or t >= n

        def bank_back(k):
            return 1 if k == 0 else 2

        def held(eng):
            eng.sem_inc(passed[str(eng.engine)], 1)

        def cols(t, n, width=None):
            return bass.ds(t * n, n if width is None else width)

        class Sorted:
            total = PATH
            loads = GROUPS

            def load_of(self, eng, s):
                return eng.value_load(path_i[0:1, bass.ds(s, 1)], min_val=0, max_val=GROUPS - 1)

            def group(self, n):
                return n

            def tile(self, eng, s):
                return eng.value_load(path_j[0:1, bass.ds(s, 1)], min_val=0, max_val=TILES - 1)

            def mask_and_sum(self, eng, s):
                word = eng.value_load(turn_word[0:1, bass.ds(s, 1)], min_val=0, max_val=256 * TILES - 1)
                return eng.snap(word % 256), eng.snap(word // 256)

            def node(self, s):
                return step_node[:, bass.ds(s, 1)]

            def terms(self, s):
                return step_terms_flat[:, bass.ds(s * 3, 3)]

            def old_max(self, s):
                return step_terms_flat[:, bass.ds(s * 3 + 2, 1)]

            def keep_max(self, s, new):
                return nc.vector.tensor_tensor(self.old_max(s + 1), new, self.old_max(s + 1), ALU.add)

            def steps_until(self, eng, n):
                return eng.value_load(path_next[0:1, bass.ds(n, 1)], min_val=1, max_val=PATH)

        class Unsorted:
            total = PAIRS
            loads = PAIRS

            def load_of(self, eng, s):
                return s

            def group(self, n):
                return n % GROUPS

            def tile(self, eng, s):
                return s // GROUPS

            def mask_and_sum(self, eng, s):
                return self.load_of(eng, s), self.tile(eng, s - SUM_LAG)

            def node(self, s):
                return node_id[:, bass.ds(s // GROUPS, 1)]

            def terms(self, s):
                return scal[:, bass.ds(s // GROUPS * 3, 3)]

            def old_max(self, s):
                return scal[:, bass.ds(s // GROUPS * 3 + 2, 1)]

            def keep_max(self, s, new):
                held(nc.vector)
                return nc.vector.tensor_copy(self.old_max(s), new)

            def steps_until(self, eng, n):
                return n + 1

        def raw(e, piece):
            a, b = PIECES[piece]
            return Wf[:, bass.ds((e % RAW) * WE + a, b - a)]

        def split(e, part, piece):
            a, b = PIECES[piece]
            return split_w[:, bass.ds((e % 2) * (2 * WE) + (part * WE + a), b - a)]

        def split_hi(eng, e):
            for piece in range(2):
                nc.scalar.activation(split(e, 0, piece), raw(e, piece), ACT.Copy).then_inc(hi_split, 1)

        def split_lo(eng, v, e, piece):
            eng.wait_ge(hi_split, 2 * e + (1 + piece))
            if not isinstance(e, int):
                held(eng)
            v.tensor_tensor(split(e, 1, piece), raw(e, piece), split(e, 0, piece).bitcast(fp32), ALU.subtract)\
                .then_inc(lo_split[piece], 1)

        def at_new_expert(eng, t, work):
            if isinstance(t, int) and t == 0:
                return
            e = eng.value_load(split_next[0:1, bass.ds(t, 1)], min_val=0, max_val=E - 1)
            with eng.If(e > 0):
                eng.wait_ge(y_psum, t)
                work(e)

        def once(eng, value):
            return value if isinstance(value, int) else eng.snap(value)

        def branch(eng, steps):
            eng.wait_ge(path_ready, 1)
            falls_at = eng.value_load(flag[0:1, 0:1], min_val=0, max_val=1)
            with eng.If(falls_at == 0):
                steps(Sorted())
            with eng.Else():
                steps(Unsorted())
            eng.sem_inc(steps_over, 1)
            eng.wait_ge(steps_over, 5)

        @block.sync
        def _(sp):
            flat = dst.rearrange("g e -> (g e)")
            sp.dma_start(dst_here, flat[0:P * QE].rearrange("(p q) -> p q", q=QE)).then_inc(dst_flat_in, 16)
            sp.dma_start(dst_next, flat[1:P * QE + 1].rearrange("(p q) -> p q", q=QE)).then_inc(dst_flat_in, 16)
            sp.dma_start(last_dst, dst_last).then_inc(dst_flat_in, 16)
            sp.dma_start(wf_nat, w_func.rearrange("(k p) c -> p k c", p=P)).then_inc(weights_in, 16)
            sp.dma_start(wfx[:, :, 0:C], w_func_t.rearrange("(k p) c -> p k c", p=P))\
                .then_inc(weights_in, 16)
            sp.dma_start(att_n[:, :, :], att_nodes.rearrange("(k p) c -> p k c", p=P))\
                .then_inc(weights_in, 16)
            for k in range(NODE_RING):
                sp.dma_start(x_in[:, k, :], x[cols(k, P), :]).then_inc(x_loaded[k], 16)
            sp.dma_start(wself_sb[:, :, :], w_self_t.rearrange("(k p) c -> p k c", p=P))\
                .then_inc(weights_in, 16)
            sp.dma_start(router_sb[:, :, :], router.rearrange("(k p) c -> p k c", p=P))\
                .then_inc(weights_in, 16)
            sp.dma_start(att_e[:, :], att_edge.to_broadcast([P, EF])).then_inc(weights_in, 16)

            def vectors_load(t, k, r):
                if at_least(t, NODE_RING):
                    sp.wait_ge(vec_multiplied, t - NODE_RING + 1)
                sp.dma_start(vec_in[:, k, :], wt[bass.ds(t, 1), :, :].rearrange("b p e -> p (b e)"))\
                    .then_inc(vec_loaded[k], 16)

            def x_load(t, k, r):
                if at_least(t, NODE_RING):
                    sp.wait_ge(hn_ready, t - NODE_RING + 1)
                    sp.dma_start(x_in[:, k, :], x[cols(t, P), :]).then_inc(x_loaded[k], 16)

            def z_store(t, k, r):
                sp.wait_ge(z_ready, t + 1)
                sp.dma_start(ztab[cols(t, P), :], z_out[:, k, :]).then_inc(z_stored[k], 16)

            run(sp, TILES, NODE_RING, 2, [(0, x_load), (0, vectors_load), (6, z_store)])
            vectors_load(TILES, 0, TILES // NODE_RING)
            sp.wait_ge(pool_consts, 8)
            sp.dma_start(out[DUMP:OUT_ROWS, :], zero_rows[:, :]).then_inc(dump_stored, 16)

            sp.wait_ge(edge_score_ready, 1)

            def steps(way):
                def load(n, k, r):
                    g = way.group(n)
                    if at_least(n, LOADS):
                        sp.wait_ge(z_gathered[k], 16 * KG * r)
                    sp.dma_start(src_in[:, k, :], src[bass.ds(g, 1), :, :].rearrange("g p k -> p (g k)"))\
                        .then_inc(src_loaded[k], 16)
                    if at_least(n, LOADS):
                        until = way.steps_until(sp, n - LOADS)
                        sp.wait_ge(masked, until)
                    sp.dma_start(dst_in[:, k * G:(k + 1) * G], dst[bass.ds(g, 1), :].to_broadcast([P, G]))\
                        .then_inc(dst_loaded[k], 16)
                    if isinstance(n, int) and n in EXPERTS_AFTER:
                        e = EXPERTS_AFTER.index(n)
                        sp.dma_start(W[:, e, :], experts[e, :, :]).then_inc(experts_in[e % RAW], 16)

                def loaded(n, k, r):
                    sp.wait_ge(dst_loaded[k], 16 * (r + 1))
                    sp.sem_inc(dst_here_now, 1)
                run(sp, way.loads, LOADS, 2, [(0, load), (2, loaded)])
            branch(sp, steps)

            for e in range(RAW):
                sp.wait_ge(experts_in[e], 16)
                sp.sem_inc(raw_in, 1)

            def x_load_again(t, k, r):
                if at_least(t, NODE_RING):
                    sp.wait_ge(xhn_ready, t - NODE_RING + 1)
                    sp.wait_ge(hn1_ready, t - NODE_RING + 1)
                sp.dma_start(x_in[:, k, :], x[cols(t, P), :]).then_inc(x_loaded[k], 16)

            def x2_store(t, k, r):
                sp.wait_ge(x2_ready, t + 1)
                sp.dma_start(out[cols(t, P), :], x2[:, k, :]).then_inc(x2_stored[k], 16)

            def hn2_store(t, k, r):
                sp.wait_ge(hn2_ready, t + 1)
                sp.dma_start(ttab[cols(t, P), 0:C], hn[:, k, :]).then_inc(hn2_stored[k], 16)

            run(sp, TILES, NODE_RING, 3, [(0, x_load_again), (5, x2_store), (8, hn2_store)])
            sp.wait_ge(logit_ready, TILES)
            for k in range(NODE_RING):
                sp.wait_ge(x2_stored[k], 16 * (TILES // NODE_RING))
                sp.wait_ge(hn2_stored[k], 16 * (TILES // NODE_RING))
            sp.sem_inc(finish_over, 1)
            sp.wait_ge(gates_ready, 1)
            sp.dma_start(ttab[:, C:TR].rearrange("(t p) e -> p t e", p=P), gates).then_inc(gates_stored, 16)
            sp.wait_ge(gates_stored, 16)
            for e in range(RAW, E):
                for piece in range(2):
                    sp.wait_ge(lo_split[piece], e + 1 - RAW)
                sp.dma_start(W[:, e % RAW, :], experts[e, :, :]).then_inc(experts_in[e % RAW], 16)
                sp.wait_ge(experts_in[e % RAW], 16 * (e // RAW + 1))
                sp.sem_inc(raw_in, 1)
            sp.wait_ge(dump_stored, 16)
            sp.wait_ge(y_added, 16 * SLOTS)

        @block.gpsimd
        def _(pool):
            nc.gpsimd.memset(ident[:, :], 0.0).then_inc(blank, 1)
            nc.gpsimd.memset(before[:, :], 1.0).then_inc(blank, 1)
            nc.gpsimd.memset(ones[:, :], 1.0).then_inc(pool_consts, 1)
            pool.wait_ge(blank, 2)
            nc.gpsimd.affine_select(out=ident[:, :], in_=ident[:, :], compare_op=ALU.not_equal, fill=1.0,
                                    base=0, pattern=[[-1, P]], channel_multiplier=1).then_inc(pool_consts, 1)
            nc.gpsimd.affine_select(out=before[:, :], in_=before[:, :], compare_op=ALU.is_gt, fill=0.0,
                                    base=0, pattern=[[1, P]], channel_multiplier=-1).then_inc(pool_consts, 1)
            nc.gpsimd.iota(io_i, pattern=[[1, P]], base=0, channel_multiplier=0).then_inc(pool_consts, 1)
            nc.gpsimd.iota(io_n, pattern=[[P, TILES]], base=0, channel_multiplier=1).then_inc(pool_consts, 1)
            nc.gpsimd.iota(io_t, pattern=[[P, TILES]], base=P, channel_multiplier=0).then_inc(pool_consts, 1)
            nc.gpsimd.iota(io_s, pattern=[[1, PATH]], base=0, channel_multiplier=0).then_inc(pool_consts, 1)
            nc.gpsimd.memset(zero_rows[:, :], 0.0).then_inc(pool_consts, 1)
            pool.wait_ge(weights_in, 16 * 6)

            def products(t, k, r):
                pool.wait_ge(vec_loaded[k], 16 * (r + 1))
                if at_least(t, 2):
                    pool.wait_ge(vec_used, t - 1)
                half = bass.ds((t % 2) * (AT_ONCE * EF), AT_ONCE * EF)
                nc.gpsimd.tensor_tensor(vec_prod_flat[:, half].rearrange("p (c f) -> p c f", f=EF),
                                        vec_in[:, k, :].rearrange("p (c f) -> p c f", f=EF),
                                        att_e[:, :].unsqueeze(1).to_broadcast([P, AT_ONCE, EF]), ALU.mult)\
                    .then_inc(vec_multiplied, 1)
            run(pool, TILES, NODE_RING, 2, [(0, products)])
            products(TILES, 0, TILES // NODE_RING)

            pool.wait_ge(edge_score_ready, 1)
            for k in range(NODE_RING):
                pool.wait_ge(z_stored[k], 16 * (TILES // NODE_RING))

            def steps(way):
                def gather(n, k, r):
                    if at_least(n, LOADS):
                        until = way.steps_until(pool, n - LOADS)
                        pool.wait_ge(sum_psum, until)
                    pool.wait_ge(src_loaded[k], 16 * (r + 1))
                    held(pool)
                    for c in range(KG):
                        nc.gpsimd.indirect_dma_start(
                            out=zg[:, k * KG + c, :], out_offset=None, in_=ztab,
                            in_offset=bass.IndirectOffsetOnAxis(ap=src_in[:, k, c:c + 1], axis=0))\
                            .then_inc(z_gathered[k], 16)

                def add_s1(n, k, r):
                    pool.wait_ge(z_gathered[k], 16 * KG * (r + 1))
                    nc.gpsimd.tensor_tensor(q[:, k * KG:(k + 1) * KG], edge_score[:, cols(way.group(n), KG)],
                                            zg[:, k * KG:(k + 1) * KG, C], ALU.add).then_inc(q_of_load, 1)
                run(pool, way.loads, LOADS, 2, [(0, gather), (1, add_s1)])
            branch(pool, steps)

            def x_plus_hn(t, k, r):
                pool.wait_ge(hn1_ready, t + 1)
                if at_least(t, NODE_RING):
                    pool.wait_ge(x2_ready, t - NODE_RING + 1)
                nc.gpsimd.tensor_tensor(x_hn[:, k, :], x_in[:, k, :], hn1[:, k, :], ALU.add)\
                    .then_inc(xhn_ready, 1)

            run(pool, TILES, NODE_RING, 1, [(0, x_plus_hn)])
            pool.wait_ge(x2_ready, TILES)
            nc.gpsimd.iota(io_slot, pattern=[[1, SLOTS]], base=0, channel_multiplier=0).then_inc(late_ramps, 1)
            nc.gpsimd.iota(io_p, pattern=[[0, 1]], base=1, channel_multiplier=1).then_inc(late_ramps, 1)
            nc.gpsimd.iota(io_e, pattern=[[1, E]], base=-E, channel_multiplier=0).then_inc(late_ramps, 1)

            pool.wait_ge(finish_over, 1)
            for e in range(2):
                for piece in range(2):
                    split_lo(pool, nc.gpsimd, e, piece)
            pool.wait_ge(gates_stored, 16)
            pool.wait_ge(dump_stored, 16)
            for k in range(NODE_RING):
                pool.wait_ge(x2_stored[k], 16 * (TILES // NODE_RING))
                pool.wait_ge(hn2_stored[k], 16 * (TILES // NODE_RING))
            pool.wait_ge(slots_ready, 1)

            def add(t, k, r):
                pool.wait_ge(y_ready, t + 1)
                held(pool)
                nc.gpsimd.indirect_dma_start(
                    out=out, out_offset=bass.IndirectOffsetOnAxis(ap=row_ix[:, k, 1:2], axis=0),
                    in_=y_out[:, k % 2, :], in_offset=None, compute_op=ALU.add).then_inc(y_added, 16)
                pool.wait_ge(y_added, 16 * (t + 1))

            def gather_rows(t, k, r):
                nc.gpsimd.tensor_copy(row_ix[:, k, :], slot_rows[:, cols(t, 2)]).then_inc(ix_ready, 1)
                pool.wait_ge(ix_ready, t + 1)
                held(pool)
                nc.gpsimd.indirect_dma_start(
                    out=xg[:, k, :], out_offset=None, in_=ttab,
                    in_offset=bass.IndirectOffsetOnAxis(ap=row_ix[:, k, 0:1], axis=0))\
                    .then_inc(row_gathered[k], 16)

            def lo_piece(t, k, r):
                at_new_expert(pool, t, lambda e: split_lo(pool, nc.gpsimd, e, 1))

            run(pool, SLOTS, RING, 1, [(4, add), (0, gather_rows), (3, lo_piece)])

        @block.scalar
        def _(act):
            act.wait_ge(eps_ready, 1)

            def std(t, k, r):
                act.wait_ge(stats_ready, t + 1)
                nc.scalar.activation(norm2[:, k, 0:1], mv2[:, k, 1:2], ACT.Sqrt, bias=eps[:, 0:1])\
                    .then_inc(std_ready, 1)

            def hn_first(t, k, r):
                act.wait_ge(nmr_ready, t + 1)
                if at_least(t, NODE_RING):
                    act.wait_ge(hnT_psum, t - NODE_RING + 1)
                nc.scalar.activation(hn[:, k, :], x_in[:, k, :], ACT.Identity, bias=nmr[:, bass.ds(t, 1)],
                                     scale=rstd[:, bass.ds(t, 1)]).then_inc(hn_ready, 1)

            def hnT_copy(t, k, r):
                act.wait_ge(hnT_psum, t + 1)
                if at_least(t, NODE_RING):
                    act.wait_ge(z_psum, t - NODE_RING + 1)
                nc.scalar.activation(hnT[:, k, :], ps[k % 2][:, 0:C], ACT.Copy).then_inc(hnT_ready, 1)

            run(act, TILES, NODE_RING, 2, [(2, hnT_copy), (0, std), (1, hn_first)])

            def steps(way):
                def q_copy(s, k, r):
                    n = once(act, way.load_of(act, s))
                    if at_least(s, RING):
                        act.wait_ge(scores_psum, s - RING + 1)
                    act.wait_ge(q_of_load, n + 1)
                    nc.scalar.activation(q_step[:, k, :], q[:, cols(n % LOADS, KG)], ACT.Copy).then_inc(q_ready, 1)

                def exps(s, k, r):
                    b = k % 2
                    act.wait_ge(bias_ready, s + 1)
                    if at_least(s, 2):
                        act.wait_ge(prob_ready, s - 1)
                    nc.scalar.activation(e_hi[:, b, :], score[:, b, :], ACT.Exp, bias=bias[:, b, 0:1],
                                         scale=1.0).then_inc(exps_done, 1)
                    nc.scalar.activation(e_lo[:, b, :], score[:, b, :], ACT.Exp, bias=bias[:, b, 1:2],
                                         scale=SLOPE).then_inc(exps_done, 1)
                    if at_least(s, RING):
                        act.wait_ge(acc_done, s - RING + 1)
                    nc.scalar.activation(corr[:, k:k + 1], bias[:, b, 2:3], ACT.Exp).then_inc(exps_done, 1)

                def probT_copy(s, k, r):
                    act.wait_ge(probT_psum, s + 1)
                    if at_least(s, 2):
                        act.wait_ge(sum_psum, s - 1)
                    nc.scalar.activation(probT[:, k % 2, :], ps[2 + k % 2][:, 0:G], ACT.Copy)\
                        .then_inc(probT_ready, 1)
                run(act, way.total, RING, 2, [(0, q_copy), (2, exps), (3, probT_copy)])
            branch(act, steps)

            act.wait_ge(den_ready, 1)

            def hn_again(t, k, r):
                act.wait_ge(x_loaded[k], 16 * (r + 1 + TILES // NODE_RING))
                if at_least(t, NODE_RING):
                    act.wait_ge(xhn_ready, t - NODE_RING + 1)
                    act.wait_ge(hn1T_psum, t - NODE_RING + 1)
                nc.scalar.activation(hn1[:, k, :], x_in[:, k, :], ACT.Identity, bias=nmr[:, bass.ds(t, 1)],
                                     scale=rstd[:, bass.ds(t, 1)]).then_inc(hn1_ready, 1)
                act.wait_ge(hn1_ready, t + 1)
                if at_least(t, NODE_RING):
                    act.wait_ge(or_idle, t - NODE_RING + 1)
                nc.scalar.activation(idle[:, k, :], hn1[:, k, :], ACT.Copy,
                                     scale=no_edge[:, bass.ds(t, 1)]).then_inc(idle_ready, 1)

            def hn1T_copy(t, k, r):
                act.wait_ge(hn1T_psum, t + 1)
                if at_least(t, NODE_RING):
                    act.wait_ge(hs_psum, t - NODE_RING + 1)
                nc.scalar.activation(hnT[:, k, :], ps[k % 2][:, 0:C], ACT.Copy).then_inc(hn1T_ready, 1)

            def std2(t, k, r):
                act.wait_ge(stats2_ready, t + 1)
                nc.scalar.activation(norm2[:, k, 0:1], mv2[:, k, 1:2], ACT.Sqrt, bias=eps[:, 0:1])\
                    .then_inc(std2_ready, 1)

            def hn_second(t, k, r):
                act.wait_ge(norm2_ready, t + 1)
                if at_least(t, NODE_RING):
                    act.wait_ge(hn2_stored[k], 16 * r)
                    act.wait_ge(hn2T_psum, t - NODE_RING + 1)
                nc.scalar.activation(hn[:, k, :], x2[:, k, :], ACT.Identity, bias=norm2[:, k, 2:3],
                                     scale=norm2[:, k, 1:2]).then_inc(hn2_ready, 1)

            def hn2T_copy(t, k, r):
                act.wait_ge(hn2T_psum, t + 1)
                if at_least(t, NODE_RING):
                    act.wait_ge(logit_psum, t - NODE_RING + 1)
                nc.scalar.activation(hn2T[:, k, :], ps[4 + k % 2][:, 0:C], ACT.Copy).then_inc(hn2T_ready, 1)

            run(act, TILES, NODE_RING, 3, [(1, hn1T_copy), (8, hn2T_copy), (0, hn_again), (7, hn_second),
                                           (5, std2)])

            act.wait_ge(shifted, 1)
            nc.scalar.activation(ex, probs, ACT.Exp).then_inc(exp_ready, 1)

            act.wait_ge(finish_over, 1)
            for e in range(2):
                act.wait_ge(raw_in, e + 1)
                split_hi(act, e)
            act.wait_ge(slots_ready, 1)

            def hi_parts(t, k, r):
                def work(e):
                    act.wait_ge(raw_in, e + 1)
                    split_hi(act, e)
                at_new_expert(act, t, work)

            def xT_copy(t, k, r):
                act.wait_ge(xT_psum, t + 1)
                if at_least(t, 2):
                    act.wait_ge(up_b_psum, t - 1)
                nc.scalar.activation(xT_hi[:, (k % 2) * C:(k % 2 + 1) * C], ps[4][:, 0:C], ACT.Copy)\
                    .then_inc(xT_ready, 1)

            def silu_first(t, k, r):
                if at_least(t, 1):
                    act.wait_ge(hid_a_ready, t)
                act.wait_ge(up_a_psum, t + 1)
                nc.scalar.activation(s_act[:, 0:HA], ps[0][:, 0:HA], ACT.Silu).then_inc(silu_a, 1)

            def hidT_copy(t, k, r):
                act.wait_ge(hidT_psum, t + 1)
                if at_least(t, 1):
                    act.wait_ge(y_psum, t)
                n = HC[-1][1]
                nc.scalar.activation(hidT_hi[:, 0:4 * P], ps[6][:, 0:4 * P], ACT.Copy).then_inc(hidT_hi_ready, 1)
                nc.scalar.activation(hidT_hi[:, 4 * P:5 * P], ps[7][:, 0:P], ACT.Copy).then_inc(hidT_hi_ready, 1)
                nc.scalar.activation(hidT_hi[0:n, 5 * P:6 * P], ps[7][0:n, P:2 * P], ACT.Copy)\
                    .then_inc(hidT_hi_ready, 1)

            def silu_second(t, k, r):
                if at_least(t, 1):
                    act.wait_ge(hid_b_ready, t)
                act.wait_ge(up_b_psum, t + 1)
                nc.scalar.activation(s_act[:, HA:H], ps[2][:, 0:HB], ACT.Silu).then_inc(silu_b, 1)

            run(act, SLOTS, RING, 1, [(2, hi_parts), (1, silu_first), (2, hidT_copy), (0, xT_copy), (1, silu_second)])

        @block.tensor
        def _(pe):
            mm, tr = nc.tensor.matmul, nc.tensor.transpose
            pe.wait_ge(pool_consts, 2)
            pe.wait_ge(begun_ready, 1)
            mm(ps[5][:, 0:PATH], ones[0:GROUPS - 1, 0:P], begun[0:GROUPS - 1, :], start=True, stop=True)
            mm(ps[5][0:1, PATH:PATH + P], start, ident[:, :], start=True, stop=True)
            mm(ps[6][0:1, 0:1], fell, ones[:, 0:1], start=True, stop=True).then_inc(path_psum, 1)
            pe.wait_ge(weights_in, 16 * 6)
            for m in range(KC):
                for k in range(KC):
                    last = mm(ps[7][:, 2 * m:2 * m + 2], wf_nat[:, k, m * P:(m + 1) * P], att_n[:, k, :],
                              start=(k == 0), stop=(k == KC - 1))
            last.then_inc(att_psum, 1)
            pe.wait_ge(wfx_ready, 1)

            def transposed(bank, rows_ap, chunks=KC):
                for c in range(chunks):
                    last = tr(bank[:, c * P:(c + 1) * P], rows_ap[:, c * P:(c + 1) * P], ident[:, :])
                return last

            def hn_T(t, k, r):
                pe.wait_ge(hn_ready, t + 1)
                if at_least(t, 1):
                    pe.wait_ge(hnT_ready, t + 1 - bank_back(k) if at_least(t, 2) else t)
                transposed(ps[k % 2], hn[:, k, :]).then_inc(hnT_psum, 1)

            def z_of(t, k, r):
                pe.wait_ge(hnT_ready, t + 1)
                if at_least(t, 2):
                    pe.wait_ge(z_ready, t + 1 - bank_back(k))
                for c in range(KC):
                    last = mm(ps[2 + k % 2][:, 0:ZR], hnT[:, k, c * P:(c + 1) * P], wfx[:, c, :],
                              start=(c == 0), stop=(c == KC - 1))
                last.then_inc(z_psum, 1)

            run(pe, TILES, NODE_RING, 2, [(0, hn_T), (1, z_of)])
            pe.wait_ge(s2_kept, 1)
            tr(ps[5][0:TILES, 0:P], scal_by_tile[:, :, 0], ident[:, :]).then_inc(s2T_psum, 1)
            pe.wait_ge(s2T_ready, 1)
            mm(ps[6][:, 0:PATH], s2T[0:TILES, :], tile_hot[0:TILES, :], start=True, stop=True)\
                .then_inc(s2_spread, 1)

            def steps(way):
                def scores(s, k, r):
                    pe.wait_ge(q_ready, s + 1)
                    if at_least(s, 2):
                        pe.wait_ge(max_done, s - 1)
                    for c in range(KG):
                        last = mm(ps[k % 2][:, c * P:(c + 1) * P], q_step[:, k, c:c + 1].to_broadcast([P, P]),
                                  ident[:, :], start=True, stop=True)
                    last.then_inc(scores_psum, 1)

                def prob_T(s, k, r):
                    b = k % 2
                    pe.wait_ge(prob_ready, s + 1)
                    if at_least(s, 2):
                        pe.wait_ge(probT_ready, s - 1)
                    transposed(ps[2 + b], prob[:, b, :], KG).then_inc(probT_psum, 1)

                def weighted(s, k, r):
                    b = k % 2
                    at = once(pe, (way.load_of(pe, s) % LOADS) * (KG * ZR))
                    pe.wait_ge(probT_ready, s + 1)
                    if at_least(s, 2):
                        pe.wait_ge(acc_done, s - 1)
                    for c in range(KG):
                        last = mm(ps[4 + b][:, 0:ZR], probT[:, b, c * P:(c + 1) * P],
                                  zg_flat[:, bass.ds(at + c * ZR, ZR)], start=(c == 0), stop=(c == KG - 1))
                    last.then_inc(sum_psum, 1)
                run(pe, way.total, RING, 2, [(0, scores), (3, weighted), (2, prob_T)])
            branch(pe, steps)

            def hn1_T(t, k, r):
                pe.wait_ge(hn1_ready, t + 1)
                if at_least(t, 1):
                    pe.wait_ge(hn1T_ready, t + 1 - bank_back(k) if at_least(t, 2) else t)
                transposed(ps[k % 2], hn1[:, k, :]).then_inc(hn1T_psum, 1)

            def self_part(t, k, r):
                pe.wait_ge(hn1T_ready, t + 1)
                if at_least(t, 2):
                    pe.wait_ge(with_hs, t + 1 - bank_back(k))
                for c in range(KC):
                    last = mm(ps[2 + k % 2][:, 0:C], hnT[:, k, c * P:(c + 1) * P], wself_sb[:, c, :],
                              start=(c == 0), stop=(c == KC - 1))
                last.then_inc(hs_psum, 1)

            def hn2_T(t, k, r):
                pe.wait_ge(hn2_ready, t + 1)
                if at_least(t, 1):
                    pe.wait_ge(hn2T_ready, t + 1 - bank_back(k) if at_least(t, 2) else t)
                transposed(ps[4 + k % 2], hn[:, k, :]).then_inc(hn2T_psum, 1)

            def logits_of(t, k, r):
                pe.wait_ge(hn2T_ready, t + 1)
                if at_least(t, 2):
                    pe.wait_ge(logit_ready, t + 1 - bank_back(k))
                for c in range(KC):
                    last = mm(ps[6 + k % 2][:, 0:E], hn2T[:, k, c * P:(c + 1) * P], router_sb[:, c, :],
                              start=(c == 0), stop=(c == KC - 1))
                last.then_inc(logit_psum, 1)

            run(pe, TILES, NODE_RING, 3, [(1, self_part), (0, hn1_T), (9, logits_of), (7, hn2_T)])

            pe.wait_ge(choice_ready, 1)
            pe.wait_ge(pool_consts, 3)
            chosen = both.rearrange("p t e -> p e t")
            mm(ps[0][:, 0:RE], before[:, :], chosen, start=True, stop=True)
            mm(ps[1][:, 0:RE], ones[:, 0:P], chosen, start=True, stop=True).then_inc(rank_psum, 1)
            pe.wait_ge(onehot_ready, 1)
            for q in range(S2):
                last = mm(ps[2][:, 0:2 * SLOTS], ohr[:, q, :], moving[:, q, :], start=(q == 0),
                          stop=(q == S2 - 1))
            last.then_inc(token_psum, 1)

            pe.wait_ge(slots_ready, 1)
            def expert(t):
                return pe.value_load(expert_of[0:1, bass.ds(t, 1)], min_val=0, max_val=E - 1)

            def tokens_T(t, k, r):
                pe.wait_ge(row_gathered[k], 16 * (r + 1))
                if at_least(t, 1):
                    pe.wait_ge(xT_lo_ready, t)
                transposed(ps[4], xg[:, k, 0:C]).then_inc(xT_psum, 1)

            def up(e, k, lo, n, banks):
                at = once(pe, (e % 2) * (2 * WE) + lo)
                for bank, w in zip(banks, (W1_AT, W3_AT)):
                    passes = [(x, part * WE, c) for x, part in ((xT_hi, 0), (xT_hi, 1), (xT_lo, 0))
                              for c in range(KC)]
                    for i, (x, part, c) in enumerate(passes):
                        last = mm(bank[:, 0:n], x[:, (k % 2 * KC + c) * P:(k % 2 * KC + c + 1) * P],
                                  split_w[:, bass.ds(at + (part + w + c * H), n)], start=(i == 0),
                                  stop=(i == len(passes) - 1))
                return last

            tile_expert = []

            def up_first(t, k, r):
                e = once(pe, expert(t))
                tile_expert.append(e)
                pe.wait_ge(xT_lo_ready, t + 1)
                for piece in range(2):
                    pe.wait_ge(lo_split[piece], e + 1)
                if at_least(t, 1):
                    pe.wait_ge(hid_a_ready, t)
                up(e, k, 0, HA, (ps[0], ps[1])).then_inc(up_a_psum, 1)

            def up_second(t, k, r):
                e = tile_expert.pop()
                if at_least(t, 1):
                    pe.wait_ge(hid_b_ready, t)
                up(e, k, HA, HB, (ps[2], ps[3])).then_inc(up_b_psum, 1)

            def hidden_T(t, k, r):
                pe.wait_ge(hid_a_ready, t + 1)
                pe.wait_ge(hid_b_ready, t + 1)
                if at_least(t, 1):
                    pe.wait_ge(hidT_lo_ready, t)
                for i, (a, n) in enumerate(HC):
                    last = tr(ps[6 + i // 4][0:n, (i % 4) * P:(i % 4 + 1) * P], hid[:, k % 2, a:a + n],
                              ident[:, :])
                last.then_inc(hidT_psum, 1)

            def down(t, k, r):
                at = once(pe, (expert(t) % 2) * (2 * WE) + W2_AT)
                pe.wait_ge(hidT_hi_ready, 3 * (t + 1))
                if at_least(t, 1):
                    pe.wait_ge(y_ready, t)
                passes = [(x, part * WE, i) for x, part in ((hidT_hi, 0), (hidT_hi, 1), (hidT_lo, 0))
                          for i in range(NH)]
                for q, (x, part, i) in enumerate(passes):
                    n = HC[i][1]
                    if q == 2 * NH:
                        pe.wait_ge(hidT_lo_ready, t + 1)
                    last = mm(ps[5][:, 0:C], x[0:n, i * P:(i + 1) * P], split_w[0:n, bass.ds(at + (part + i * C), C)],
                              start=(q == 0), stop=(q == len(passes) - 1))
                last.then_inc(y_psum, 1)

            run(pe, SLOTS, RING, 1, [(1, up_first), (2, hidden_T), (0, tokens_T), (1, up_second), (2, down)])

        @block.vector
        def _(dve):
            v = nc.vector
            count = [0]

            def link(ins):
                count[0] += 1
                ins.then_inc(chain, 1)
                dve.wait_ge(chain, count[0])

            v.memset(eps[:, :], EPS).then_inc(eps_ready, 1)
            link(v.memset(acc[:, :], 0.0))
            link(v.memset(z_out[:, :, C + 1:ZR], 1.0))
            dve.wait_ge(pool_consts, 7)
            v.tensor_copy(iota_row[:, :], io_i)
            v.tensor_copy(thr[:, :], io_t)
            v.tensor_copy(step_no, io_s)
            link(v.tensor_copy(node_id[:, :], io_n))
            link(v.tensor_scalar(valid[:, :], node_id[:, :], float(N), None, ALU.is_lt))
            dve.wait_ge(dst_flat_in, 48)
            v.tensor_tensor(falls, dst_here, dst_next, ALU.is_gt)
            link(v.tensor_copy(last_f, last_dst))
            v.tensor_reduce(fell, falls, AX.X, ALU.max)
            link(v.tensor_scalar(ge_thr[:, 0:TILES - 1], thr[:, 0:TILES - 1], last_f, None, ALU.is_le))
            link(v.tensor_reduce(start, ge_thr[:, 0:TILES - 1], AX.X, ALU.add))
            link(v.tensor_scalar(start, start, node_id[:, 0:1], 1.0, ALU.add, ALU.add))
            link(v.tensor_scalar(begun, step_no, start, None, ALU.is_ge))
            v.memset(tick[:, :], 0.0).then_inc(begun_ready, 1)
            dve.wait_ge(path_psum, 1)
            v.tensor_scalar(flag[0:1, :], ps[6][0:1, 0:1], 0.0, None, ALU.is_gt)
            v.tensor_copy(path_i[0:1, :], ps[5][0:1, 0:PATH])
            v.tensor_copy(path_next[0:1, :], ps[5][0:1, PATH:PATH + P])
            link(v.tensor_tensor(step_tile, step_no, ps[5][:, 0:PATH], ALU.subtract))
            v.tensor_copy(path_j[0:1, :], step_tile[0:1, :])
            v.memset(word_f[:, 0:SUM_LAG], 0.0)
            link(v.tensor_scalar(word_f[:, SUM_LAG:PATH], step_tile[:, 0:PATH - SUM_LAG], 256.0, None, ALU.mult))
            link(v.tensor_tensor(word_f, word_f, ps[5][:, 0:PATH], ALU.add))
            v.tensor_copy(turn_word[0:1, :], word_f[0:1, :])
            v.tensor_scalar(step_node, step_tile, float(P), node_id[:, 0:1], ALU.mult, ALU.add)
            v.tensor_scalar(tile_hot, step_tile, node_id[:, 0:1], None, ALU.is_equal)
            link(v.memset(step_terms_flat, NO_MAX))
            link(v.tensor_tensor(step_terms[:, 1:PATH, 2], step_tile[:, 1:PATH], step_tile[:, 0:PATH - 1],
                                 ALU.not_equal))
            link(v.tensor_scalar(step_terms[:, 1:PATH, 2], step_terms[:, 1:PATH, 2], NO_MAX, None, ALU.mult))
            v.memset(tick[:, :], 0.0).then_inc(path_ready, 1)
            dve.wait_ge(weights_in, 16 * 6)
            dve.wait_ge(att_psum, 1)
            for m in range(KC):
                last = v.tensor_copy(wfx[:, m, C:ZR], ps[7][:, 2 * m:2 * m + 2])
            last.then_inc(wfx_ready, 1)

            def norm(t, k, r):
                dve.wait_ge(x_loaded[k], 16 * (r + 1))
                v.bn_stats(st6[:, k, :], x_in[:, k, :]).then_inc(bn_done, 1)

            def mean_var(t, k, r):
                dve.wait_ge(bn_done, t + 1)
                held(dve)
                v.bn_aggr(mv2[:, k, :], st6[:, k, :]).then_inc(stats_ready, 1)

            def inv_std(t, k, r):
                dve.wait_ge(std_ready, t + 1)
                v.reciprocal(rstd[:, bass.ds(t, 1)], norm2[:, k, 0:1]).then_inc(rstd_ready, 1)

            def neg_mean(t, k, r):
                dve.wait_ge(rstd_ready, t + 1)
                v.scalar_tensor_tensor(nmr[:, bass.ds(t, 1)], mv2[:, k, 0:1], -1.0, rstd[:, bass.ds(t, 1)], ALU.mult,
                                       ALU.mult).then_inc(nmr_ready, 1)

            def z_copy(t, k, r):
                bank = ps[2 + k % 2]
                dve.wait_ge(z_psum, t + 1)
                if at_least(t, NODE_RING):
                    dve.wait_ge(z_stored[k], 16 * r)
                v.tensor_copy(z_out[:, k, 0:C + 1], bank[:, 0:C + 1])
                v.tensor_copy(scal[:, cols(t, 3, 1)], bank[:, C + 1:ZR])
                v.tensor_scalar(scal[:, bass.ds(t * 3 + 1, 1)], bank[:, C + 1:ZR], SLOPE, None, ALU.mult)\
                    .then_inc(z_ready, 1)

            def edge_scores(t, k, r):
                dve.wait_ge(vec_multiplied, t + 1)
                half = bass.ds((t % 2) * (AT_ONCE * EF), AT_ONCE * EF)
                v.tensor_reduce(edge_score[:, cols(t, AT_ONCE)],
                                vec_prod_flat[:, half].rearrange("p (c f) -> p c f", f=EF), AX.X, ALU.add)\
                    .then_inc(vec_used, 1)

            run(dve, TILES, NODE_RING, 2, [(0, norm), (1, inv_std), (0, mean_var), (1, neg_mean), (4, z_copy),
                                           (0, edge_scores)])
            dve.wait_ge(z_ready, TILES)
            v.memset(scal_by_tile[:, :, 2], NO_MAX).then_inc(s2_kept, 1)
            dve.wait_ge(s2T_psum, 1)
            v.tensor_copy(s2T[0:TILES, :], ps[5][0:TILES, 0:P]).then_inc(s2T_ready, 1)
            dve.wait_ge(s2_spread, 1)
            v.tensor_copy(step_terms[:, 0:PATH, 0], ps[6][:, 0:PATH])
            link(v.tensor_scalar(step_terms[:, 0:PATH, 1], ps[6][:, 0:PATH], SLOPE, None, ALU.mult))
            edge_scores(TILES, 0, TILES // NODE_RING)
            dve.wait_ge(vec_used, EDGE_LOADS)
            v.memset(tick[:, :], 0.0).then_inc(edge_score_ready, 1)

            def steps(way):
                sum_tile = []

                def mask_of(s, k, r):
                    if isinstance(s, int):
                        n = once(dve, way.load_of(dve, s))
                    else:
                        n, j = way.mask_and_sum(dve, s)
                        sum_tile.append(j)
                    dve.wait_ge(dst_here_now, n + 1)
                    v.tensor_scalar(mask[:, k % 2, :], dst_in[:, cols(n % LOADS, G)], way.node(s),
                                    MASKED, ALU.not_equal, ALU.mult).then_inc(masked, 1)

                def largest(s, k, r):
                    b = k % 2
                    dve.wait_ge(masked, s + 1)
                    dve.wait_ge(scores_psum, s + 1)
                    held(dve)
                    v.tensor_tensor_reduce(out=score[:, b, :], in0=ps[b][:, 0:G], in1=mask[:, b, :], scale=1.0,
                                           scalar=2 * MASKED, op0=ALU.add, op1=ALU.max,
                                           accum_out=small[:, k, 0:1]).then_inc(max_done, 1)

                def with_s2(s, k, r):
                    dve.wait_ge(max_done, s + 1)
                    v.tensor_scalar(small[:, k, 1:2], small[:, k, 0:1], way.terms(s)[:, 0:1], None, ALU.add)\
                        .then_inc(plus_s2, 1)

                def leaky(s, k, r):
                    dve.wait_ge(plus_s2, s + 1)
                    v.scalar_tensor_tensor(small[:, k, 2:3], small[:, k, 1:2], SLOPE, small[:, k, 1:2], ALU.mult,
                                           ALU.max).then_inc(leaky_done, 1)

                def new_max(s, k, r):
                    dve.wait_ge(leaky_done, s + 1)
                    if at_least(s, 1):
                        dve.wait_ge(run_done, s)
                    v.tensor_tensor(small[:, k, 3:4], small[:, k, 2:3], way.old_max(s), ALU.max)\
                        .then_inc(newmax_done, 1)
                    dve.wait_ge(newmax_done, s + 1)
                    v.tensor_scalar(bias[:, k % 2, :], way.terms(s), small[:, k, 3:4], None,
                                    ALU.subtract).then_inc(bias_ready, 1)

                def keep_max(s, k, r):
                    dve.wait_ge(bias_ready, s + 1)
                    way.keep_max(s, small[:, k, 3:4]).then_inc(run_done, 1)

                def probs_of(s, k, r):
                    b = k % 2
                    dve.wait_ge(exps_done, 3 * (s + 1))
                    v.tensor_tensor(prob[:, b, :], e_hi[:, b, :], e_lo[:, b, :], ALU.max)\
                        .then_inc(prob_ready, 1)

                def add_sum(s, k, r):
                    j = way.tile(dve, s) if isinstance(s, int) else sum_tile.pop()
                    dve.wait_ge(sum_psum, s + 1)
                    if at_least(s, 1):
                        dve.wait_ge(acc_done, s)
                    at = acc[:, cols(j, ZR)]
                    v.scalar_tensor_tensor(at, at, corr[:, k:k + 1], ps[4 + k % 2][:, 0:ZR], ALU.mult, ALU.add)\
                        .then_inc(acc_done, 1)
                run(dve, way.total, RING, 2, [(1, largest), (2, keep_max), (0, mask_of), (1, with_s2),
                                              (SUM_LAG, add_sum), (1, leaky), (2, probs_of), (1, new_max)])
                dve.wait_ge(acc_done, way.total)
            branch(dve, steps)

            den = acc[:, :].rearrange("p (t c) -> p t c", c=ZR)[:, :, C + 1]
            v.tensor_scalar(has_edge[:, :], den, 0.0, None, ALU.is_gt)
            v.tensor_scalar(no_edge[:, :], den, 0.0, None, ALU.is_le)
            link(v.tensor_scalar(inv_den[:, :], den, 1e-30, None, ALU.max))
            link(v.reciprocal(inv_den[:, :], inv_den[:, :]))
            v.memset(tick[:, :], 0.0).then_inc(den_ready, 1)

            def add_hs(t, k, r):
                a = acc[:, cols(t, ZR, C)]
                dve.wait_ge(hs_psum, t + 1)
                v.scalar_tensor_tensor(a, a, inv_den[:, bass.ds(t, 1)], ps[2 + k % 2][:, 0:C], ALU.mult, ALU.add)\
                    .then_inc(with_hs, 1)

            def where_edge(t, k, r):
                a = acc[:, cols(t, ZR, C)]
                dve.wait_ge(with_hs, t + 1)
                dve.wait_ge(idle_ready, t + 1)
                v.scalar_tensor_tensor(a, a, has_edge[:, bass.ds(t, 1)], idle[:, k, :], ALU.mult, ALU.add)\
                    .then_inc(or_idle, 1)

            def residual(t, k, r):
                a = acc[:, cols(t, ZR, C)]
                dve.wait_ge(or_idle, t + 1)
                dve.wait_ge(xhn_ready, t + 1)
                if at_least(t, NODE_RING):
                    dve.wait_ge(x2_stored[k], 16 * r)
                    dve.wait_ge(hn2_ready, t - NODE_RING + 1)
                v.scalar_tensor_tensor(x2[:, k, :], a, 0.0, x_hn[:, k, :], ALU.max, ALU.add).then_inc(x2_ready, 1)

            def stats2(t, k, r):
                dve.wait_ge(x2_ready, t + 1)
                v.bn_stats(st6[:, k, :], x2[:, k, :]).then_inc(bn2_done, 1)

            def mean_var2(t, k, r):
                dve.wait_ge(bn2_done, t + 1)
                held(dve)
                v.bn_aggr(mv2[:, k, :], st6[:, k, :]).then_inc(stats2_ready, 1)

            def inv_std2(t, k, r):
                dve.wait_ge(std2_ready, t + 1)
                v.reciprocal(norm2[:, k, 1:2], norm2[:, k, 0:1]).then_inc(rstd2_ready, 1)

            def neg_mean2(t, k, r):
                dve.wait_ge(rstd2_ready, t + 1)
                v.scalar_tensor_tensor(norm2[:, k, 2:3], mv2[:, k, 0:1], -1.0, norm2[:, k, 1:2], ALU.mult,
                                       ALU.mult).then_inc(norm2_ready, 1)

            def logit_copy(t, k, r):
                dve.wait_ge(logit_psum, t + 1)
                v.tensor_copy(logits[:, cols(t, E)], ps[6 + k % 2][:, 0:E]).then_inc(logit_ready, 1)

            run(dve, TILES, NODE_RING, 3, [(2, add_hs), (4, stats2), (3, where_edge), (4, mean_var2),
                                           (6, inv_std2), (3, residual), (6, neg_mean2), (10, logit_copy)])
            dve.wait_ge(logit_ready, TILES)

            lg = logits[:, :].rearrange("p (t e) -> p t e", e=E)

            def over_e(a):
                return a.unsqueeze(2).to_broadcast([P, TILES, E])

            def flat(a):
                return a.rearrange("p a b -> p (a b)")

            dve.wait_ge(late_ramps, 3)
            link(v.tensor_copy(exp_neg, io_e))
            link(v.tensor_reduce(t25[:, 0, :], lg, AX.X, ALU.max))
            link(v.tensor_tensor(probs, lg, over_e(t25[:, 0, :]), ALU.subtract))
            v.memset(tick[:, :], 0.0).then_inc(shifted, 1)
            dve.wait_ge(exp_ready, 1)
            link(v.tensor_reduce(t25[:, 1, :], ex, AX.X, ALU.add))
            link(v.reciprocal(t25[:, 1, :], t25[:, 1, :]))
            link(v.tensor_tensor(probs, ex, over_e(t25[:, 1, :]), ALU.mult))
            en = exp_neg.unsqueeze(1).to_broadcast([P, TILES, E])
            for c, (of, top) in enumerate(((probs, top0), (rest, top1))):
                best = t25[:, 2 + c, :]
                link(v.tensor_reduce(best, of, AX.X, ALU.max))
                link(v.tensor_tensor(eq, of, over_e(best), ALU.is_ge))
                link(v.tensor_tensor(cand, eq, en, ALU.mult))
                link(v.tensor_reduce(t25[:, 4, :], cand, AX.X, ALU.min))
                link(v.tensor_tensor(top, en, over_e(t25[:, 4, :]), ALU.is_equal))
                if c == 0:
                    link(v.scalar_tensor_tensor(flat(rest), flat(top0), -2.0, flat(probs), ALU.mult, ALU.add))
            link(v.tensor_tensor(both, top0, top1, ALU.add))
            for top in (top0, top1):
                v.tensor_tensor(top, top, over_e(valid[:, :]), ALU.mult)
            link(v.tensor_tensor(both, both, over_e(valid[:, :]), ALU.mult))
            v.memset(tick[:, :], 0.0).then_inc(choice_ready, 1)
            link(v.tensor_tensor(t25[:, 5, :], t25[:, 2, :], t25[:, 3, :], ALU.add))
            link(v.tensor_scalar(t25[:, 5, :], t25[:, 5, :], 1e-9, None, ALU.add))
            link(v.reciprocal(t25[:, 5, :], t25[:, 5, :]))
            link(v.tensor_tensor(gates, probs, both, ALU.mult))
            link(v.tensor_tensor(gates, gates, over_e(t25[:, 5, :]), ALU.mult))
            v.memset(tick[:, :], 0.0).then_inc(gates_ready, 1)
            dve.wait_ge(rank_psum, 1)
            link(v.tensor_tensor_scan(flat(cum), ones[:, 0:RE], ps[1][:, 0:RE], 0.0, ALU.mult, ALU.add))
            link(v.tensor_tensor(flat(cum_ex), flat(cum), ps[1][:, 0:RE], ALU.subtract))
            link(v.tensor_tensor(e8[:, 0, :], cum[:, :, TILES - 1], cum_ex[:, :, 0], ALU.subtract))
            link(v.tensor_scalar(t25[:, 0, :], thr[:, :], -float(P), None, ALU.add))
            link(v.tensor_tensor(tmp_ej, e8[:, 0, :].unsqueeze(2).to_broadcast([P, E, TILES]),
                                 t25[:, 0, :].unsqueeze(1).to_broadcast([P, E, TILES]), ALU.is_gt))
            link(v.tensor_reduce(e8[:, 1, :], tmp_ej, AX.X, ALU.add))
            link(v.tensor_scalar(e8[:, 1, :], e8[:, 1, :], 1.0, None, ALU.max))
            link(v.tensor_tensor_scan(e8[:, 2, :], ones[:, 0:E], e8[:, 1, :], 0.0, ALU.mult, ALU.add))
            link(v.tensor_tensor(e8[:, 3, :], e8[:, 2, :], e8[:, 1, :], ALU.subtract))
            link(v.scalar_tensor_tensor(e8[:, 4, :], e8[:, 3, :], float(P), cum_ex[:, :, 0], ALU.mult,
                                        ALU.subtract))
            link(v.tensor_tensor(flat(slot), flat(cum_ex), ps[0][:, 0:RE], ALU.add))
            link(v.tensor_tensor(slot, slot, e8[:, 4, :].unsqueeze(2).to_broadcast([P, E, TILES]), ALU.add))
            for c, top in enumerate((top0, top1)):
                link(v.tensor_tensor(cand, top, slot.rearrange("p e t -> p t e"), ALU.mult))
                link(v.tensor_reduce(slots_f[:, c * TILES:(c + 1) * TILES], cand, AX.X, ALU.add))
            link(v.tensor_copy(slots_i, slots_f))
            v.tensor_scalar(st_i, slots_i, 7, None, ALU.logical_shift_right)
            link(v.tensor_scalar(sr_i, slots_i, P - 1, None, ALU.bitwise_and))
            v.tensor_copy(st_f, st_i)
            link(v.tensor_copy(sr_f, sr_i))
            link(v.tensor_scalar(sr_f, sr_f, 1.0, None, ALU.add))
            for c in range(2):
                a = sr_f[:, c * TILES:(c + 1) * TILES]
                link(v.tensor_tensor(a, a, valid[:, :], ALU.mult))
                v.tensor_copy(tile_b[:, c * TILES:(c + 1) * TILES], iota_row[:, 0:TILES])
            link(v.tensor_scalar(sr_f, sr_f, -1.0, None, ALU.add))
            v.tensor_copy(sr_b, sr_f)
            v.tensor_copy(st_b, st_f)
            v.tensor_copy(iota_b, iota_row[:, :])
            link(v.tensor_copy(slot_no, io_slot))
            v.tensor_copy(slot_b, slot_no)
            link(v.tensor_copy(p_plus1, io_p))
            link(v.tensor_scalar(dump_p, p_plus1, float(DUMP), None, ALU.add))
            v.tensor_tensor(ohr, iota_b.unsqueeze(1).to_broadcast([P, S2, P]),
                            sr_b.unsqueeze(2).to_broadcast([P, S2, P]), ALU.is_equal)
            link(v.tensor_tensor(oht, slot_b.unsqueeze(1).to_broadcast([P, S2, SLOTS]),
                                 st_b.unsqueeze(2).to_broadcast([P, S2, SLOTS]), ALU.is_equal))
            v.tensor_tensor(moving[:, :, 0:SLOTS], oht, tile_b.unsqueeze(2).to_broadcast([P, S2, SLOTS]),
                            ALU.mult)
            link(v.tensor_scalar(moving[:, :, SLOTS:2 * SLOTS], oht, p_plus1, None, ALU.mult))
            v.memset(tick[:, :], 0.0).then_inc(onehot_ready, 1)
            link(v.tensor_tensor(exp_cmp, e8[:, 3, 1:E].unsqueeze(1).to_broadcast([P, SLOTS, E - 1]),
                                 slot_no.unsqueeze(2).to_broadcast([P, SLOTS, E - 1]), ALU.is_le))
            link(v.tensor_reduce(exp_f, exp_cmp, AX.X, ALU.add))
            link(v.tensor_copy(expert_of[0:1, :], exp_f[0:1, :]))
            link(v.memset(split_f, 0.0))
            link(v.tensor_scalar(behind_f, exp_f, 1.0, None, ALU.add))
            link(v.scalar_tensor_tensor(behind_f, exp_f, float(E - 1), behind_f, ALU.is_lt, ALU.mult))
            link(v.tensor_tensor(split_f[:, 1:SLOTS], exp_f[:, 1:SLOTS], exp_f[:, 0:SLOTS - 1], ALU.subtract))
            link(v.tensor_tensor(split_f, split_f, behind_f, ALU.mult))
            link(v.tensor_copy(split_next[0:1, :], split_f[0:1, :]))
            dve.wait_ge(token_psum, 1)
            link(v.tensor_copy(tok, ps[2][:, SLOTS:2 * SLOTS]))
            link(v.scalar_tensor_tensor(tok, ps[2][:, 0:SLOTS], float(P), tok, ALU.mult, ALU.add))
            link(v.tensor_scalar(tok, tok, -1.0, None, ALU.add))
            link(v.tensor_scalar(unused, tok, 0.0, None, ALU.is_lt))
            link(v.scalar_tensor_tensor(row_f, unused, dump_p, tok, ALU.mult, ALU.add))
            link(v.tensor_scalar(tok, tok, 0.0, None, ALU.max))
            pair = slot_rows[:, :].rearrange("p (t c) -> p t c", c=2)
            v.tensor_copy(pair[:, :, 0], tok)
            link(v.tensor_copy(pair[:, :, 1], row_f))
            dve.wait_ge(gates_stored, 16)
            v.memset(tick[:, :], 0.0).then_inc(slots_ready, 1)

            def hid_first(t, k, r):
                dve.wait_ge(silu_a, t + 1)
                v.tensor_tensor(hid[:, k % 2, 0:HA], s_act[:, 0:HA], ps[1][:, 0:HA], ALU.mult)\
                    .then_inc(hid_a_ready, 1)

            def hid_second(t, k, r):
                dve.wait_ge(silu_b, t + 1)
                v.tensor_tensor(hid[:, k % 2, HA:H], s_act[:, HA:H], ps[3][:, 0:HB], ALU.mult)\
                    .then_inc(hid_b_ready, 1)

            def xT_low(t, k, r):
                dve.wait_ge(xT_ready, t + 1)
                at = slice((k % 2) * C, (k % 2 + 1) * C)
                v.tensor_tensor(xT_lo[:, at], ps[4][:, 0:C], xT_hi[:, at].bitcast(fp32), ALU.subtract)\
                    .then_inc(xT_lo_ready, 1)

            def hidT_low(t, k, r):
                n = HC[-1][1]
                if at_least(t, 1):
                    dve.wait_ge(y_psum, t)
                for m, bank, lo, hi, copied in ((P, ps[6], 0, 4, 1), (P, ps[7], 4, 5, 3), (n, ps[7], 5, 6, 3)):
                    dve.wait_ge(hidT_hi_ready, 3 * t + copied)
                    at = slice(lo * P, hi * P)
                    last = v.tensor_tensor(hidT_lo[0:m, at], bank[0:m, lo % 4 * P:lo % 4 * P + (hi - lo) * P],
                                           hidT_hi[0:m, at].bitcast(fp32), ALU.subtract)
                last.then_inc(hidT_lo_ready, 1)

            def lo_piece(t, k, r):
                at_new_expert(dve, t, lambda e: split_lo(dve, v, e, 0))

            def gated(t, k, r):
                e = dve.value_load(expert_of[0:1, bass.ds(t, 1)], min_val=0, max_val=E - 1)
                dve.wait_ge(y_psum, t + 1)
                if at_least(t, 2):
                    dve.wait_ge(y_added, 16 * (t - 1))
                v.tensor_scalar(y_out[:, k % 2, :], ps[5][:, 0:C], xg_flat[:, bass.ds(e + (k * TR + C), 1)],
                                None, ALU.mult).then_inc(y_ready, 1)

            run(dve, SLOTS, RING, 1, [(2, lo_piece), (1, hid_first), (2, hidT_low), (0, xT_low), (1, hid_second),
                                      (2, gated)])


def kernel(x, src, dst, edge_attr_64, node_vec1, L0_gnn_W_self, L0_gnn_W_func, L0_gnn_W_att,
           L0_ffn_router_w, L0_ffn_w1, L0_ffn_w2, L0_ffn_w3):
    import numpy as np
    import concourse.bacc as bacc
    from concourse.bass_utils import run_bass_kernel_spmd

    pad = lambda a, n, value=0: np.concatenate([a, np.full((n - a.shape[0],) + a.shape[1:], value, a.dtype)])
    f = lambda a: np.ascontiguousarray(a)
    x, src, dst = np.asarray(x), np.asarray(src), np.asarray(dst)
    ea, att = np.asarray(edge_attr_64), np.asarray(L0_gnn_W_att)
    wfunc, wself = np.asarray(L0_gnn_W_func), np.asarray(L0_gnn_W_self)
    w1, w2, w3 = np.asarray(L0_ffn_w1), np.asarray(L0_ffn_w2), np.asarray(L0_ffn_w3)
    n = GROUPS * G
    up = [w.transpose(0, 2, 1).reshape(E, KC, P, H).transpose(0, 2, 1, 3).reshape(E, P, KC * H) for w in (w1, w3)]
    w2p = np.concatenate([w2.transpose(0, 2, 1), np.zeros((E, NH * P - H, C), w2.dtype)], axis=1)
    down = w2p.reshape(E, NH, P, C).transpose(0, 2, 1, 3).reshape(E, P, NH * C)
    dst_rows = pad(dst, n + G, PAD_DST).reshape(GROUPS + 1, G)
    arrays = {
        "in_x": f(pad(x, NP)),
        "in_src": f(pad(src, n).reshape(GROUPS, KG, P).transpose(0, 2, 1)),
        "in_dst": f(dst_rows),
        "in_last": f(pad(dst_rows[0:GROUPS, G - 1], P, PAD_DST).reshape(P, 1)),
        "in_wt": f(pad(ea, n).reshape(EDGE_LOADS, AT_ONCE, P, EF).transpose(0, 2, 1, 3)
                   .reshape(EDGE_LOADS, P, AT_ONCE * EF)),
        "in_wfunc": f(wfunc),
        "in_wfunct": f(wfunc.T),
        "in_wselft": f(wself.T),
        "in_attn": f(att[0, 0:2 * C].reshape(2, C).T),
        "in_atte": f(att[0, 2 * C:].reshape(1, EF)),
        "in_router": f(np.asarray(L0_ffn_router_w).T),
        "in_experts": f(np.concatenate([up[0], up[1], down], axis=2)),
    }
    nc = bacc.Bacc("TRN2", target_bir_lowering=False, num_devices=1)
    args = [nc.dram_tensor(k, a.shape, mybir.dt.from_np(a.dtype), kind="ExternalInput").ap()
            for k, a in arrays.items()]
    out = nc.dram_tensor("out_rows", (OUT_ROWS, C), mybir.dt.float32, kind="ExternalOutput").ap()
    build(nc, *args, out)
    r = run_bass_kernel_spmd(nc, [arrays], core_ids=[0])
    return r.results[0]["out_rows"][0:N]
```
